# Optimizing a Trainium2 kernel written in Bass

```python
import numpy as np
import jax
import jax.numpy as jnp

def _softmax(x, axis=-1):
    return jax.nn.softmax(x, axis=axis)

def _gelu(x):
    return jax.nn.gelu(x, approximate=True)

def _silu(x):
    return jax.nn.silu(x)

def _sigmoid(x):
    return jax.nn.sigmoid(x)

def _layernorm(x, axis=-1, eps=1e-05):
    m = jnp.mean(x, axis=axis, keepdims=True)
    v = jnp.var(x, axis=axis, keepdims=True)
    return (x - m) / jnp.sqrt(v + eps)

def _scatter_add(tgt, idx, src, axis=0):
    return tgt.at[idx].add(src)

def _segment_sum(src, seg, n):
    return jax.ops.segment_sum(src, seg, n)
kernel_name = 'mk_decoder_preln_d1_seqx_r2_888d49'

def setup_inputs(seed: int=0):
    np.random.seed(seed)
    _w = jnp.asarray

    def _rec_inputs():
        import jax
        import jax.numpy as jnp
        _rk = jax.random.key(seed)
        x = -0.000125 + 0.9999 * jax.random.normal(jax.random.fold_in(_rk, 1), (8, 100, 1024), jnp.float32)
        _lenS = 100 - jax.random.randint(jax.random.fold_in(_rk, 7), (8,), 0, max(1, 100 // 4) + 1, jnp.int32)
        _lenS2 = 722 - jax.random.randint(jax.random.fold_in(_rk, 8), (8,), 0, max(1, 722 // 4) + 1, jnp.int32)
        _ctx_2048P = jax.random.normal(jax.random.fold_in(_rk, 11), (8, 16, 1024), jnp.float32)
        _ctx_2048c = jax.random.dirichlet(jax.random.fold_in(_rk, 511), 0.3 * jnp.ones((16,), jnp.float32), (8, 722))
        _ctx_2048t = jnp.einsum('bsk,bkd->bsd', _ctx_2048c, _ctx_2048P)
        _ctx_2048t = _ctx_2048t * jax.lax.rsqrt(jnp.mean(jnp.square(_ctx_2048t)) + 1e-12) * 0.953939
        ctx_2048 = -0.000540021 + 0.99982 * (_ctx_2048t + 0.3 * jax.random.normal(jax.random.fold_in(_rk, 611), (8, 722, 1024), jnp.float32))
        return (x, ctx_2048)
    x, ctx_2048 = _rec_inputs()

    def _L0_attn_setup():
        import jax, jax.numpy as jnp
        import numpy as np
        HIDDEN = 1024
        HEADS = 16
        HEAD_DIM = HIDDEN // HEADS
        NEG = -10000000000.0
        key = jax.random.key(seed)
        k1, k2, k3 = jax.random.split(key, 3)
        x = jax.random.normal(k1, (2, 1024, HIDDEN), dtype=jnp.float32)
        w_qkv = jax.random.normal(k2, (HIDDEN, 3 * HIDDEN), dtype=jnp.float32) / np.sqrt(HIDDEN)
        w_out = jax.random.normal(k3, (HIDDEN, HIDDEN), dtype=jnp.float32) / np.sqrt(HIDDEN)
        return {'x': x, 'w_qkv': w_qkv, 'w_out': w_out}
    _L0_attn_all = _L0_attn_setup()
    _L0_attn_in = {k: v for k, v in _L0_attn_all.items() if k in ('w_qkv', 'w_out')}
    del _L0_attn_all

    def _L0_xattn_setup():
        import jax, jax.numpy as jnp
        import numpy as np
        DIM = 1024
        N_HEADS = 16
        HEAD_DIM = DIM // N_HEADS
        EPS = 1e-06
        IMG_LEN = 257

        def rms_norm(x, g, eps=EPS):
            var = jnp.mean(x * x, axis=-1, keepdims=True)
            return x * jax.lax.rsqrt(var + eps) * g

        def _attend(q, k, v, k_mask=None):
            scale = 1.0 / jnp.sqrt(jnp.asarray(HEAD_DIM, q.dtype))
            scores = jnp.einsum('bqnd,bknd->bnqk', q, k) * scale
            if k_mask is not None:
                neg = jnp.asarray(jnp.finfo(scores.dtype).min, scores.dtype)
                scores = jnp.where(k_mask[:, None, None, :], scores, neg)
            probs = jax.nn.softmax(scores, axis=-1)
            return jnp.einsum('bnqk,bknd->bqnd', probs, v)
        key = jax.random.key(seed)
        ks = jax.random.split(key, 16)
        B, L1, L2 = (1, 8192, 769)
        std = 0.02
        inp = {'x': jax.random.normal(ks[0], (B, L1, DIM), jnp.float32), 'context': jax.random.normal(ks[1], (B, L2, DIM), jnp.float32), 'context_lens': jax.random.randint(ks[2], (B,), 128, 513, jnp.int32), 'Wq': jax.random.normal(ks[3], (DIM, DIM), jnp.float32) * std, 'bq': jnp.zeros((DIM,), jnp.float32), 'gq': jnp.ones((DIM,), jnp.float32), 'Wk': jax.random.normal(ks[4], (DIM, DIM), jnp.float32) * std, 'bk': jnp.zeros((DIM,), jnp.float32), 'gk': jnp.ones((DIM,), jnp.float32), 'Wv': jax.random.normal(ks[5], (DIM, DIM), jnp.float32) * std, 'bv': jnp.zeros((DIM,), jnp.float32), 'Wk_img': jax.random.normal(ks[6], (DIM, DIM), jnp.float32) * std, 'bk_img': jnp.zeros((DIM,), jnp.float32), 'gk_img': jnp.ones((DIM,), jnp.float32), 'Wv_img': jax.random.normal(ks[7], (DIM, DIM), jnp.float32) * std, 'bv_img': jnp.zeros((DIM,), jnp.float32), 'Wo': jax.random.normal(ks[8], (DIM, DIM), jnp.float32) * std, 'bo': jnp.zeros((DIM,), jnp.float32)}
        return inp
    _L0_xattn_all = _L0_xattn_setup()
    _L0_xattn_in = {k: v for k, v in _L0_xattn_all.items() if k in ('context_lens', 'Wq', 'bq', 'gq', 'Wk', 'bk', 'gk', 'Wv', 'bv', 'Wk_img', 'bk_img', 'gk_img', 'Wv_img', 'bv_img', 'Wo', 'bo')}
    del _L0_xattn_all

    def _L0_ffn_setup():
        import jax, jax.numpy as jnp
        import numpy as np
        NUM_EXPERTS = 64
        TOP_K = 8
        key = jax.random.key(seed)
        ks = jax.random.split(key, 5)
        B, S, H, E, I = (4, 1024, 1024, NUM_EXPERTS, 384)
        hidden_states = jax.random.normal(ks[0], (B, S, H), jnp.float32)
        gate_w = jax.random.normal(ks[1], (H, E), jnp.float32) * 0.02
        gate_proj = jax.random.normal(ks[2], (E, H, I), jnp.float32) * 0.02
        up_proj = jax.random.normal(ks[3], (E, H, I), jnp.float32) * 0.02
        down_proj = jax.random.normal(ks[4], (E, I, H), jnp.float32) * 0.02
        return {'hidden_states': hidden_states, 'gate_w': gate_w, 'gate_proj': gate_proj, 'up_proj': up_proj, 'down_proj': down_proj}
    _L0_ffn_all = _L0_ffn_setup()
    _L0_ffn_in = {k: v for k, v in _L0_ffn_all.items() if k in ('gate_w', 'gate_proj', 'up_proj', 'down_proj')}
    del _L0_ffn_all
    return {'x': x, 'ctx_2048': ctx_2048, 'L0_attn_w_qkv': _L0_attn_in['w_qkv'], 'L0_attn_w_out': _L0_attn_in['w_out'], 'L0_xattn_context_lens': _L0_xattn_in['context_lens'], 'L0_xattn_Wq': _L0_xattn_in['Wq'], 'L0_xattn_bq': _L0_xattn_in['bq'], 'L0_xattn_gq': _L0_xattn_in['gq'], 'L0_xattn_Wk': _L0_xattn_in['Wk'], 'L0_xattn_bk': _L0_xattn_in['bk'], 'L0_xattn_gk': _L0_xattn_in['gk'], 'L0_xattn_Wv': _L0_xattn_in['Wv'], 'L0_xattn_bv': _L0_xattn_in['bv'], 'L0_xattn_Wk_img': _L0_xattn_in['Wk_img'], 'L0_xattn_bk_img': _L0_xattn_in['bk_img'], 'L0_xattn_gk_img': _L0_xattn_in['gk_img'], 'L0_xattn_Wv_img': _L0_xattn_in['Wv_img'], 'L0_xattn_bv_img': _L0_xattn_in['bv_img'], 'L0_xattn_Wo': _L0_xattn_in['Wo'], 'L0_xattn_bo': _L0_xattn_in['bo'], 'L0_ffn_gate_w': _L0_ffn_in['gate_w'], 'L0_ffn_gate_proj': _L0_ffn_in['gate_proj'], 'L0_ffn_up_proj': _L0_ffn_in['up_proj'], 'L0_ffn_down_proj': _L0_ffn_in['down_proj']}

def reference(x, ctx_2048, L0_attn_w_qkv, L0_attn_w_out, L0_xattn_context_lens, L0_xattn_Wq, L0_xattn_bq, L0_xattn_gq, L0_xattn_Wk, L0_xattn_bk, L0_xattn_gk, L0_xattn_Wv, L0_xattn_bv, L0_xattn_Wk_img, L0_xattn_bk_img, L0_xattn_gk_img, L0_xattn_Wv_img, L0_xattn_bv_img, L0_xattn_Wo, L0_xattn_bo, L0_ffn_gate_w, L0_ffn_gate_proj, L0_ffn_up_proj, L0_ffn_down_proj):
    import jax
    import jax.numpy as jnp

    def _L0_attn_ref(x, w_qkv, w_out):
        import jax, jax.numpy as jnp
        import numpy as np
        HIDDEN = 1024
        HEADS = 16
        HEAD_DIM = HIDDEN // HEADS
        NEG = -10000000000.0
        b, s, _ = x.shape
        qkv = x @ w_qkv
        qkv = qkv.reshape(b, s, 3, HEADS, HEAD_DIM)
        q, k, v = (qkv[:, :, 0], qkv[:, :, 1], qkv[:, :, 2])
        scale = jnp.sqrt(jnp.float32(HEAD_DIM)).astype(x.dtype)
        q = q / scale
        scores = jnp.einsum('bqhd,bkhd->bhqk', q, k)
        causal_mask = jnp.arange(s)[:, None] >= jnp.arange(s)[None, :]
        scores = jnp.where(causal_mask[None, None], scores, NEG)
        attn = jax.nn.softmax(scores, axis=-1)
        out = jnp.einsum('bhqk,bkhd->bqhd', attn, v).reshape(b, s, HIDDEN)
        return out @ w_out

    def _L0_xattn_ref(x, context, context_lens, Wq, bq, gq, Wk, bk, gk, Wv, bv, Wk_img, bk_img, gk_img, Wv_img, bv_img, Wo, bo):
        import jax, jax.numpy as jnp
        import numpy as np
        DIM = 1024
        N_HEADS = 16
        HEAD_DIM = DIM // N_HEADS
        EPS = 1e-06
        IMG_LEN = 257

        def rms_norm(x, g, eps=EPS):
            var = jnp.mean(x * x, axis=-1, keepdims=True)
            return x * jax.lax.rsqrt(var + eps) * g

        def _attend(q, k, v, k_mask=None):
            scale = 1.0 / jnp.sqrt(jnp.asarray(HEAD_DIM, q.dtype))
            scores = jnp.einsum('bqnd,bknd->bnqk', q, k) * scale
            if k_mask is not None:
                neg = jnp.asarray(jnp.finfo(scores.dtype).min, scores.dtype)
                scores = jnp.where(k_mask[:, None, None, :], scores, neg)
            probs = jax.nn.softmax(scores, axis=-1)
            return jnp.einsum('bnqk,bknd->bqnd', probs, v)
        b = x.shape[0]
        n, d = (N_HEADS, HEAD_DIM)
        ctx_img = context[:, :IMG_LEN]
        ctx_txt = context[:, IMG_LEN:]
        q = rms_norm(x @ Wq + bq, gq).reshape(b, -1, n, d)
        k = rms_norm(ctx_txt @ Wk + bk, gk).reshape(b, -1, n, d)
        v = (ctx_txt @ Wv + bv).reshape(b, -1, n, d)
        k_img = rms_norm(ctx_img @ Wk_img + bk_img, gk_img).reshape(b, -1, n, d)
        v_img = (ctx_img @ Wv_img + bv_img).reshape(b, -1, n, d)
        img_x = _attend(q, k_img, v_img)
        k_mask = jnp.arange(k.shape[1])[None, :] < context_lens[:, None]
        txt_x = _attend(q, k, v, k_mask)
        out = (txt_x + img_x).reshape(b, -1, n * d)
        return out @ Wo + bo

    def _L0_ffn_ref(hidden_states, gate_w, gate_proj, up_proj, down_proj):
        import jax, jax.numpy as jnp
        import numpy as np
        NUM_EXPERTS = 64
        TOP_K = 8
        B, S, H = hidden_states.shape
        x2d = hidden_states.reshape(-1, H)
        router_logits = x2d @ gate_w
        routing_weights = jax.nn.softmax(router_logits, axis=-1)
        routing_weights, selected_experts = jax.lax.top_k(routing_weights, TOP_K)
        routing_weights = routing_weights / jnp.sum(routing_weights, axis=-1, keepdims=True)
        flat_sel = selected_experts.reshape(-1)
        sorted_sel = jnp.argsort(flat_sel)
        token_idx = sorted_sel // TOP_K
        sorted_inputs = jnp.take(x2d, token_idx, axis=0).astype(jnp.bfloat16)
        group_sizes = jnp.bincount(flat_sel, length=NUM_EXPERTS)
        gate_k = gate_proj.astype(jnp.bfloat16)
        up_k = up_proj.astype(jnp.bfloat16)
        down_k = down_proj.astype(jnp.bfloat16)
        layer_w0 = jax.lax.ragged_dot(sorted_inputs, gate_k, group_sizes, preferred_element_type=jnp.bfloat16)
        layer_w1 = jax.lax.ragged_dot(sorted_inputs, up_k, group_sizes, preferred_element_type=jnp.bfloat16)
        intermediate = jax.nn.silu(layer_w0) * layer_w1
        expert_out = jax.lax.ragged_dot(intermediate, down_k, group_sizes, preferred_element_type=jnp.bfloat16)
        unsorted = jnp.take(expert_out, jnp.argsort(sorted_sel), axis=0)
        unsorted = unsorted.reshape(-1, TOP_K, H).astype(jnp.float32)
        out = jnp.einsum('tke,tk->te', unsorted, routing_weights.astype(jnp.float32))
        return out.reshape(B, S, H).astype(jnp.bfloat16)
    x = x + _L0_attn_ref(_layernorm(x, axis=-1), L0_attn_w_qkv, L0_attn_w_out)
    x = x + _L0_xattn_ref(_layernorm(x, axis=-1), ctx_2048, L0_xattn_context_lens, L0_xattn_Wq, L0_xattn_bq, L0_xattn_gq, L0_xattn_Wk, L0_xattn_bk, L0_xattn_gk, L0_xattn_Wv, L0_xattn_bv, L0_xattn_Wk_img, L0_xattn_bk_img, L0_xattn_gk_img, L0_xattn_Wv_img, L0_xattn_bv_img, L0_xattn_Wo, L0_xattn_bo)
    x = x + _L0_ffn_ref(_layernorm(x, axis=-1), L0_ffn_gate_w, L0_ffn_gate_proj, L0_ffn_up_proj, L0_ffn_down_proj)
    return x

_drawn_inputs = setup_inputs


def setup_inputs(seed=0):
    import zlib

    import numpy as np

    out = dict(_drawn_inputs(seed))
    spreads = {'L0_xattn_bq': (0.0, 0.457),
     'L0_xattn_gq': (1.0, 0.6),
     'L0_xattn_bk': (0.0, 0.8),
     'L0_xattn_gk': (1.0, 0.6),
     'L0_xattn_bv': (0.0, 0.1),
     'L0_xattn_bk_img': (0.0, 0.8),
     'L0_xattn_gk_img': (1.0, 0.6),
     'L0_xattn_bv_img': (0.0, 0.1),
     'L0_xattn_bo': (0.0, 0.1)}
    factors = {}
    for name, (base, spread) in spreads.items():
        noise = np.random.default_rng([zlib.crc32(name.encode()), seed]).standard_normal(out[name].shape)
        drawn = base * np.exp(spread * noise) if base else spread * noise
        out[name] = jnp.asarray(drawn.astype(out[name].dtype))
    for name, factor in factors.items():
        out[name] = (out[name] * factor).astype(out[name].dtype)
    return out
```

```python
from contextlib import ExitStack

import concourse.bass as bass
import concourse.mybir as mybir
import numpy as np

F32 = mybir.dt.float32
F32R = mybir.dt.float32r
BF16 = mybir.dt.bfloat16
I32 = mybir.dt.int32
ALU = mybir.AluOpType
ACT = mybir.ActivationFunctionType
AX = mybir.AxisListType

P = 128
B, S, D = 8, 100, 1024
HEADS, HD = 16, 64
KT = D // P
BANK = 512
IMG, TXT = 257, 465
LN_EPS, RMS_EPS = 1e-5, 1e-6
HALF = B // 2
SH = HALF * S


def wait(eng, sem, value):
    if not isinstance(value, int) or value > 0:
        eng.wait_ge(sem, value)


class Scope:

    def __init__(self, nc, ctx, sems, name):
        self.nc, self.ctx, self.sems, self.name = nc, ctx, sems, name

    def sb(self, name, shape, dt=F32):
        return self.ctx.enter_context(self.nc.sbuf_tensor(f"{self.name}_{name}", shape, dt))

    def ps(self, name, shape, dt=F32):
        return self.ctx.enter_context(self.nc.psum_tensor(f"{self.name}_{name}", shape, dt))

    def sem(self, name):
        self.sems.append(self.nc.alloc_semaphore(name=f"{self.name}_{name}"))
        return self.sems[-1]


def clear_semaphores(nc, sems):
    nc.clear_and_free_semaphores(sems)
    nc.all_engine_barrier()
    sems.clear()


def make_identity(eng, ident, cleared, made):
    eng.memset(ident[:, :], 0.0).then_inc(cleared, 1)
    eng.wait_ge(cleared, 1)
    n = ident.shape[1]
    eng.affine_select(out=ident[:, :], in_=ident[:, :], compare_op=ALU.not_equal, fill=1.0, base=0,
                      pattern=[[-1, n]], channel_multiplier=1).then_inc(made, 1)


def split_matmul(eng, out, w_hi, w_lo, a_hi, a_lo, first, last):
    eng.matmul(out, w_hi, a_hi, start=first, stop=False)
    eng.matmul(out, w_hi, a_lo, start=False, stop=False)
    return eng.matmul(out, w_lo, a_hi, start=False, stop=last)


def ln_project_phase(nc, sems, name, x_d, w_d, out_d, scales, bias_d=None, rms=None):
    groups = len(scales)
    with ExitStack() as ctx:
        sc = Scope(nc, ctx, sems, name)
        ident = sc.sb("ident", [P, P])
        x_row = sc.sb("x_row", [S, 2, D])
        xn = sc.sb("xn", [S, 2, D])
        stats = sc.sb("stats", [S, 2, 2, 6])
        mean_var = sc.sb("mean_var", [S, 2, 2])
        std = sc.sb("std", [S, 2])
        rstd = sc.sb("rstd", [S, 2])
        eps = sc.sb("eps", [P, 1])
        xnT_hi = sc.sb("xnT_hi", [P, B, KT, S], F32R)
        xnT_lo = sc.sb("xnT_lo", [P, B, KT, S], F32R)
        w_raw = sc.sb("w_raw", [P, 2, KT, P])
        w_hi = sc.sb("w_hi", [P, 2, KT, P], F32R)
        w_lo = sc.sb("w_lo", [P, 2, KT, P], F32R)
        proj = sc.sb("proj", [P, groups, B, KT, S])
        turn = sc.ps("turn", [P, 4, BANK])
        acc = sc.ps("acc", [P, 4, BANK])

        x_loaded = [sc.sem(f"x_loaded{u}") for u in range(2)]
        w_loaded = [sc.sem(f"w_loaded{u}") for u in range(2)]
        cleared, made = sc.sem("cleared"), sc.sem("made")
        stats_done, stats_seen = sc.sem("stats_done"), sc.sem("stats_seen")
        var_ready = sc.sem("var_ready")
        std_ready, rstd_ready = sc.sem("std_ready"), sc.sem("rstd_ready")
        xn_ready, turned = sc.sem("xn_ready"), sc.sem("turned")
        x_hi_ready, x_split = sc.sem("x_hi_ready"), sc.sem("x_split")
        w_hi_ready, w_split = sc.sem("w_hi_ready"), sc.sem("w_split")
        acc_ready, acc_used = sc.sem("acc_ready"), sc.sem("acc_used")
        stored = sc.sem("stored")
        if rms:
            bias = sc.sb("bias", [P, KT])
            gain = sc.sb("gain", [P, 1 + len(rms[1]), KT])
            ones = sc.sb("ones", [P, P])
            rms_eps = sc.sb("rms_eps", [P, 1])
            square = sc.sb("square", [P, HALF, KT, S])
            sumsq = sc.sb("sumsq", [P, SH])
            scaled = sc.sb("scaled", [P, HALF, KT, S])
            inv_rms = sc.sb("inv_rms", [P, SH])
            small_loaded, gains_made = sc.sem("small_loaded"), sc.sem("gains_made")
            rms_step, sumsq_ready = sc.sem("rms_step"), sc.sem("sumsq_ready")
            total_ready, rms_ready = sc.sem("total_ready"), sc.sem("rms_ready")
            out_ready = sc.sem("out_ready")
        block = ctx.enter_context(nc.Block())

        SLOTS, ACCS = 2, 4

        @block.sync
        def _(sp):
            def load_w(nt, u):
                sp.wait_ge(w_split, nt + 1)
                sp.dma_start(w_raw[:, u], w_d[nt]).then_inc(w_loaded[u], 16)

            if rms:
                sp.dma_start(bias[:, :], bias_d).then_inc(small_loaded, 16)
                for n, g_d in enumerate((rms[0], *rms[1])):
                    sp.dma_start(gain[:, n, :], g_d).then_inc(small_loaded, 16)
            for u in range(2):
                load_w(u, u)
            with sp.Fori(0, B // 2) as g:
                for u in range(2):
                    sp.wait_ge(xn_ready, 2 * g + u + 1)
                    sp.dma_start(x_row[:, u, :], x_d[2 * g + u]).then_inc(x_loaded[u], 16)
            with sp.Fori(1, groups * KT // 2) as g:
                for u in range(2):
                    load_w(2 * g + u, u)
            if rms:
                for h in range(2):
                    for o in range(len(out_d)):
                        sp.wait_ge(out_ready, h * len(out_d) + o + 1)
                        sp.dma_start(out_d[o][:, HALF * h:HALF * (h + 1)],
                                     (scaled, square)[o][:, :]).then_inc(stored, 16)
                sp.wait_ge(stored, 2 * len(out_d) * 16)
            else:
                for n in range(groups):
                    sp.wait_ge(acc_used, ACCS + 2 * KT * (n + 1))
                    sp.dma_start(out_d[n], proj[:, n]).then_inc(stored, 16)
                sp.wait_ge(stored, groups * 16)

        @block.gpsimd
        def _(pool):
            pool.memset(eps[:, :], LN_EPS)
            if rms:
                pool.memset(ones[:, :], 1.0)
                pool.memset(rms_eps[:, :], RMS_EPS)
            make_identity(pool, ident, cleared, made)

        @block.vector
        def _(dve):
            dve.sem_inc(xn_ready, SLOTS)
            dve.sem_inc(x_split, SLOTS)
            dve.sem_inc(w_split, SLOTS)
            with dve.Fori(0, B // 2) as g:
                for u in range(2):
                    dve.wait_ge(x_loaded[u], 16 * g + 16)
                    for c in range(2):
                        dve.bn_stats(stats[:, u, c, :],
                                     x_row[:, u, c * BANK:(c + 1) * BANK]).then_inc(stats_done, 1)
                    dve.wait_ge(stats_done, 4 * g + 2 * u + 2)
                    dve.sem_inc(stats_seen, 1)
                    dve.bn_aggr(mean_var[:, u, :],
                                stats[:, u].rearrange("p c s -> p (c s)")).then_inc(var_ready, 1)
                for u in range(2):
                    b = 2 * g + u
                    dve.wait_ge(std_ready, b + 1)
                    dve.reciprocal(rstd[:, u:u + 1], std[:, u:u + 1]).then_inc(rstd_ready, 1)
                    dve.wait_ge(rstd_ready, b + 1)
                    dve.wait_ge(turned, b + 1)
                    dve.tensor_scalar(xn[:, u, :], x_row[:, u, :], mean_var[:, u, 0:1],
                                      rstd[:, u:u + 1], ALU.subtract, ALU.mult).then_inc(xn_ready, 1)
                for u in range(2):
                    b = 2 * g + u
                    dve.wait_ge(x_hi_ready, b + 1)
                    dve.tensor_tensor(
                        xnT_lo[:, b].rearrange("p (c k) s -> p c (k s)", c=2),
                        turn[:, 2 * u:2 * u + 2, 0:SH],
                        xnT_hi[:, b].bitcast(F32).rearrange("p (c k) s -> p c (k s)", c=2),
                        ALU.subtract).then_inc(x_split, 1)
            with dve.Fori(0, groups * KT // 2) as g:
                for u in range(2):
                    dve.wait_ge(w_hi_ready, 2 * g + u + 1)
                    dve.tensor_tensor(w_lo[:, u], w_raw[:, u], w_hi[:, u].bitcast(F32),
                                      ALU.subtract).then_inc(w_split, 1)
            if rms:
                dve.wait_ge(small_loaded, 16 * (2 + len(rms[1])))
                for n in range(len(rms[1])):
                    dve.tensor_tensor(gain[:, 1 + n, :], gain[:, 1 + n, :], gain[:, 0, :],
                                      ALU.mult).then_inc(gains_made, 1)
                dve.wait_ge(gains_made, len(rms[1]))
                dve.wait_ge(acc_used, ACCS + 2 * KT)
                steps = 0
                for h in range(2):
                    part = proj[:, 0, HALF * h:HALF * (h + 1)]
                    if h:
                        dve.wait_ge(stored, 16 * len(out_d))
                    dve.tensor_tensor(square[:, :], part, part, ALU.mult).then_inc(rms_step, 1)
                    dve.wait_ge(rms_step, steps + 1)
                    dve.tensor_reduce(sumsq[:, :].rearrange("p (b s) -> p b s", b=HALF),
                                      square[:, :].rearrange("p b k s -> p b s k"),
                                      AX.X, ALU.add).then_inc(sumsq_ready, 1)
                    dve.wait_ge(rms_ready, h + 1)
                    dve.reciprocal(inv_rms[:, :], inv_rms[:, :]).then_inc(rms_step, 1)
                    dve.wait_ge(rms_step, steps + 2)
                    inv = inv_rms[:, :].rearrange("p (b s) -> p b s", b=HALF)
                    for nt in range(KT):
                        dve.tensor_tensor(part[:, :, nt, :], part[:, :, nt, :], inv,
                                          ALU.mult).then_inc(rms_step, 1)
                    steps += 2 + KT
                    dve.wait_ge(rms_step, steps)
                    for o in range(len(out_d)):
                        for nt in range(KT):
                            last = dve.tensor_scalar((scaled, square)[o][:, :, nt, :], part[:, :, nt, :],
                                                     gain[:, 1 + o, nt:nt + 1], None, ALU.mult)
                        last.then_inc(out_ready, 1)

        @block.scalar
        def _(act):
            act.sem_inc(acc_used, ACCS)
            act.wait_ge(made, 1)
            with act.Fori(0, B // 2) as g:
                for u in range(2):
                    act.wait_ge(var_ready, 2 * g + u + 1)
                    act.activation(std[:, u:u + 1], mean_var[:, u, 1:2], ACT.Sqrt,
                                   bias=eps[0:S, :]).then_inc(std_ready, 1)
                for u in range(2):
                    b = 2 * g + u
                    act.wait_ge(turned, SLOTS + b + 1)
                    act.copy(xnT_hi[:, b].rearrange("p (c k) s -> p c (k s)", c=2),
                             turn[:, 2 * u:2 * u + 2, 0:SH]).then_inc(x_hi_ready, 1)

            def split_w(g, u):
                act.wait_ge(w_loaded[u], 16 * g + 16)
                act.wait_ge(acc_ready, ACCS + 2 * (2 * g + u) - 2)
                act.copy(w_hi[:, u], w_raw[:, u]).then_inc(w_hi_ready, 1)

            if rms:
                act.wait_ge(small_loaded, 16 * (2 + len(rms[1])))
            for n in range(groups):
                with act.Fori(0, KT // 2) as g:
                    for u in range(2):
                        split_w(g + n * (KT // 2), u)
                    for u in range(2):
                        nt = 2 * g + u
                        for h in range(2):
                            act.wait_ge(acc_ready, ACCS + 2 * (n * KT + nt) + h + 1)
                            dst = proj[:, n, HALF * h:HALF * (h + 1), nt, :]
                            src = acc[:, 2 * u + h, 0:SH].rearrange("p (b s) -> p b s", b=HALF)
                            if bias_d is None:
                                done = act.activation(dst, src, ACT.Copy, scale=scales[n])
                            else:
                                done = act.activation(dst, src, ACT.Identity, bias=bias[:, bass.ts(nt, 1)])
                            done.then_inc(acc_used, 1)
            if rms:
                for h in range(2):
                    act.wait_ge(total_ready, h + 1)
                    act.activation(inv_rms[:, :], turn[:, 0, 0:SH], ACT.Sqrt, bias=rms_eps[:, :],
                                   scale=1.0 / D).then_inc(rms_ready, 1)

        @block.tensor
        def _(pe):
            pe.sem_inc(turned, SLOTS)
            pe.sem_inc(acc_ready, ACCS)
            pe.wait_ge(made, 1)
            with pe.Fori(0, B // 2) as g:
                for u in range(2):
                    b = 2 * g + u
                    pe.wait_ge(xn_ready, SLOTS + b + 1)
                    pe.wait_ge(x_split, b + 1)
                    for kt in range(KT):
                        col = (kt % 4) * S
                        mm = pe.transpose(turn[:, 2 * u + kt // 4, col:col + S],
                                          xn[:, u, kt * P:(kt + 1) * P], ident[0:S, 0:S])
                    mm.then_inc(turned, 1)
            pe.wait_ge(x_split, SLOTS + B)
            with pe.Fori(0, groups * KT // 2) as g:
                for u in range(2):
                    nt = 2 * g + u
                    pe.wait_ge(w_split, SLOTS + nt + 1)
                    for h in range(2):
                        pe.wait_ge(acc_used, 2 * nt + h + 1)
                        out = acc[:, 2 * u + h, 0:SH].rearrange("p (b s) -> p b s", b=HALF)
                        for kt in range(KT):
                            half = (slice(None), slice(HALF * h, HALF * (h + 1)), kt)
                            mm = split_matmul(pe, out, w_hi[:, u, kt, :], w_lo[:, u, kt, :],
                                              xnT_hi[half], xnT_lo[half], kt == 0, kt == KT - 1)
                        mm.then_inc(acc_ready, 1)
            if rms:
                for h in range(2):
                    pe.wait_ge(sumsq_ready, h + 1)
                    if h:
                        pe.wait_ge(rms_ready, h)
                    pe.matmul(turn[:, 0, 0:SH], ones[:, :], sumsq[:, :],
                              start=True, stop=True).then_inc(total_ready, 1)


def self_attention_phase(nc, sems, x_d, qkv_d, w_out_d, x1_d):
    QUADS, QP = 2, KT // 2
    with ExitStack() as ctx:
        sc = Scope(nc, ctx, sems, "self")
        ident = sc.sb("ident", [P, P])
        causal = sc.sb("causal", [S, S])
        w_raw = sc.sb("w_raw", [P, 2, D])
        w_hi = sc.sb("w_hi", [P, KT, D], F32R)
        w_lo = sc.sb("w_lo", [P, KT, D], F32R)
        qkvT = sc.sb("qkvT", [P, 3, KT, S])
        v_rows = sc.sb("v_rows", [S, D])
        probs = sc.sb("probs", [S, QUADS, 8, S])
        row_max = sc.sb("row_max", [S, QUADS, 8])
        row_sum = sc.sb("row_sum", [S, QUADS, 8])
        probsT = sc.sb("probsT", [S, QUADS, 8, S])
        at_hi = sc.sb("at_hi", [P, KT, S], F32R)
        at_lo = sc.sb("at_lo", [P, KT, S], F32R)
        x_row = sc.sb("x_row", [S, D])
        x1_row = sc.sb("x1_row", [S, D])
        scores = sc.ps("scores", [P, 2 * QUADS, BANK])
        turn = sc.ps("turn", [P, 2, BANK])
        mixed = sc.ps("mixed", [P, BANK])
        outp = sc.ps("outp", [P, BANK])

        cleared, made = sc.sem("cleared"), sc.sem("made")
        w_loaded = [sc.sem(f"w_loaded{u}") for u in range(2)]
        w_hi_ready, w_split = sc.sem("w_hi_ready"), sc.sem("w_split")
        qkv_loaded, x_loaded = sc.sem("qkv_loaded"), sc.sem("x_loaded")
        scores_ready, masked = sc.sem("scores_ready"), sc.sem("masked")
        centred, exp_ready = sc.sem("centred"), sc.sem("exp_ready")
        soft_step, probs_ready = sc.sem("soft_step"), sc.sem("probs_ready")
        turned, turn_used = sc.sem("turned"), sc.sem("turn_used")
        mixed_ready, at_hi_ready, at_split = sc.sem("mixed_ready"), sc.sem("at_hi_ready"), sc.sem("at_split")
        outp_ready, x1_ready = sc.sem("outp_ready"), sc.sem("x1_ready")
        x1_stored = sc.sem("x1_stored")
        block = ctx.enter_context(nc.Block())


        @block.sync
        def _(sp):
            sp.dma_start(qkvT[:, 0], qkv_d[0][:, 0]).then_inc(qkv_loaded, 16)
            sp.dma_start(qkvT[:, 1], qkv_d[1][:, 0]).then_inc(qkv_loaded, 16)
            sp.dma_start(qkvT[:, 2], qkv_d[2][:, 0]).then_inc(qkv_loaded, 16)
            for kt in range(KT):
                if kt >= 2:
                    sp.wait_ge(w_split, kt - 1)
                sp.dma_start(w_raw[:, kt % 2], w_out_d[kt]).then_inc(w_loaded[kt % 2], 16)
            sp.dma_start(x_row[:, :], x_d[0]).then_inc(x_loaded, 16)

            def load_qkv(b):
                sp.wait_ge(turned, 3 * (b - 1) + 1)
                for n in range(3):
                    sp.dma_start(qkvT[:, n], qkv_d[n][:, b]).then_inc(qkv_loaded, 16)

            def store_x1(b):
                sp.wait_ge(x1_ready, 2 * b + 2)
                sp.dma_start(x1_d[b], x1_row[:, :]).then_inc(x1_stored, 16)

            load_qkv(1)
            with sp.Fori(1, B - 1) as b:
                load_qkv(b + 1)
                store_x1(b - 1)
                sp.dma_start(x_row[:, :], x_d[b]).then_inc(x_loaded, 16)
            store_x1(B - 2)
            sp.dma_start(x_row[:, :], x_d[B - 1]).then_inc(x_loaded, 16)
            store_x1(B - 1)
            sp.wait_ge(x1_stored, 16 * B)

        @block.gpsimd
        def _(pool):
            make_identity(pool, ident, cleared, made)
            pool.memset(causal[:, :], 0.0).then_inc(cleared, 1)
            pool.wait_ge(cleared, 2)
            pool.affine_select(out=causal[:, :], in_=causal[:, :], compare_op=ALU.is_ge, fill=-1e10,
                               base=0, pattern=[[-1, S]], channel_multiplier=1).then_inc(made, 1)

        @block.vector
        def _(dve):
            STEPS = 2 * 3

            def centre(b, q):
                dve.wait_ge(scores_ready, 2 * b + q + 1)
                rows = probs[:, q].rearrange("s (e j) k -> s e j k", e=2)
                dve.tensor_tensor(rows, scores[0:S, 2 * q:2 * q + 2, 0:QP * S].rearrange(
                    "s e (j k) -> s e j k", j=QP),
                    causal[:, :].unsqueeze(1).unsqueeze(1).broadcast_to([S, 2, QP, S]),
                    ALU.add).then_inc(masked, 1)
                dve.wait_ge(masked, 2 * b + q + 1)
                dve.tensor_reduce(row_max[:, q], probs[:, q], AX.X, ALU.max).then_inc(soft_step, 1)
                dve.wait_ge(soft_step, STEPS * b + q + 1)
                dve.tensor_tensor(probs[:, q], probs[:, q],
                                  row_max[:, q].unsqueeze(2).broadcast_to([S, 8, S]),
                                  ALU.subtract).then_inc(centred, 1)

            def normalise(b, q):
                dve.wait_ge(exp_ready, 2 * b + q + 1)
                dve.tensor_reduce(row_sum[:, q], probs[:, q], AX.X, ALU.add).then_inc(soft_step, 1)
                dve.wait_ge(soft_step, STEPS * b + 2 + 2 * q + 1)
                dve.reciprocal(row_sum[:, q], row_sum[:, q]).then_inc(soft_step, 1)
                dve.wait_ge(soft_step, STEPS * b + 2 + 2 * q + 2)
                dve.tensor_tensor(probs[:, q], probs[:, q],
                                  row_sum[:, q].unsqueeze(2).broadcast_to([S, 8, S]),
                                  ALU.mult).then_inc(probs_ready, 1)

            def add_residual(b, h):
                dve.wait_ge(outp_ready, 2 * b + h + 1)
                if h == 0:
                    dve.wait_ge(x_loaded, 16 * b + 16)
                    wait(dve, x1_stored, 16 * b)
                cols = slice(h * BANK, (h + 1) * BANK)
                dve.tensor_tensor(x1_row[:, cols], outp[0:S, :], x_row[:, cols],
                                  ALU.add).then_inc(x1_ready, 1)

            def split_mixed(b):
                for q in range(QUADS):
                    dve.wait_ge(at_hi_ready, 2 * b + q + 1)
                    hi = at_hi[:, q * QP:(q + 1) * QP]
                    dve.tensor_tensor(at_lo[:, q * QP:(q + 1) * QP],
                                      mixed[:, 0:QP * S].rearrange("p (j s) -> p j s", j=QP),
                                      hi.bitcast(F32), ALU.subtract).then_inc(at_split, 1)

            dve.wait_ge(made, 2)
            for q in range(QUADS):
                centre(0, q)
            for q in range(QUADS):
                normalise(0, q)
            split_mixed(0)
            for kt in range(KT):
                dve.wait_ge(w_hi_ready, kt + 1)
                dve.tensor_tensor(w_lo[:, kt], w_raw[:, kt % 2], w_hi[:, kt].bitcast(F32),
                                  ALU.subtract).then_inc(w_split, 1)
            with dve.Fori(1, B) as b:
                for q in range(QUADS):
                    centre(b, q)
                for q in range(QUADS):
                    normalise(b, q)
                    add_residual(b - 1, q)
                split_mixed(b)
            for h in range(2):
                add_residual(B - 1, h)

        @block.scalar
        def _(act):
            def attend(b):
                act.wait_ge(turned, 3 * b + 1)
                wait(act, mixed_ready, 2 * b)
                act.copy(v_rows[:, :].rearrange("s (c n) -> s c n", c=2),
                         turn[0:S, :, :]).then_inc(turn_used, 1)
                for q in range(QUADS):
                    act.wait_ge(centred, 2 * b + q + 1)
                    act.activation(probs[:, q], probs[:, q], ACT.Exp).then_inc(exp_ready, 1)
                for q in range(QUADS):
                    act.wait_ge(turned, 3 * b + 2 + q)
                    act.copy(probsT[:, q].rearrange("k (e j) s -> k e (j s)", e=2),
                             turn[0:S, :, 0:QP * S]).then_inc(turn_used, 1)
                for q in range(QUADS):
                    act.wait_ge(mixed_ready, 2 * b + q + 1)
                    act.copy(at_hi[:, q * QP:(q + 1) * QP],
                             mixed[:, 0:QP * S].rearrange("p (j s) -> p j s", j=QP)).then_inc(at_hi_ready, 1)

            attend(0)
            for kt in range(KT):
                act.wait_ge(w_loaded[kt % 2], 16 * (kt // 2) + 16)
                act.copy(w_hi[:, kt], w_raw[:, kt % 2]).then_inc(w_hi_ready, 1)
            with act.Fori(1, B) as b:
                attend(b)

        @block.tensor
        def _(pe):
            def attend_scores(b):
                pe.wait_ge(qkv_loaded, 48 * b + 48)
                for q in range(QUADS):
                    wait(pe, masked, 2 * (b - 1) + q + 1)
                    for j in range(QP):
                        for e in range(2):
                            rows = slice(e * HD, (e + 1) * HD)
                            mm = pe.matmul(scores[0:S, 2 * q + e, j * S:(j + 1) * S],
                                           qkvT[rows, 0, q * QP + j, :], qkvT[rows, 1, q * QP + j, :],
                                           start=True, stop=True)
                    mm.then_inc(scores_ready, 1)
                wait(pe, turn_used, 3 * b)
                for nt in range(KT):
                    mm = pe.transpose(turn[0:S, nt // 4, (nt % 4) * P:(nt % 4 + 1) * P],
                                      qkvT[:, 2, nt, :], ident[:, :])
                mm.then_inc(turned, 1)

            def attend_mix(b):
                for q in range(QUADS):
                    pe.wait_ge(probs_ready, 2 * b + q + 1)
                    pe.wait_ge(turn_used, 3 * b + 1 + q)
                    for e in range(2):
                        for j in range(QP):
                            mm = pe.transpose(turn[0:S, e, j * S:(j + 1) * S], probs[:, q, e * QP + j, :],
                                              ident[0:S, 0:S])
                    mm.then_inc(turned, 1)
                for q in range(QUADS):
                    pe.wait_ge(turn_used, 3 * b + 2 + q)
                    wait(pe, at_split, 2 * b + q)
                    for j in range(QP):
                        for e in range(2):
                            head = 2 * (q * QP + j) + e
                            mm = pe.matmul(mixed[e * HD:(e + 1) * HD, j * S:(j + 1) * S],
                                           v_rows[:, head * HD:(head + 1) * HD], probsT[:, q, e * QP + j, :],
                                           start=True, stop=True)
                    mm.then_inc(mixed_ready, 1)

            def project(b):
                pe.wait_ge(at_split, 2 * b + 2)
                for h in range(2):
                    wait(pe, x1_ready, 2 * b + h)
                    for kt in range(KT):
                        cols = slice(h * BANK, (h + 1) * BANK)
                        mm = split_matmul(pe, outp[0:S, :], at_hi[:, kt, :], at_lo[:, kt, :],
                                          w_hi[:, kt, cols], w_lo[:, kt, cols], kt == 0, kt == KT - 1)
                    mm.then_inc(outp_ready, 1)

            pe.wait_ge(made, 1)
            attend_scores(0)
            attend_mix(0)
            pe.wait_ge(w_split, KT)
            with pe.Fori(1, B) as b:
                attend_scores(b)
                project(b - 1)
                attend_mix(b)
            project(B - 1)


class Keys:

    def __init__(self, units, tiles):
        self.units, self.tiles = units, tiles
        self.real = units[-1][0] + units[-1][2]
        self.tiles_of = [[(t, s, m) for t, (s, m) in enumerate(tiles) if u <= s < u + n]
                         for u, n, _ in units]
        self.runs = []
        for t, (_, m) in enumerate(tiles):
            if self.runs and self.runs[-1][2] == m:
                self.runs[-1][1] += 1
            else:
                self.runs.append([t, 1, m])


IMG_PAD = IMG + 1
TXT_PAD = TXT + 1
TXT_UNIT = 256
IMG_KEYS = Keys([(0, IMG_PAD, IMG)], [(0, 86), (86, 86), (172, 86)])
TXT_SHORT = Keys([(0, TXT_UNIT, TXT_UNIT)], [(0, P), (P, P)])
TXT_FULL = Keys([(0, TXT_UNIT, TXT_UNIT), (TXT_UNIT, TXT_PAD - TXT_UNIT, TXT - TXT_UNIT)],
                [(0, P), (P, P), (2 * P, P), (3 * P, TXT - 3 * P)])
MASKED = -2.0 ** 127


class CrossSems:

    def __init__(self, sc, tag):
        def sem(name):
            return sc.sem(f"{tag}_{name}")

        self.ctx_loaded = sem("ctx_loaded")
        self.ctx_hi_ready = sem("ctx_hi_ready")
        self.ctx_split = sem("ctx_split")
        self.w_loaded = [sem(f"w_loaded{u}") for u in range(2)]
        self.w_hi_ready = sem("w_hi_ready")
        self.w_split = sem("w_split")
        self.acc_ready = sem("acc_ready")
        self.acc_used = sem("acc_used")
        self.square_step = sem("square_step")
        self.total_ready = sem("total_ready")
        self.rms_ready = sem("rms_ready")
        self.inverted = sem("inverted")
        self.k_ready = sem("k_ready")
        self.v_turned = sem("v_turned")
        self.v_used = sem("v_used")
        self.q_loaded = sem("q_loaded")
        self.old_loaded = sem("old_loaded")
        self.scores_ready = sem("scores_ready")
        self.masked = sem("masked")
        self.max_ready = sem("max_ready")
        self.shift_ready = sem("shift_ready")
        self.exp_ready = sem("exp_ready")
        self.sum_inverted = sem("sum_inverted")
        self.probs_ready = sem("probs_ready")
        self.p_turned = sem("p_turned")
        self.p_used = sem("p_used")
        self.mixed_ready = sem("mixed_ready")
        self.mixed_used = sem("mixed_used")
        self.stored = sem("stored")


class CrossMemory:

    def __init__(self, sc, width, tiles, rows):
        self.ident = sc.sb("ident", [P, P])
        self.ones = sc.sb("ones", [P, P])
        self.eps = sc.sb("eps", [P, 1])
        self.bias = sc.sb("bias", [P, 2, KT])
        self.wk_hi = sc.sb("wk_hi", [P, KT, KT, P], F32R)
        self.wk_lo = sc.sb("wk_lo", [P, KT, KT, P], F32R)
        self.wv_hi = sc.sb("wv_hi", [P, KT, KT, P], F32R)
        self.wv_lo = sc.sb("wv_lo", [P, KT, KT, P], F32R)
        self.raw = sc.sb("raw", [P, KT * IMG_PAD])
        self.ctx_hi = sc.sb("ctx_hi", [P, KT, IMG_PAD], F32R)
        self.ctx_lo = sc.sb("ctx_lo", [P, KT, IMG_PAD], F32R)
        self.kT = sc.sb("kT", [P, KT, width])
        self.vT = sc.sb("vT", [P, 2, IMG_PAD])
        self.v = sc.sb("v", [rows, tiles, D])
        self.square = sc.sb("square", [P, IMG_PAD])
        self.norm = sc.sb("norm", [P, IMG_PAD])
        self.qT = sc.sb("qT", [P, KT, S])
        self.attn = sc.sb("attn", [P, KT, S])
        self.row_max = sc.sb("row_max", [S, 2, 2])
        self.shift = sc.sb("shift", [S, 2, 2])
        self.row_sum = sc.sb("row_sum", [S, 2, 2])
        self.probs = sc.sb("probs", [S, 2, 2, width])
        self.probsT = sc.sb("probsT", [rows, 2, tiles, S])
        self.acc = sc.ps("acc", [P, 2, BANK])
        self.scores = sc.ps("scores", [P, 2, BANK])
        self.v_turn = sc.ps("v_turn", [P, BANK])
        self.p_turn = sc.ps("p_turn", [P, 2, BANK])
        self.mixed = sc.ps("mixed", [P, BANK])

    def scores_of(self, j):
        return self.acc if j % 2 else self.scores

    def w_raw(self, slot):
        half = KT * IMG_PAD // 2
        return self.raw[:, slot * half:slot * half + KT * P].rearrange("p (k n) -> p k n", k=KT)

    def ctx_raw(self, n):
        return self.raw[:, 0:KT * n].rearrange("p (k n) -> p k n", k=KT)


SCALE = HD ** -0.5
W_TILES = 2 * KT


def cross_sp(sp, m, s, keys, ctx_d, w_d, q_d, old_d, out_d):
    units = len(keys.units)

    def load_ctx(b, c):
        first, n, _ = keys.units[c]
        sp.dma_start(m.ctx_raw(n), ctx_d[b][:, :, first:first + n]).then_inc(s.ctx_loaded, 16)

    def next_ctx(b, c):
        sp.wait_ge(s.ctx_split, KT * (b * units + c))
        load_ctx(b, c)

    def load_q(b):
        wait(sp, s.scores_ready, KT * b)
        sp.dma_start(m.qT[:, :, :], q_d[:, b]).then_inc(s.q_loaded, 16)

    def load_old(b):
        if old_d is not None:
            wait(sp, s.stored, 16 * b)
            sp.dma_start(m.attn[:, :, :], old_d[b]).then_inc(s.old_loaded, 16)

    def store(b):
        sp.wait_ge(s.mixed_used, KT * b + KT)
        sp.dma_start(out_d[b], m.attn[:, :, :]).then_inc(s.stored, 16)

    load_ctx(0, 0)
    load_q(0)
    load_old(0)
    sp.wait_ge(s.ctx_split, KT)
    for i in range(W_TILES):
        wait(sp, s.w_split, i - 1)
        sp.dma_start(m.w_raw(i % 2), w_d[i // KT][i % KT]).then_inc(s.w_loaded[i % 2], 16)
    sp.wait_ge(s.w_split, W_TILES)
    for c in range(1, units):
        next_ctx(0, c)
    next_ctx(1, 0)
    with sp.Fori(1, B - 1) as b:
        load_q(b)
        store(b - 1)
        load_old(b)
        for c in range(1, units):
            next_ctx(b, c)
        next_ctx(b + 1, 0)
    b = B - 1
    load_q(b)
    store(b - 1)
    load_old(b)
    for c in range(1, units):
        next_ctx(b, c)
    store(b)
    sp.wait_ge(s.stored, 16 * B)


def cross_pool(pool, m, s, keys):
    units, steps = len(keys.units), 2 * KT - 1

    def unit(b, c):
        first, _, n = keys.units[c]
        ui = b * units + c
        for nt in range(KT):
            pool.wait_ge(s.acc_used, W_TILES * ui + nt + 1)
            k = m.kT[:, nt, first:first + n]
            if nt == 0:
                wait(pool, s.k_ready, ui)
                pool.tensor_tensor(m.norm[:, 0:n], k, k, ALU.mult).then_inc(s.square_step, 1)
            else:
                pool.wait_ge(s.square_step, steps * ui + 2 * nt - 1)
                pool.tensor_tensor(m.square[:, 0:n], k, k, ALU.mult).then_inc(s.square_step, 1)
                pool.wait_ge(s.square_step, steps * ui + 2 * nt)
                pool.tensor_tensor(m.norm[:, 0:n], m.norm[:, 0:n], m.square[:, 0:n],
                                   ALU.add).then_inc(s.square_step, 1)

    with pool.Fori(0, B) as b:
        for c in range(units):
            unit(b, c)


def cross_act(act, m, s, keys, masked):
    units = len(keys.units)

    def split_ctx(b, c, kt):
        ui = b * units + c
        n = keys.units[c][1]
        if kt == 0:
            act.wait_ge(s.ctx_loaded, 16 * ui + 16)
            wait(act, s.acc_ready, W_TILES * ui)
        act.copy(m.ctx_hi[:, kt, 0:n], m.ctx_raw(n)[:, kt, :]).then_inc(s.ctx_hi_ready, 1)

    def split_w(i):
        act.wait_ge(s.w_loaded[i % 2], 16 * (i // 2) + 16)
        dst = (m.wk_hi, m.wv_hi)[i // KT]
        act.copy(dst[:, i % KT], m.w_raw(i % 2)).then_inc(s.w_hi_ready, 1)

    def project(b, c, first_batch):
        ui = b * units + c
        first, n, real = keys.units[c]
        for i in range(W_TILES):
            nt = i % KT
            if first_batch and i + 2 < W_TILES and c == 0:
                split_w(i + 2)
            if i == KT + 1:
                act.wait_ge(s.total_ready, ui + 1)
                act.activation(m.norm[:, 0:real], m.mixed[:, 0:real], ACT.Sqrt, bias=m.eps[:, :],
                               scale=1.0 / D).then_inc(s.rms_ready, 1)
            act.wait_ge(s.acc_ready, W_TILES * ui + i + 1)
            if i < KT:
                dst, src = m.kT[:, nt, first:first + real], m.acc[:, i % 2, 0:real]
            else:
                wait(act, s.v_turned, KT * ui + nt - 1)
                dst, src = m.vT[:, nt % 2, 0:n], m.acc[:, i % 2, 0:n]
            act.activation(dst, src, ACT.Identity,
                           bias=m.bias[:, i // KT, nt:nt + 1]).then_inc(s.acc_used, 1)

    def exponentials(b, j):
        slot = j % 2
        act.wait_ge(s.shift_ready, KT * b + j + 1)
        for e in range(2):
            src = (m.probs[:, slot, e, 0:keys.real] if masked
                   else m.scores_of(j)[0:S, e, 0:keys.real])
            done = act.activation(m.probs[:, slot, e, 0:keys.real], src, ACT.Exp,
                                  bias=m.shift[:, slot, e:e + 1], scale=SCALE,
                                  accum_out=m.row_sum[:, slot, e:e + 1])
        done.then_inc(s.exp_ready, 1)

    def attend(b, ahead):
        exponentials(b, 0)
        for j in range(KT):
            if j + 1 < KT:
                exponentials(b, j + 1)
            if ahead is not None:
                split_ctx(ahead, 0, j)
            act.wait_ge(s.p_turned, KT * b + j + 1)
            for t, count, rows in keys.runs:
                done = act.copy(m.probsT[0:rows, :, t:t + count, :],
                                m.p_turn[0:rows, :, t * S:(t + count) * S].rearrange(
                                    "k e (t s) -> k e t s", t=count))
            done.then_inc(s.p_used, 1)

    def batch(b, first_batch, ahead):
        for c in range(units):
            if c or first_batch:
                for kt in range(KT):
                    split_ctx(b, c, kt)
            if c == 0 and first_batch:
                split_w(0)
                split_w(1)
            project(b, c, first_batch)
        attend(b, ahead)

    batch(0, True, 1)
    with act.Fori(1, B - 1) as b:
        batch(b, False, b + 1)
    batch(B - 1, False, None)


def cross_dve(dve, m, s, keys, mask, add):
    units = len(keys.units)

    def split_ctx(b, c, kt):
        ui = b * units + c
        n = keys.units[c][1]
        dve.wait_ge(s.ctx_hi_ready, KT * ui + kt + 1)
        dve.tensor_tensor(m.ctx_lo[:, kt, 0:n], m.ctx_raw(n)[:, kt, :], m.ctx_hi[:, kt, 0:n].bitcast(F32),
                          ALU.subtract).then_inc(s.ctx_split, 1)

    def split_w(i):
        dve.wait_ge(s.w_hi_ready, i + 1)
        hi, lo = ((m.wk_hi, m.wk_lo), (m.wv_hi, m.wv_lo))[i // KT]
        dve.tensor_tensor(lo[:, i % KT], m.w_raw(i % 2), hi[:, i % KT].bitcast(F32),
                          ALU.subtract).then_inc(s.w_split, 1)

    def project(b, c, first_batch):
        ui = b * units + c
        first, _, real = keys.units[c]
        if first_batch and c == 0:
            for i in range(KT + 2):
                split_w(i)
        for nt in range(KT):
            if first_batch and c == 0 and KT + 2 + nt < W_TILES:
                split_w(KT + 2 + nt)
            dve.wait_ge(s.v_turned, KT * ui + nt + 1)
            if nt == 0:
                wait(dve, s.mixed_ready, KT * b)
            tiles = keys.tiles_of[c]
            for t, count, rows in keys.runs:
                here = [k for k in range(t, t + count) if tiles[0][0] <= k <= tiles[-1][0]]
                if here:
                    src = (here[0] - tiles[0][0]) * P
                    done = dve.tensor_copy(m.v[0:rows, here[0]:here[-1] + 1, nt * P:(nt + 1) * P],
                                           m.v_turn[0:rows, src:src + len(here) * P].rearrange(
                                               "k (t n) -> k t n", t=len(here)))
            done.then_inc(s.v_used, 1)
            if nt == 1:
                dve.wait_ge(s.rms_ready, ui + 1)
                dve.reciprocal(m.norm[:, 0:real], m.norm[:, 0:real]).then_inc(s.inverted, 1)
                dve.wait_ge(s.inverted, ui + 1)
                k = m.kT[:, :, first:first + real]
                dve.tensor_tensor(k, k, m.norm[:, 0:real].unsqueeze(1).broadcast_to([P, KT, real]),
                                  ALU.mult).then_inc(s.k_ready, 1)

    def maxima(b, j):
        slot, n = j % 2, KT * b + j
        dve.wait_ge(s.scores_ready, n + 1)
        src = m.scores_of(j)[0:S, :, 0:keys.real]
        if mask is None:
            dve.tensor_reduce(m.row_max[:, slot, :], src, AX.X, ALU.max).then_inc(s.max_ready, 1)
        else:
            dst = m.probs[:, slot, :, 0:keys.real]
            dve.tensor_tensor(dst, src, mask[:, 0:keys.real].unsqueeze(1).broadcast_to([S, 2, keys.real]),
                              ALU.add).then_inc(s.masked, 1)
            dve.wait_ge(s.masked, n + 1)
            dve.tensor_reduce(m.row_max[:, slot, :], dst, AX.X, ALU.max).then_inc(s.max_ready, 1)
        dve.wait_ge(s.max_ready, n + 1)
        dve.tensor_scalar(m.shift[:, slot, :], m.row_max[:, slot, :], -SCALE, None,
                          ALU.mult).then_inc(s.shift_ready, 1)

    def normalise(b, j):
        slot, n = j % 2, KT * b + j
        dve.wait_ge(s.exp_ready, n + 1)
        dve.reciprocal(m.row_sum[:, slot, :], m.row_sum[:, slot, :]).then_inc(s.sum_inverted, 1)
        dve.wait_ge(s.sum_inverted, n + 1)
        for e in range(2):
            p = m.probs[:, slot, e, 0:keys.real]
            done = dve.tensor_scalar(p, p, m.row_sum[:, slot, e:e + 1], None, ALU.mult)
        done.then_inc(s.probs_ready, 1)

    def collect(b, j):
        dve.wait_ge(s.mixed_ready, KT * b + j + 1)
        if j == 0:
            if add:
                dve.wait_ge(s.old_loaded, 16 * b + 16)
            else:
                wait(dve, s.stored, 16 * b)
        dst, src = m.attn[:, j, :], m.mixed[:, 0:S]
        if add:
            done = dve.tensor_tensor(dst, src, dst, ALU.add)
        else:
            done = dve.tensor_copy(dst, src)
        done.then_inc(s.mixed_used, 1)

    def attend(b, ahead):
        maxima(b, 0)
        maxima(b, 1)
        for j in range(KT):
            normalise(b, j)
            if j + 2 < KT:
                maxima(b, j + 2)
            if ahead is not None:
                split_ctx(ahead, 0, j)
            if j:
                collect(b, j - 1)
        collect(b, KT - 1)

    def batch(b, first_batch, ahead):
        for c in range(units):
            if c or first_batch:
                for kt in range(KT):
                    split_ctx(b, c, kt)
            project(b, c, first_batch)
        attend(b, ahead)

    batch(0, True, 1)
    with dve.Fori(1, B - 1) as b:
        batch(b, False, b + 1)
    batch(B - 1, False, None)


def cross_pe(pe, m, s, keys, masked):
    units = len(keys.units)
    scores_left = s.masked if masked else s.exp_ready

    def project(b, c, first_batch):
        ui = b * units + c
        first, n, real = keys.units[c]
        pe.wait_ge(s.ctx_split, KT * ui + KT)
        if c == 0:
            wait(pe, scores_left, KT * b)

        def turn_v(nt):
            pe.wait_ge(s.acc_used, W_TILES * ui + KT + nt + 1)
            wait(pe, s.v_used, KT * ui + nt)
            for i, (_, start, rows) in enumerate(keys.tiles_of[c]):
                mm = pe.transpose(m.v_turn[0:rows, i * P:(i + 1) * P],
                                  m.vT[:, nt % 2, start - first:start - first + rows], m.ident[:, :])
            mm.then_inc(s.v_turned, 1)

        for i in range(W_TILES):
            nt = i % KT
            hi, lo = ((m.wk_hi, m.wk_lo), (m.wv_hi, m.wv_lo))[i // KT]
            if first_batch and c == 0:
                pe.wait_ge(s.w_split, i + 1)
            wait(pe, s.acc_used, W_TILES * ui + i - 1)
            for kt in range(KT):
                mm = split_matmul(pe, m.acc[:, i % 2, 0:n], hi[:, nt, kt, :], lo[:, nt, kt, :],
                                  m.ctx_hi[:, kt, 0:n], m.ctx_lo[:, kt, 0:n], kt == 0, kt == KT - 1)
            mm.then_inc(s.acc_ready, 1)
            if i == KT:
                pe.wait_ge(s.square_step, (2 * KT - 1) * (ui + 1))
                wait(pe, s.mixed_used, KT * b)
                wait(pe, s.rms_ready, ui)
                pe.matmul(m.mixed[:, 0:real], m.ones[:, :], m.norm[:, 0:real],
                          start=True, stop=True).then_inc(s.total_ready, 1)
            if i > KT:
                turn_v(nt - 1)
        turn_v(KT - 1)

    def scores(b, j):
        wait(pe, scores_left, KT * b + j - 1)
        for e in range(2):
            rows = slice(e * HD, (e + 1) * HD)
            mm = pe.matmul(m.scores_of(j)[0:S, e, 0:keys.real], m.qT[rows, j, :], m.kT[rows, j, 0:keys.real],
                           start=True, stop=True)
        mm.then_inc(s.scores_ready, 1)

    def turn_probs(b, j):
        pe.wait_ge(s.probs_ready, KT * b + j + 1)
        wait(pe, s.p_used, KT * b + j)
        for e in range(2):
            for t, (start, rows) in enumerate(keys.tiles):
                mm = pe.transpose(m.p_turn[0:rows, e, t * S:(t + 1) * S],
                                  m.probs[:, j % 2, e, start:start + rows], m.ident[0:S, 0:S])
        mm.then_inc(s.p_turned, 1)

    def mix(b, j):
        pe.wait_ge(s.p_used, KT * b + j + 1)
        wait(pe, s.mixed_used, KT * b + j)
        for e in range(2):
            head = 2 * j + e
            for t, (_, rows) in enumerate(keys.tiles):
                mm = pe.matmul(m.mixed[e * HD:(e + 1) * HD, 0:S], m.v[0:rows, t, head * HD:(head + 1) * HD],
                               m.probsT[0:rows, e, t, :], start=t == 0, stop=t == len(keys.tiles) - 1)
        mm.then_inc(s.mixed_ready, 1)

    def batch(b, first_batch):
        for c in range(units):
            project(b, c, first_batch)
        pe.wait_ge(s.k_ready, units * b + units)
        pe.wait_ge(s.q_loaded, 16 * b + 16)
        pe.wait_ge(s.acc_used, W_TILES * units * (b + 1))
        pe.wait_ge(s.v_used, KT * units * (b + 1))
        scores(b, 0)
        scores(b, 1)
        for j in range(KT):
            turn_probs(b, j)
            if j + 2 < KT:
                scores(b, j + 2)
            mix(b, j)

    batch(0, True)
    with pe.Fori(1, B) as b:
        batch(b, False)


def cross_image_phase(nc, sems, ctx_d, w_d, bias_d, q_d, out_d):
    with ExitStack() as ctx:
        sc = Scope(nc, ctx, sems, "img")
        m = CrossMemory(sc, IMG_PAD, len(IMG_KEYS.tiles), IMG_KEYS.tiles[0][1])
        s = CrossSems(sc, "all")
        cleared, made, bias_loaded = sc.sem("cleared"), sc.sem("made"), sc.sem("bias_loaded")
        block = ctx.enter_context(nc.Block())

        @block.sync
        def _(sp):
            for n in range(2):
                sp.dma_start(m.bias[:, n, :], bias_d[n]).then_inc(bias_loaded, 16)
            cross_sp(sp, m, s, IMG_KEYS, ctx_d, w_d, q_d, None, out_d)

        @block.gpsimd
        def _(pool):
            make_identity(pool, m.ident, cleared, made)
            pool.memset(m.ones[:, :], 1.0)
            pool.memset(m.probs[:, :, :, IMG:IMG_PAD], 0.0)
            pool.memset(m.eps[:, :], RMS_EPS).then_inc(made, 1)
            cross_pool(pool, m, s, IMG_KEYS)

        @block.vector
        def _(dve):
            cross_dve(dve, m, s, IMG_KEYS, None, False)

        @block.scalar
        def _(act):
            act.wait_ge(made, 2)
            act.wait_ge(bias_loaded, 32)
            cross_act(act, m, s, IMG_KEYS, False)

        @block.tensor
        def _(pe):
            pe.wait_ge(made, 2)
            cross_pe(pe, m, s, IMG_KEYS, False)


def cross_text_phase(nc, sems, ctx_d, w_d, bias_d, lens_d, q_d, old_d, out_d):
    with ExitStack() as ctx:
        sc = Scope(nc, ctx, sems, "txt")
        m = CrossMemory(sc, TXT, len(TXT_FULL.tiles), P)
        mask = sc.sb("mask", [S, TXT])
        length = sc.sb("length", [S, 1])
        outside = sc.sb("outside", [S, 2])
        full = sc.sb("full", [S, 1], I32)
        s = CrossSems(sc, "all")
        cleared, made, bias_loaded = sc.sem("cleared"), sc.sem("made"), sc.sem("bias_loaded")
        len_loaded, len_step, mask_ready = sc.sem("len_loaded"), sc.sem("len_step"), sc.sem("mask_ready")
        key_index = m.probs[:, 0, 0, :].bitcast(I32)
        len_int = full[:, :]
        block = ctx.enter_context(nc.Block())

        def by_length(eng, run):
            eng.wait_ge(mask_ready, 3)
            is_full = eng.value_load(full[0:1, 0:1], min_val=0, max_val=1)
            with eng.If(is_full > 0):
                run(TXT_FULL)
            with eng.Else():
                run(TXT_SHORT)

        @block.sync
        def _(sp):
            sp.dma_start(len_int, lens_d).then_inc(len_loaded, 16)
            for n in range(2):
                sp.dma_start(m.bias[:, n, :], bias_d[n]).then_inc(bias_loaded, 16)
            by_length(sp, lambda keys: cross_sp(sp, m, s, keys, ctx_d, w_d, q_d, old_d, out_d))

        @block.gpsimd
        def _(pool):
            make_identity(pool, m.ident, cleared, made)
            pool.iota(key_index, [[1, TXT]], base=0, channel_multiplier=0).then_inc(made, 1)
            pool.memset(m.ones[:, :], 1.0)
            pool.memset(m.eps[:, :], RMS_EPS).then_inc(made, 1)
            by_length(pool, lambda keys: cross_pool(pool, m, s, keys))

        @block.vector
        def _(dve):
            dve.wait_ge(len_loaded, 16)
            dve.wait_ge(made, 2)
            dve.tensor_copy(length[:, :], len_int).then_inc(len_step, 1)
            dve.tensor_copy(mask[:, :], key_index).then_inc(len_step, 1)
            dve.wait_ge(len_step, 2)
            dve.tensor_scalar(mask[:, :], mask[:, :], length[:, :], MASKED, ALU.is_ge,
                              ALU.mult).then_inc(mask_ready, 1)
            dve.tensor_scalar(outside[:, 0:1], length[:, :], float(TXT_UNIT), None, ALU.is_gt).then_inc(len_step, 1)
            dve.tensor_scalar(outside[:, 1:2], length[:, :], 1.0, None, ALU.is_lt).then_inc(len_step, 1)
            dve.wait_ge(len_step, 4)
            dve.tensor_reduce(outside[:, 0:1], outside[:, :], AX.X, ALU.max).then_inc(mask_ready, 1)
            dve.wait_ge(mask_ready, 2)
            dve.tensor_copy(full[:, :], outside[:, 0:1]).then_inc(mask_ready, 1)
            by_length(dve, lambda keys: cross_dve(dve, m, s, keys, mask, True))

        @block.scalar
        def _(act):
            act.wait_ge(made, 3)
            act.wait_ge(bias_loaded, 32)
            by_length(act, lambda keys: cross_act(act, m, s, keys, True))

        @block.tensor
        def _(pe):
            pe.wait_ge(made, 3)
            by_length(pe, lambda keys: cross_pe(pe, m, s, keys, True))


EXPERTS, TOP_K, FF = 64, 8, 384
FT = FF // P
ROWS = B * S * TOP_K
MAX_TILES_OF = -(-B * S // P)
MAX_TILES = ROWS // P + EXPERTS
MAX_PAIRS = -(-MAX_TILES // 2)
PAIRS_AT = 2 * P


class Routing:

    def __init__(self, sc):
        self.x2 = sc.sb("x2", [S, B, D])
        self.weights = sc.sb("weights", [S, B, TOP_K])
        self.places = sc.sb("places", [S, B * TOP_K], I32)
        self.table = sc.sb("table", [1, 2 * P + 1], I32)


def route_phase(nc, sems, r, x1_d, attn_d, w_out_d, b_out_d, gate_d, rows_d):
    with ExitStack() as ctx:
        sc = Scope(nc, ctx, sems, "route")
        ident = sc.sb("ident", [P, P])
        eps = sc.sb("eps", [P, 1])
        before = sc.sb("before", [S, S], BF16)
        ones = sc.sb("ones", [S, P], BF16)
        w_raw = sc.sb("w_raw", [P, 2, D])
        w_hi = sc.sb("w_hi", [P, KT, D], F32R)
        w_lo = sc.sb("w_lo", [P, KT, D], F32R)
        b_out = sc.sb("b_out", [S, D])
        gate = sc.sb("gate", [P, KT, EXPERTS])
        at_raw = sc.sb("at_raw", [P, 2, KT, S])
        at_hi = sc.sb("at_hi", [P, 2, KT, S], F32R)
        at_lo = sc.sb("at_lo", [P, 2, KT, S], F32R)
        x1 = sc.sb("x1", [S, 2, D])
        xn = sc.sb("xn", [S, 2, D])
        xn_bf = sc.sb("xn_bf", [S, B, D], BF16)
        xnT = sc.sb("xnT", [P, KT, S])
        stats = sc.sb("stats", [S, 2, 2, 6])
        mean_var = sc.sb("mean_var", [S, 2, 2])
        std = sc.sb("std", [S, 2])
        zeros = sc.sb("zeros", [P, D], BF16)
        logits = sc.sb("logits", [S, B, EXPERTS])
        logit_max = sc.sb("logit_max", [S, B])
        top = sc.sb("top", [S, B, TOP_K])
        rest = sc.sb("rest", [S, B, EXPERTS])
        chosen = sc.sb("chosen", [S, B, EXPERTS])
        chosen_bf = sc.sb("chosen_bf", [S, B, EXPERTS], BF16)
        top_sum = sc.sb("top_sum", [S, B])
        prior = sc.sb("prior", [P, B + 1, EXPERTS])
        place = sc.sb("place", [S, B, EXPERTS])
        top_place = sc.sb("top_place", [S, B, TOP_K])
        match = sc.sb("match", [S, B, TOP_K, EXPERTS])
        row_end = sc.sb("row_end", [P, EXPERTS])
        row_start = sc.sb("row_start", [P, EXPERTS])
        tiles_of = sc.sb("tiles_of", [P, EXPERTS])
        tile_end = sc.sb("tile_end", [P, EXPERTS])
        tile_start = sc.sb("tile_start", [P, EXPERTS])
        unit = sc.sb("unit", [P, EXPERTS])
        passed = sc.sb("passed", [P, EXPERTS])
        owner = sc.sb("owner", [P, EXPERTS])
        origin = sc.sb("origin", [P, EXPERTS])
        inside = sc.sb("inside", [P, 1])
        offset = sc.sb("offset", [P, 1])
        tile_no = sc.sb("tile_no", [P, 1])
        tile_no_int = sc.sb("tile_no_int", [P, 1], I32)
        even_int = sc.sb("even_int", [1, P // 2], I32)
        even = sc.sb("even", [1, P // 2])
        pairs = sc.sb("pairs", [1, 1])
        columns = sc.sb("columns", [P, 2])
        outp = sc.ps("outp", [P, 2, BANK])
        turn = sc.ps("turn", [P, 2, BANK])
        logit_ps = sc.ps("logit_ps", [P, BANK])
        rank_ps = sc.ps("rank_ps", [P, BANK])
        count_ps = sc.ps("count_ps", [P, BANK])

        cleared, made, const_made = sc.sem("cleared"), sc.sem("made"), sc.sem("const_made")
        w_loaded = [sc.sem(f"w_loaded{u}") for u in range(2)]
        w_hi_ready, w_split = sc.sem("w_hi_ready"), sc.sem("w_split")
        small_loaded = sc.sem("small_loaded")
        at_loaded = [sc.sem(f"at_loaded{u}") for u in range(2)]
        x1_loaded = [sc.sem(f"x1_loaded{u}") for u in range(2)]
        x1_biased = sc.sem("x1_biased")
        at_hi_ready, at_split = sc.sem("at_hi_ready"), sc.sem("at_split")
        outp_ready, x2_ready, x2_seen = sc.sem("outp_ready"), sc.sem("x2_ready"), sc.sem("x2_seen")
        stats_done, stats_seen, var_ready = sc.sem("stats_done"), sc.sem("stats_seen"), sc.sem("var_ready")
        std_ready, rstd_ready, xn_ready = sc.sem("std_ready"), sc.sem("rstd_ready"), sc.sem("xn_ready")
        xn_bf_ready = sc.sem("xn_bf_ready")
        turned, xnT_ready = sc.sem("turned"), sc.sem("xnT_ready")
        router_ready, logits_ready = sc.sem("router_ready"), sc.sem("logits_ready")
        step = sc.sem("step")
        centred, exp_ready = sc.sem("centred"), sc.sem("exp_ready")
        chosen_ready, ranked = sc.sem("chosen_ready"), sc.sem("ranked")
        places_ready, columns_ready = sc.sem("places_ready"), sc.sem("columns_ready")
        columns_turned = sc.sem("columns_turned")
        pad_stored, sent = sc.sem("pad_stored"), sc.sem("sent")
        block = ctx.enter_context(nc.Block())

        @block.sync
        def _(sp):
            sp.dma_start(b_out[:, :], b_out_d.partition_broadcast(S)).then_inc(small_loaded, 16)
            sp.dma_start(gate[:, :, :], gate_d).then_inc(small_loaded, 16)

            def load(b, u):
                wait(sp, at_split, b - 1)
                sp.dma_start(at_raw[:, u], attn_d[b]).then_inc(at_loaded[u], 16)
                wait(sp, x2_ready, 2 * (b - 1))
                sp.dma_start(x1[:, u], x1_d[b]).then_inc(x1_loaded[u], 16)

            for u in range(2):
                load(u, u)
            for kt in range(KT):
                wait(sp, w_split, kt - 1)
                sp.dma_start(w_raw[:, kt % 2], w_out_d[kt]).then_inc(w_loaded[kt % 2], 16)
            with sp.Fori(1, B // 2) as g:
                for u in range(2):
                    load(2 * g + u, u)
            sp.wait_ge(const_made, 1)
            sp.dma_start(rows_d[ROWS:ROWS + P, :], zeros[:, :]).then_inc(pad_stored, 16)
            sp.wait_ge(pad_stored, 16)

        @block.gpsimd
        def _(pool):
            make_identity(pool, ident, cleared, made)
            pool.memset(eps[:, :], LN_EPS)
            pool.memset(unit[:, :], 1.0)
            pool.memset(ones[:, :], 1.0)
            pool.memset(prior[:, 0, :], 0.0)
            pool.iota(tile_no_int[:, :], [[0, 1]], base=0, channel_multiplier=1)
            pool.iota(even_int[:, :], [[2, P // 2]], base=0, channel_multiplier=0)
            pool.memset(before[:, :], 1.0).then_inc(cleared, 1)
            pool.wait_ge(cleared, 2)
            pool.affine_select(out=before[:, :], in_=before[:, :], compare_op=ALU.is_ge, fill=0.0,
                               base=-1, pattern=[[1, S]], channel_multiplier=-1).then_inc(made, 1)
            pool.memset(zeros[:, :], 0.0).then_inc(const_made, 1)
            pool.wait_ge(small_loaded, 32)

            def add_bias(b, u):
                pool.wait_ge(x1_loaded[u], 16 * (b // 2) + 16 if isinstance(b, int) else 8 * (b - u) + 16)
                pool.tensor_tensor(x1[:, u], x1[:, u], b_out[:, :], ALU.add).then_inc(x1_biased, 1)

            def narrow(b, u):
                pool.wait_ge(xn_ready, b + 1)
                pool.tensor_copy(xn_bf[:, b], xn[:, u]).then_inc(xn_bf_ready, 1)

            add_bias(0, 0)
            add_bias(1, 1)
            with pool.Fori(0, B // 2 - 1) as g:
                for u in range(2):
                    narrow(2 * g + u, u)
                    add_bias(2 * g + 2 + u, u)
            for u in range(2):
                narrow(B - 2 + u, u)
            pool.wait_ge(places_ready, 1)
            pool.wait_ge(xn_bf_ready, B)
            for b in range(B):
                for k in range(TOP_K):
                    c = b * TOP_K + k
                    pool.indirect_dma_start(
                        out=rows_d[:, :], out_offset=bass.IndirectOffsetOnAxis(ap=r.places[:, c:c + 1], axis=0),
                        in_=xn_bf[:, b, :], in_offset=None).then_inc(sent, 16)
            pool.wait_ge(sent, 16 * B * TOP_K)

        @block.vector
        def _(dve):
            def split_at(b, u):
                dve.wait_ge(at_hi_ready, b + 1)
                dve.tensor_tensor(at_lo[:, u], at_raw[:, u], at_hi[:, u].bitcast(F32),
                                  ALU.subtract).then_inc(at_split, 1)

            def norm(b, u):
                dve.wait_ge(x1_biased, b + 1)
                for h in range(2):
                    cols = slice(h * BANK, (h + 1) * BANK)
                    dve.wait_ge(outp_ready, 2 * b + h + 1)
                    dve.tensor_tensor(r.x2[:, b, cols], outp[0:S, h, :], x1[:, u, cols],
                                      ALU.add).then_inc(x2_ready, 1)
                dve.wait_ge(x2_ready, 2 * b + 2)
                dve.sem_inc(x2_seen, 1)
                for h in range(2):
                    dve.bn_stats(stats[:, u, h, :],
                                 r.x2[:, b, h * BANK:(h + 1) * BANK]).then_inc(stats_done, 1)
                dve.wait_ge(stats_done, 2 * b + 2)
                dve.sem_inc(stats_seen, 1)
                dve.bn_aggr(mean_var[:, u, :], stats[:, u].rearrange("p c s -> p (c s)")).then_inc(var_ready, 1)
                dve.wait_ge(std_ready, b + 1)
                dve.reciprocal(std[:, u:u + 1], std[:, u:u + 1]).then_inc(rstd_ready, 1)
                dve.wait_ge(rstd_ready, b + 1)
                wait(dve, turned, b - 1)
                wait(dve, xn_bf_ready, b - 1)
                dve.tensor_scalar(xn[:, u, :], r.x2[:, b, :], mean_var[:, u, 0:1], std[:, u:u + 1],
                                  ALU.subtract, ALU.mult).then_inc(xn_ready, 1)

            split_at(0, 0)
            split_at(1, 1)
            for kt in range(KT):
                dve.wait_ge(w_hi_ready, kt + 1)
                dve.tensor_tensor(w_lo[:, kt], w_raw[:, kt % 2], w_hi[:, kt].bitcast(F32),
                                  ALU.subtract).then_inc(w_split, 1)
            for u in range(2):
                norm(u, u)
                split_at(2 + u, u)
            with dve.Fori(1, B // 2 - 1) as g:
                for u in range(2):
                    norm(2 * g + u, u)
                    split_at(2 * g + 2 + u, u)
            for u in range(2):
                norm(B - 2 + u, u)

            steps = [0]

            def link(ins):
                steps[0] += 1
                ins.then_inc(step, 1)
                dve.wait_ge(step, steps[0])

            dve.wait_ge(logits_ready, B)
            link(dve.tensor_reduce(logit_max[:, :], logits[:, :, :], AX.X, ALU.max))
            dve.tensor_tensor(logits[:, :, :], logits[:, :, :],
                              logit_max[:, :].unsqueeze(2).broadcast_to([S, B, EXPERTS]),
                              ALU.subtract).then_inc(centred, 1)
            dve.wait_ge(exp_ready, 1)
            for b in range(B):
                last = dve.max(top[:, b, :], logits[:, b, :])
            link(last)
            for b in range(B):
                last = dve.match_replace(rest[:, b, :], top[:, b, :], logits[:, b, :], -1.0)
            link(last)
            link(dve.tensor_scalar(chosen[:, :, :], rest[:, :, :], 0.0, None, ALU.is_lt))
            dve.tensor_copy(chosen_bf[:, :, :], chosen[:, :, :]).then_inc(chosen_ready, 1)
            link(dve.tensor_reduce(top_sum[:, :], top[:, :, :], AX.X, ALU.add))
            link(dve.reciprocal(top_sum[:, :], top_sum[:, :]))
            link(dve.tensor_tensor(logits[:, :, :], logits[:, :, :],
                                   top_sum[:, :].unsqueeze(2).broadcast_to([S, B, EXPERTS]), ALU.mult))
            dve.wait_ge(ranked, 1)
            for b in range(B):
                link(dve.tensor_tensor(prior[:, b + 1, :], prior[:, b, :],
                                       count_ps[:, b * EXPERTS:(b + 1) * EXPERTS], ALU.add))
            total = prior[:, B, :]
            link(dve.tensor_tensor_scan(row_end[:, :], unit[:, :], total, 0.0, ALU.mult, ALU.add))
            link(dve.tensor_tensor(row_start[:, :], row_end[:, :], total, ALU.subtract))
            link(dve.tensor_tensor(place[:, :, :], prior[0:S, 0:B, :],
                                   rank_ps[0:S, :].rearrange("s (b e) -> s b e", b=B), ALU.add))
            link(dve.scalar_tensor_tensor(out=place[:, :, :], in0=place[:, :, :], scalar=1.0,
                                          in1=row_start[0:S, :].unsqueeze(1).broadcast_to([S, B, EXPERTS]),
                                          op0=ALU.add, op1=ALU.add))
            link(dve.tensor_tensor(place[:, :, :], place[:, :, :], chosen[:, :, :], ALU.mult))
            for b in range(B):
                last = dve.max(top_place[:, b, :], place[:, b, :])
            link(last)
            dve.tensor_scalar(r.places[:, :], top_place[:, :, :].rearrange("s b k -> s (b k)"), -1.0, None,
                              ALU.add).then_inc(places_ready, 1)
            link(dve.tensor_scalar(tiles_of[:, :], total, float(P), 1.0, ALU.is_gt, ALU.add))
            for n in range(2, MAX_TILES_OF):
                link(dve.scalar_tensor_tensor(out=tiles_of[:, :], in0=total, scalar=float(n * P),
                                              in1=tiles_of[:, :], op0=ALU.is_gt, op1=ALU.add))
            link(dve.tensor_tensor_scan(tile_end[:, :], unit[:, :], tiles_of[:, :], 0.0, ALU.mult, ALU.add))
            link(dve.tensor_tensor(tile_start[:, :], tile_end[:, :], tiles_of[:, :], ALU.subtract))
            link(dve.tensor_copy(tile_no[:, :], tile_no_int[:, :]))
            link(dve.tensor_scalar(passed[:, :], tile_end[:, :], tile_no[:, :], None, ALU.is_le))
            link(dve.tensor_reduce(columns[:, 0:1], passed[:, :], AX.X, ALU.add))
            link(dve.tensor_scalar(columns[:, 0:1], columns[:, 0:1], float(EXPERTS - 1), None, ALU.min))
            link(dve.tensor_scalar(owner[:, :], tile_start[:, :], tile_no[:, :], None, ALU.is_le))
            link(dve.tensor_tensor(owner[:, :], owner[:, :], passed[:, :], ALU.subtract))
            link(dve.tensor_reduce(inside[:, :], owner[:, :], AX.X, ALU.add))
            link(dve.scalar_tensor_tensor(out=origin[:, :], in0=tile_start[:, :], scalar=-float(P),
                                          in1=row_start[:, :], op0=ALU.mult, op1=ALU.add))
            link(dve.tensor_tensor(origin[:, :], origin[:, :], owner[:, :], ALU.mult))
            link(dve.tensor_reduce(columns[:, 1:2], origin[:, :], AX.X, ALU.add))
            link(dve.tensor_scalar(offset[:, :], tile_no[:, :], float(P), -float(ROWS), ALU.mult, ALU.add))
            link(dve.tensor_tensor(offset[:, :], offset[:, :], inside[:, :], ALU.mult))
            link(dve.scalar_tensor_tensor(out=columns[:, 1:2], in0=offset[:, :], scalar=float(ROWS),
                                          in1=columns[:, 1:2], op0=ALU.add, op1=ALU.add))
            dve.sem_inc(columns_ready, 1)
            link(dve.tensor_copy(even[:, :], even_int[:, :]))
            link(dve.tensor_scalar(even[:, :], even[:, :], tile_end[0:1, EXPERTS - 1:EXPERTS], None, ALU.is_lt))
            link(dve.tensor_reduce(pairs[:, :], even[:, :], AX.X, ALU.add))
            link(dve.tensor_copy(r.table[:, PAIRS_AT:PAIRS_AT + 1], pairs[:, :]))
            shape = [S, B, TOP_K, EXPERTS]
            link(dve.tensor_tensor(match[:, :, :, :], place[:, :, :].unsqueeze(2).broadcast_to(shape),
                                   top_place[:, :, :].unsqueeze(3).broadcast_to(shape), ALU.is_equal))
            link(dve.tensor_tensor(match[:, :, :, :], match[:, :, :, :],
                                   logits[:, :, :].unsqueeze(2).broadcast_to(shape), ALU.mult))
            link(dve.tensor_reduce(r.weights[:, :, :], match[:, :, :, :], AX.X, ALU.add))
            dve.wait_ge(columns_turned, 1)
            link(dve.tensor_copy(r.table[:, 0:2 * P], rank_ps[0:1, 0:2 * P]))

        @block.scalar
        def _(act):
            act.wait_ge(made, 2)

            def split_at(b, u):
                act.wait_ge(at_loaded[u], 16 * (b // 2) + 16 if isinstance(b, int) else 8 * (b - u) + 16)
                wait(act, outp_ready, 2 * (b - 1))
                act.copy(at_hi[:, u], at_raw[:, u]).then_inc(at_hi_ready, 1)

            def root(b, u):
                act.wait_ge(var_ready, b + 1)
                act.activation(std[:, u:u + 1], mean_var[:, u, 1:2], ACT.Sqrt,
                               bias=eps[0:S, :]).then_inc(std_ready, 1)

            def collect(b):
                act.wait_ge(turned, b + 1)
                act.copy(xnT[:, :, :].rearrange("p (c k) s -> p c (k s)", c=2),
                         turn[:, :, 0:SH]).then_inc(xnT_ready, 1)
                act.wait_ge(router_ready, b + 1)
                act.copy(logits[:, b, :], logit_ps[0:S, 0:EXPERTS]).then_inc(logits_ready, 1)

            split_at(0, 0)
            split_at(1, 1)
            for kt in range(KT):
                act.wait_ge(w_loaded[kt % 2], 16 * (kt // 2) + 16)
                act.copy(w_hi[:, kt], w_raw[:, kt % 2]).then_inc(w_hi_ready, 1)
            with act.Fori(0, B // 2 - 1) as g:
                for u in range(2):
                    root(2 * g + u, u)
                    split_at(2 * g + 2 + u, u)
                    collect(2 * g + u)
            for u in range(2):
                root(B - 2 + u, u)
                collect(B - 2 + u)
            act.wait_ge(centred, 1)
            act.activation(logits[:, :, :], logits[:, :, :], ACT.Exp).then_inc(exp_ready, 1)

        @block.tensor
        def _(pe):
            def project(b, u):
                pe.wait_ge(at_split, b + 1)
                for h in range(2):
                    cols = slice(h * BANK, (h + 1) * BANK)
                    wait(pe, x2_ready, 2 * (b - 1) + h + 1)
                    for kt in range(KT):
                        mm = split_matmul(pe, outp[0:S, h, :], at_hi[:, u, kt, :], at_lo[:, u, kt, :],
                                          w_hi[:, kt, cols], w_lo[:, kt, cols], kt == 0, kt == KT - 1)
                    mm.then_inc(outp_ready, 1)

            def router(b, u):
                pe.wait_ge(xn_ready, b + 1)
                wait(pe, xnT_ready, b)
                for kt in range(KT):
                    mm = pe.transpose(turn[:, kt // 4, (kt % 4) * S:(kt % 4 + 1) * S],
                                      xn[:, u, kt * P:(kt + 1) * P], ident[0:S, 0:S])
                mm.then_inc(turned, 1)
                pe.wait_ge(xnT_ready, b + 1)
                wait(pe, logits_ready, b)
                for kt in range(KT):
                    mm = pe.matmul(logit_ps[0:S, 0:EXPERTS], xnT[:, kt, :], gate[:, kt, :],
                                   start=kt == 0, stop=kt == KT - 1)
                mm.then_inc(router_ready, 1)

            pe.wait_ge(made, 2)
            pe.wait_ge(small_loaded, 32)
            pe.wait_ge(w_split, KT)
            project(0, 0)
            project(1, 1)
            router(0, 0)
            project(2, 0)
            router(1, 1)
            with pe.Fori(1, B // 2 - 1) as g:
                project(2 * g + 1, 1)
                router(2 * g, 0)
                project(2 * g + 2, 0)
                router(2 * g + 1, 1)
            project(B - 1, 1)
            router(B - 2, 0)
            router(B - 1, 1)
            pe.wait_ge(chosen_ready, 1)
            picks = chosen_bf[:, :, :].rearrange("s b e -> s (b e)")
            pe.matmul(rank_ps[0:S, :], before[:, :], picks, start=True, stop=True)
            pe.matmul(count_ps[:, :], ones[:, :], picks, start=True, stop=True).then_inc(ranked, 1)
            pe.wait_ge(places_ready, 1)
            pe.wait_ge(columns_ready, 1)
            for n in range(2):
                mm = pe.transpose(rank_ps[0:1, n * P:(n + 1) * P], columns[:, n:n + 1], ident[:, :])
            mm.then_inc(columns_turned, 1)


def experts_phase(nc, sems, r, gate_d, up_d, down_d, rows_d, out_d):
    with ExitStack() as ctx:
        sc = Scope(nc, ctx, sems, "moe")
        ident = sc.sb("ident", [P, P], BF16)
        gate_raw = sc.sb("gate_raw", [P, 2, KT * FF])
        up_raw = sc.sb("up_raw", [P, 2, KT * FF])
        down_raw = sc.sb("down_raw", [P, 2, FT * D])
        gate = sc.sb("gate", [P, 2, KT, FF], BF16)
        up = sc.sb("up", [P, 2, KT, FF], BF16)
        down = sc.sb("down", [P, 2, FT, D], BF16)
        rows = sc.sb("rows", [P, 2, D], BF16)
        rowsT = sc.sb("rowsT", [P, 2, KT, P], BF16)
        silu = sc.sb("silu", [P, 2, FT * P])
        inner = sc.sb("inner", [P, 2, FT, P], BF16)
        out = sc.sb("out", [P, 2, D], BF16)
        turn = sc.ps("turn", [P, KT, P], BF16)
        gate_ps = sc.ps("gate_ps", [P, 2, BANK])
        up_ps = sc.ps("up_ps", [P, 2, BANK])
        out_ps = sc.ps("out_ps", [P, 2, BANK])

        cleared, made = sc.sem("cleared"), sc.sem("made")
        gate_loaded = [sc.sem(f"gate_loaded{u}") for u in range(2)]
        up_loaded = [sc.sem(f"up_loaded{u}") for u in range(2)]
        down_loaded = [sc.sem(f"down_loaded{u}") for u in range(2)]
        rows_loaded = [sc.sem(f"rows_loaded{u}") for u in range(2)]
        gate_cast, up_cast, down_cast = sc.sem("gate_cast"), sc.sem("up_cast"), sc.sem("down_cast")
        turned, rowsT_ready = sc.sem("turned"), sc.sem("rowsT_ready")
        gate_ready, up_ready = sc.sem("gate_ready"), sc.sem("up_ready")
        silu_ready, inner_ready = sc.sem("silu_ready"), sc.sem("inner_ready")
        out_ready, out_copied = sc.sem("out_ready"), sc.sem("out_copied")
        stored, all_stored = sc.sem("stored"), sc.sem("all_stored")
        block = ctx.enter_context(nc.Block())

        SLOTS = 2

        def over_tiles(eng, tile):
            pairs = eng.value_load(r.table[0:1, PAIRS_AT:PAIRS_AT + 1], min_val=1, max_val=MAX_PAIRS)
            with eng.Fori(0, MAX_PAIRS) as g:
                with eng.If(g < pairs):
                    for u in range(2):
                        tile(2 * g + u, g, u)
            return pairs

        @block.sync
        def _(sp):
            def tile(i, g, u):
                e = sp.value_load(r.table[0:1, bass.ts(i, 1)], min_val=0, max_val=EXPERTS - 1)
                first = sp.value_load(r.table[0:1, bass.ds(i + P, 1)], min_val=0, max_val=ROWS)
                sp.wait_ge(turned, i + 1)
                sp.dma_start(rows[:, u], rows_d[bass.ds(first, P), :]).then_inc(rows_loaded[u], 16)
                for raw, w_d, cast, loaded in ((gate_raw, gate_d, gate_cast, gate_loaded),
                                               (up_raw, up_d, up_cast, up_loaded),
                                               (down_raw, down_d, down_cast, down_loaded)):
                    sp.wait_ge(cast, i + 1)
                    sp.dma_start(raw[:, u], w_d[e]).then_inc(loaded[u], 16)

            over_tiles(sp, tile)

        @block.gpsimd
        def _(pool):
            make_identity(pool, ident, cleared, made)

        @block.vector
        def _(dve):
            dve.sem_inc(gate_cast, SLOTS)
            dve.sem_inc(up_cast, SLOTS)
            dve.sem_inc(inner_ready, SLOTS)
            dve.sem_inc(rowsT_ready, 1)

            def tile(i, g, u):
                dve.wait_ge(turned, SLOTS + i + 1)
                dve.tensor_copy(rowsT[:, u], turn[:, :, :]).then_inc(rowsT_ready, 1)
                dve.wait_ge(gate_loaded[u], 16 * g + 16)
                dve.wait_ge(gate_ready, i + 1)
                dve.tensor_copy(gate[:, u].rearrange("p k f -> p (k f)"), gate_raw[:, u]).then_inc(gate_cast, 1)
                dve.wait_ge(up_loaded[u], 16 * g + 16)
                dve.wait_ge(up_ready, i + 1)
                dve.tensor_copy(up[:, u].rearrange("p k f -> p (k f)"), up_raw[:, u]).then_inc(up_cast, 1)
                dve.wait_ge(silu_ready, SLOTS + i + 1)
                dve.wait_ge(up_ready, SLOTS + i + 1)
                dve.wait_ge(out_ready, i + 1)
                dve.tensor_tensor(inner[:, u].rearrange("p f s -> p (f s)"), silu[:, u],
                                  up_ps[:, u, 0:FT * P], ALU.mult).then_inc(inner_ready, 1)

            over_tiles(dve, tile)

        @block.scalar
        def _(act):
            act.sem_inc(down_cast, SLOTS)
            act.sem_inc(silu_ready, SLOTS)
            act.sem_inc(out_copied, 1)

            def tile(i, g, u):
                first = act.value_load(r.table[0:1, bass.ds(i + P, 1)], min_val=0, max_val=ROWS)
                act.wait_ge(down_loaded[u], 16 * g + 16)
                act.wait_ge(out_ready, i + 1)
                act.copy(down[:, u].rearrange("p f n -> p (f n)"), down_raw[:, u]).then_inc(down_cast, 1)
                act.wait_ge(gate_ready, SLOTS + i + 1)
                act.wait_ge(inner_ready, i + 1)
                act.activation(silu[:, u], gate_ps[:, u, 0:FT * P], ACT.Silu).then_inc(silu_ready, 1)
                act.wait_ge(out_ready, SLOTS + i + 1)
                act.wait_ge(stored, 16 * i + 16)
                act.copy(out[:, u].rearrange("s (h n) -> s h n", h=2), out_ps[:, :, :]).then_inc(out_copied, 1)
                act.wait_ge(out_copied, i + 2)
                act.wait_ge(stored, 16 * i + 32)
                act.dma_start(out_d[bass.ds(first, P), :], out[:, u]).then_inc(stored, 16)

            act.sem_inc(stored, 32)
            pairs = over_tiles(act, tile)
            act.wait_ge(stored, 32 * pairs + 32)
            act.sem_inc(all_stored, 1)

        @block.tensor
        def _(pe):
            pe.sem_inc(turned, SLOTS)
            pe.sem_inc(gate_ready, SLOTS)
            pe.sem_inc(up_ready, SLOTS)
            pe.sem_inc(out_ready, SLOTS)
            pe.wait_ge(made, 1)

            def tile(i, g, u):
                pe.wait_ge(rows_loaded[u], 16 * g + 16)
                pe.wait_ge(rowsT_ready, i + 1)
                for k in range(KT):
                    mm = pe.transpose(turn[:, k, :], rows[:, u, k::KT], ident[:, :])
                mm.then_inc(turned, 1)
                pe.wait_ge(rowsT_ready, i + 2)
                for w, ps, cast, left, ready in ((gate, gate_ps, gate_cast, silu_ready, gate_ready),
                                                 (up, up_ps, up_cast, inner_ready, up_ready)):
                    pe.wait_ge(cast, SLOTS + i + 1)
                    pe.wait_ge(left, i + 1)
                    for f in range(FT):
                        for k in range(KT):
                            mm = pe.matmul(ps[:, u, f * P:(f + 1) * P], w[:, u, k, f::FT], rowsT[:, u, k, :],
                                           start=k == 0, stop=k == KT - 1)
                    mm.then_inc(ready, 1)
                pe.wait_ge(inner_ready, SLOTS + i + 1)
                pe.wait_ge(down_cast, SLOTS + i + 1)
                pe.wait_ge(out_copied, i + 1)
                for h in range(2):
                    for f in range(FT):
                        mm = pe.matmul(out_ps[:, h, :], inner[:, u, f, :], down[:, u, f, h * BANK:(h + 1) * BANK],
                                       start=f == 0, stop=f == FT - 1)
                mm.then_inc(out_ready, 1)

            over_tiles(pe, tile)


def combine_phase(nc, sems, r, rows_d, out_d):
    GATHERS = 4
    with ExitStack() as ctx:
        sc = Scope(nc, ctx, sems, "comb")
        part = sc.sb("part", [S, GATHERS, D], BF16)
        gathered = [sc.sem(f"gathered{n}") for n in range(GATHERS)]
        added, stored = sc.sem("added"), sc.sem("stored")
        block = ctx.enter_context(nc.Block())

        @block.gpsimd
        def _(pool):
            for c in range(B * TOP_K):
                wait(pool, added, c - GATHERS + 1)
                pool.indirect_dma_start(
                    out=part[:, c % GATHERS, :], out_offset=None, in_=rows_d[:, :],
                    in_offset=bass.IndirectOffsetOnAxis(ap=r.places[:, c:c + 1], axis=0)
                ).then_inc(gathered[c % GATHERS], 16)

        @block.vector
        def _(dve):
            for c in range(B * TOP_K):
                b, k = c // TOP_K, c % TOP_K
                dve.wait_ge(gathered[c % GATHERS], 16 * (c // GATHERS) + 16)
                wait(dve, added, c)
                dve.scalar_tensor_tensor(out=r.x2[:, b, :], in0=part[:, c % GATHERS, :],
                                         scalar=r.weights[:, b, k:k + 1], in1=r.x2[:, b, :],
                                         op0=ALU.mult, op1=ALU.add).then_inc(added, 1)

        @block.sync
        def _(sp):
            for b in range(B):
                sp.wait_ge(added, TOP_K * (b + 1))
                sp.dma_start(out_d[b], r.x2[:, b, :]).then_inc(stored, 16)
            sp.wait_ge(stored, 16 * B)


def decoder_kernel(nc, a, out):
    def scratch(name, shape, dt=F32):
        return nc.dram_tensor(name, shape, dt).ap()

    qkv_d = [scratch(f"self_{n}_dram", (P, B, KT, S)) for n in ("q", "k", "v")]
    q_d = [scratch(f"cross_q_{n}_dram", (P, B, KT, S)) for n in ("img", "txt")]
    x1_d = scratch("x1_dram", (B, S, D))
    img_d = scratch("attn_img_dram", (B, P, KT, S))
    attn_d = scratch("attn_dram", (B, P, KT, S))
    rows_d = scratch("expert_rows_dram", (ROWS + P, D), BF16)
    results_d = scratch("expert_results_dram", (ROWS + P, D), BF16)
    sems = []
    with ExitStack() as memory:
        ln_project_phase(nc, sems, "qkv", a["x"], a["w_qkv"], qkv_d, [HD ** -0.5, 1.0, 1.0])
        self_attention_phase(nc, sems, a["x"], qkv_d, a["w_self_out"], x1_d)
        ln_project_phase(nc, sems, "q", x1_d, a["wq"], q_d, [1.0], bias_d=a["bq"],
                         rms=(a["gq"], [a["gk_img"], a["gk"]]))
        cross_image_phase(nc, sems, a["ctx_img"], (a["wk_img"], a["wv_img"]), (a["bk_img"], a["bv_img"]),
                          q_d[0], img_d)
        cross_text_phase(nc, sems, a["ctx_txt"], (a["wk"], a["wv"]), (a["bk"], a["bv"]), a["lens"],
                         q_d[1], img_d, attn_d)
        clear_semaphores(nc, sems)
        r = Routing(Scope(nc, memory, sems, "routing"))
        route_phase(nc, sems, r, x1_d, attn_d, a["wo"], a["bo"], a["gate"], rows_d)
        experts_phase(nc, sems, r, a["moe_gate"], a["moe_up"], a["moe_down"], rows_d, results_d)
        combine_phase(nc, sems, r, results_d, out)



def _layouts(i):
    def columns(w):
        n = w.shape[1] // P
        return w.reshape(KT, P, n, P).transpose(2, 1, 0, 3)

    def rows(w):
        return w.reshape(KT, P, w.shape[1])

    def vector(v):
        return v.reshape(KT, P).T

    def context(c):
        c = c.transpose(0, 2, 1).reshape(B, KT, P, c.shape[1]).transpose(0, 2, 1, 3)
        return np.pad(c, ((0, 0), (0, 0), (0, 0), (0, 1)))

    ctx = i["ctx_2048"]
    return {
        "x": i["x"], "ctx_img": context(ctx[:, :IMG]), "ctx_txt": context(ctx[:, IMG:]),
        "w_qkv": columns(i["L0_attn_w_qkv"]), "w_self_out": rows(i["L0_attn_w_out"]),
        "lens": np.broadcast_to(i["L0_xattn_context_lens"].reshape(1, 1), (S, 1)),
        "wq": columns(i["L0_xattn_Wq"]), "bq": vector(i["L0_xattn_bq"]), "gq": vector(i["L0_xattn_gq"]),
        "wk": columns(i["L0_xattn_Wk"]), "bk": vector(i["L0_xattn_bk"]), "gk": vector(i["L0_xattn_gk"]),
        "wv": columns(i["L0_xattn_Wv"]), "bv": vector(i["L0_xattn_bv"]),
        "wk_img": columns(i["L0_xattn_Wk_img"]), "bk_img": vector(i["L0_xattn_bk_img"]),
        "gk_img": vector(i["L0_xattn_gk_img"]),
        "wv_img": columns(i["L0_xattn_Wv_img"]), "bv_img": vector(i["L0_xattn_bv_img"]),
        "wo": rows(i["L0_xattn_Wo"]), "bo": i["L0_xattn_bo"],
        "gate": i["L0_ffn_gate_w"].reshape(KT, P, EXPERTS).transpose(1, 0, 2),
        "moe_gate": i["L0_ffn_gate_proj"].reshape(EXPERTS, P, KT * FF),
        "moe_up": i["L0_ffn_up_proj"].reshape(EXPERTS, P, KT * FF),
        "moe_down": i["L0_ffn_down_proj"].reshape(EXPERTS, P, FT * D),
    }


def kernel(**inputs):
    import concourse.bacc as bacc
    from concourse.bass_utils import run_bass_kernel_spmd

    nc = bacc.Bacc("TRN2", target_bir_lowering=False, num_devices=1)
    laid_out = _layouts({name: np.asarray(value) for name, value in inputs.items()})
    arrays, args = {}, {}
    for name, value in laid_out.items():
        value = np.ascontiguousarray(value)
        arrays[f"in_{name}_dram"] = value
        args[name] = nc.dram_tensor(f"in_{name}_dram", value.shape, mybir.dt.from_np(value.dtype),
                                    kind="ExternalInput").ap()
    out = nc.dram_tensor("out_dram", (B, S, D), F32, kind="ExternalOutput").ap()
    decoder_kernel(nc, args, out)
    result = run_bass_kernel_spmd(nc, [arrays], core_ids=[0])
    return result.results[0]["out_dram"]
```

```python
from contextlib import ExitStack

import concourse.bass as bass
import concourse.mybir as mybir
import numpy as np

F32 = mybir.dt.float32
F32R = mybir.dt.float32r
BF16 = mybir.dt.bfloat16
I32 = mybir.dt.int32
ALU = mybir.AluOpType
ACT = mybir.ActivationFunctionType
AX = mybir.AxisListType

P = 128
B, S, D = 8, 100, 1024
HEADS, HD = 16, 64
KT = D // P
BANK = 512
IMG, TXT = 257, 465
LN_EPS, RMS_EPS = 1e-5, 1e-6
HALF = B // 2
SH = HALF * S
CASTS_QKV, CASTS_SELF, CASTS_Q = (0, 40), (40, 32), (72, 26)
CASTS_IMG, CASTS_TXT = ((98, 18), (116, 32)), ((148, 12), (160, 32))


def wait(eng, sem, value):
    if not isinstance(value, int) or value > 0:
        eng.wait_ge(sem, value)


class Scope:

    def __init__(self, nc, ctx, sems, name):
        self.nc, self.ctx, self.sems, self.name = nc, ctx, sems, name

    def sb(self, name, shape, dt=F32):
        return self.ctx.enter_context(self.nc.sbuf_tensor(f"{self.name}_{name}", shape, dt))

    def ps(self, name, shape, dt=F32):
        return self.ctx.enter_context(self.nc.psum_tensor(f"{self.name}_{name}", shape, dt))

    def sem(self, name):
        self.sems.append(self.nc.alloc_semaphore(name=f"{self.name}_{name}"))
        return self.sems[-1]


def clear_semaphores(nc, sems):
    nc.clear_and_free_semaphores(sems)
    nc.all_engine_barrier()
    sems.clear()


def make_identity(eng, ident, cleared, made):
    eng.memset(ident[:, :], 0.0).then_inc(cleared, 1)
    eng.wait_ge(cleared, 1)
    n = ident.shape[1]
    eng.affine_select(out=ident[:, :], in_=ident[:, :], compare_op=ALU.not_equal, fill=1.0, base=0,
                      pattern=[[-1, n]], channel_multiplier=1).then_inc(made, 1)


def split_matmul(eng, out, w_hi, w_lo, a_hi, a_lo, first, last):
    eng.matmul(out, w_hi, a_hi, start=first, stop=False)
    eng.matmul(out, w_hi, a_lo, start=False, stop=False)
    return eng.matmul(out, w_lo, a_hi, start=False, stop=last)


def ln_project_phase(nc, sems, cast, casts, name, x_d, w_d, out_d, scales, bias_d=None, rms=None):
    groups = len(scales)
    with ExitStack() as ctx:
        sc = Scope(nc, ctx, sems, name)
        ident = sc.sb("ident", [P, P])
        x_row = sc.sb("x_row", [S, 2, D])
        xn = sc.sb("xn", [S, 2, D])
        stats = sc.sb("stats", [S, 2, 2, 6])
        mean_var = sc.sb("mean_var", [S, 2, 2])
        std = sc.sb("std", [S, 2])
        rstd = sc.sb("rstd", [S, 2])
        eps = sc.sb("eps", [P, 1])
        xnT_hi = sc.sb("xnT_hi", [P, B, KT, S], F32R)
        xnT_lo = sc.sb("xnT_lo", [P, B, KT, S], F32R)
        w_raw = sc.sb("w_raw", [P, 2, KT, P])
        w_hi = sc.sb("w_hi", [P, 2, KT, P], F32R)
        w_lo = sc.sb("w_lo", [P, 2, KT, P], F32R)
        proj = sc.sb("proj", [P, groups, B, KT, S])
        turn = sc.ps("turn", [P, 4, BANK])
        acc = sc.ps("acc", [P, 4, BANK])

        x_loaded = [sc.sem(f"x_loaded{u}") for u in range(2)]
        w_loaded = [sc.sem(f"w_loaded{u}") for u in range(2)]
        cleared, made = sc.sem("cleared"), sc.sem("made")
        stats_done, stats_seen = sc.sem("stats_done"), sc.sem("stats_seen")
        var_ready = sc.sem("var_ready")
        std_ready, rstd_ready = sc.sem("std_ready"), sc.sem("rstd_ready")
        xn_ready, turned = sc.sem("xn_ready"), sc.sem("turned")
        x_hi_ready, x_split = sc.sem("x_hi_ready"), sc.sem("x_split")
        w_hi_ready, w_split = sc.sem("w_hi_ready"), sc.sem("w_split")
        acc_ready, acc_used = sc.sem("acc_ready"), sc.sem("acc_used")
        stored = sc.sem("stored")
        if rms:
            bias = sc.sb("bias", [P, KT])
            gain = sc.sb("gain", [P, 1 + len(rms[1]), KT])
            ones = sc.sb("ones", [P, P])
            rms_eps = sc.sb("rms_eps", [P, 1])
            square = sc.sb("square", [P, KT, HALF, S])
            sumsq = sc.sb("sumsq", [P, SH])
            scaled = sc.sb("scaled", [P, KT, HALF, S])
            inv_rms = sc.sb("inv_rms", [P, SH])
            small_loaded, gains_made = sc.sem("small_loaded"), sc.sem("gains_made")
            rms_step, sumsq_ready = sc.sem("rms_step"), sc.sem("sumsq_ready")
            total_ready, rms_ready = sc.sem("total_ready"), sc.sem("rms_ready")
            out_ready = sc.sem("out_ready")
        block = ctx.enter_context(nc.Block())

        SLOTS, ACCS = 2, 4

        @block.sync
        def _(sp):
            def load_w(nt, u):
                sp.wait_ge(w_split, nt + 1)
                sp.dma_start(w_raw[:, u], w_d[nt]).then_inc(w_loaded[u], 16)

            if rms:
                sp.dma_start(bias[:, :], bias_d).then_inc(small_loaded, 16)
                for n, g_d in enumerate((rms[0], *rms[1])):
                    sp.dma_start(gain[:, n, :], g_d).then_inc(small_loaded, 16)
            for u in range(2):
                load_w(u, u)
            with sp.Fori(0, B // 2) as g:
                for u in range(2):
                    sp.wait_ge(xn_ready, 2 * g + u + 1)
                    sp.dma_start(x_row[:, u, :], x_d[2 * g + u]).then_inc(x_loaded[u], 16)
            with sp.Fori(1, groups * KT // 2) as g:
                for u in range(2):
                    load_w(2 * g + u, u)
            if rms:
                for h in range(2):
                    for o in range(len(out_d)):
                        sp.wait_ge(out_ready, h * len(out_d) + o + 1)
                        sp.dma_start(out_d[o].rearrange("k p (h s) -> h p k s", h=2)[h],
                                     (scaled, square)[o][:, :].rearrange("p k b s -> p k (b s)")
                                     ).then_inc(stored, 16)
                sp.wait_ge(stored, 2 * len(out_d) * 16)
            else:
                for n in range(groups):
                    sp.wait_ge(acc_used, ACCS + 2 * KT * (n + 1))
                    sp.dma_start(out_d[n], proj[:, n]).then_inc(stored, 16)
                sp.wait_ge(stored, groups * 16)

        @block.gpsimd
        def _(pool):
            pool.memset(eps[:, :], LN_EPS)
            if rms:
                pool.memset(ones[:, :], 1.0)
                pool.memset(rms_eps[:, :], RMS_EPS)
            make_identity(pool, ident, cleared, made)
            cast.start_some(pool, *casts)

        @block.vector
        def _(dve):
            dve.sem_inc(xn_ready, SLOTS)
            dve.sem_inc(x_split, SLOTS)
            dve.sem_inc(w_split, SLOTS)
            with dve.Fori(0, B // 2) as g:
                for u in range(2):
                    dve.wait_ge(x_loaded[u], 16 * g + 16)
                    for c in range(2):
                        dve.bn_stats(stats[:, u, c, :],
                                     x_row[:, u, c * BANK:(c + 1) * BANK]).then_inc(stats_done, 1)
                    dve.wait_ge(stats_done, 4 * g + 2 * u + 2)
                    dve.sem_inc(stats_seen, 1)
                    dve.bn_aggr(mean_var[:, u, :],
                                stats[:, u].rearrange("p c s -> p (c s)")).then_inc(var_ready, 1)
                for u in range(2):
                    b = 2 * g + u
                    dve.wait_ge(std_ready, b + 1)
                    dve.reciprocal(rstd[:, u:u + 1], std[:, u:u + 1]).then_inc(rstd_ready, 1)
                    dve.wait_ge(rstd_ready, b + 1)
                    dve.wait_ge(turned, b + 1)
                    dve.tensor_scalar(xn[:, u, :], x_row[:, u, :], mean_var[:, u, 0:1],
                                      rstd[:, u:u + 1], ALU.subtract, ALU.mult).then_inc(xn_ready, 1)
                for u in range(2):
                    b = 2 * g + u
                    dve.wait_ge(x_hi_ready, b + 1)
                    dve.tensor_tensor(
                        xnT_lo[:, b].rearrange("p (c k) s -> p c (k s)", c=2),
                        turn[:, 2 * u:2 * u + 2, 0:SH],
                        xnT_hi[:, b].bitcast(F32).rearrange("p (c k) s -> p c (k s)", c=2),
                        ALU.subtract).then_inc(x_split, 1)
            with dve.Fori(0, groups * KT // 2) as g:
                for u in range(2):
                    dve.wait_ge(w_hi_ready, 2 * g + u + 1)
                    dve.tensor_tensor(w_lo[:, u], w_raw[:, u], w_hi[:, u].bitcast(F32),
                                      ALU.subtract).then_inc(w_split, 1)
            if rms:
                dve.wait_ge(small_loaded, 16 * (2 + len(rms[1])))
                for n in range(len(rms[1])):
                    dve.tensor_tensor(gain[:, 1 + n, :], gain[:, 1 + n, :], gain[:, 0, :],
                                      ALU.mult).then_inc(gains_made, 1)
                dve.wait_ge(gains_made, len(rms[1]))
                dve.wait_ge(acc_used, ACCS + 2 * KT)
                steps = 0
                for h in range(2):
                    part = proj[:, 0, HALF * h:HALF * (h + 1)]
                    if h:
                        dve.wait_ge(stored, 16 * len(out_d))
                    dve.tensor_tensor(square[:, :].rearrange("p k b s -> p b k s"), part, part, ALU.mult).then_inc(rms_step, 1)
                    dve.wait_ge(rms_step, steps + 1)
                    dve.tensor_reduce(sumsq[:, :].rearrange("p (b s) -> p b s", b=HALF),
                                      square[:, :].rearrange("p k b s -> p b s k"),
                                      AX.X, ALU.add).then_inc(sumsq_ready, 1)
                    dve.wait_ge(rms_ready, h + 1)
                    dve.reciprocal(inv_rms[:, :], inv_rms[:, :]).then_inc(rms_step, 1)
                    dve.wait_ge(rms_step, steps + 2)
                    inv = inv_rms[:, :].rearrange("p (b s) -> p b s", b=HALF)
                    for nt in range(KT):
                        dve.tensor_tensor(part[:, :, nt, :], part[:, :, nt, :], inv,
                                          ALU.mult).then_inc(rms_step, 1)
                    steps += 2 + KT
                    dve.wait_ge(rms_step, steps)
                    for o in range(len(out_d)):
                        for nt in range(KT):
                            last = dve.tensor_scalar((scaled, square)[o][:, nt, :, :], part[:, :, nt, :],
                                                     gain[:, 1 + o, nt:nt + 1], None, ALU.mult)
                        last.then_inc(out_ready, 1)

        @block.scalar
        def _(act):
            act.sem_inc(acc_used, ACCS)
            act.wait_ge(made, 1)
            with act.Fori(0, B // 2) as g:
                for u in range(2):
                    act.wait_ge(var_ready, 2 * g + u + 1)
                    act.activation(std[:, u:u + 1], mean_var[:, u, 1:2], ACT.Sqrt,
                                   bias=eps[0:S, :]).then_inc(std_ready, 1)
                for u in range(2):
                    b = 2 * g + u
                    act.wait_ge(turned, SLOTS + b + 1)
                    act.copy(xnT_hi[:, b].rearrange("p (c k) s -> p c (k s)", c=2),
                             turn[:, 2 * u:2 * u + 2, 0:SH]).then_inc(x_hi_ready, 1)

            def split_w(g, u):
                act.wait_ge(w_loaded[u], 16 * g + 16)
                act.wait_ge(acc_ready, ACCS + 2 * (2 * g + u) - 2)
                act.copy(w_hi[:, u], w_raw[:, u]).then_inc(w_hi_ready, 1)

            if rms:
                act.wait_ge(small_loaded, 16 * (2 + len(rms[1])))
            for n in range(groups):
                with act.Fori(0, KT // 2) as g:
                    for u in range(2):
                        split_w(g + n * (KT // 2), u)
                    for u in range(2):
                        nt = 2 * g + u
                        for h in range(2):
                            act.wait_ge(acc_ready, ACCS + 2 * (n * KT + nt) + h + 1)
                            dst = proj[:, n, HALF * h:HALF * (h + 1), nt, :]
                            src = acc[:, 2 * u + h, 0:SH].rearrange("p (b s) -> p b s", b=HALF)
                            if bias_d is None:
                                done = act.activation(dst, src, ACT.Copy, scale=scales[n])
                            else:
                                done = act.activation(dst, src, ACT.Identity, bias=bias[:, bass.ts(nt, 1)])
                            done.then_inc(acc_used, 1)
            if rms:
                for h in range(2):
                    act.wait_ge(total_ready, h + 1)
                    act.activation(inv_rms[:, :], turn[:, 0, 0:SH], ACT.Sqrt, bias=rms_eps[:, :],
                                   scale=1.0 / D).then_inc(rms_ready, 1)

        @block.tensor
        def _(pe):
            pe.sem_inc(turned, SLOTS)
            pe.sem_inc(acc_ready, ACCS)
            pe.wait_ge(made, 1)
            with pe.Fori(0, B // 2) as g:
                for u in range(2):
                    b = 2 * g + u
                    pe.wait_ge(xn_ready, SLOTS + b + 1)
                    pe.wait_ge(x_split, b + 1)
                    for kt in range(KT):
                        col = (kt % 4) * S
                        mm = pe.transpose(turn[:, 2 * u + kt // 4, col:col + S],
                                          xn[:, u, kt * P:(kt + 1) * P], ident[0:S, 0:S])
                    mm.then_inc(turned, 1)
            pe.wait_ge(x_split, SLOTS + B)
            with pe.Fori(0, groups * KT // 2) as g:
                for u in range(2):
                    nt = 2 * g + u
                    pe.wait_ge(w_split, SLOTS + nt + 1)
                    for h in range(2):
                        pe.wait_ge(acc_used, 2 * nt + h + 1)
                        out = acc[:, 2 * u + h, 0:SH].rearrange("p (b s) -> p b s", b=HALF)
                        for kt in range(KT):
                            half = (slice(None), slice(HALF * h, HALF * (h + 1)), kt)
                            mm = split_matmul(pe, out, w_hi[:, u, kt, :], w_lo[:, u, kt, :],
                                              xnT_hi[half], xnT_lo[half], kt == 0, kt == KT - 1)
                        mm.then_inc(acc_ready, 1)
            if rms:
                for h in range(2):
                    pe.wait_ge(sumsq_ready, h + 1)
                    if h:
                        pe.wait_ge(rms_ready, h)
                    pe.matmul(turn[:, 0, 0:SH], ones[:, :], sumsq[:, :],
                              start=True, stop=True).then_inc(total_ready, 1)


def self_attention_phase(nc, sems, cast, x_d, qkv_d, w_out_d, x1_d):
    QUADS, QP = 2, KT // 2
    with ExitStack() as ctx:
        sc = Scope(nc, ctx, sems, "self")
        ident = sc.sb("ident", [P, P])
        causal = sc.sb("causal", [S, S])
        w_raw = sc.sb("w_raw", [P, 2, D])
        w_hi = sc.sb("w_hi", [P, KT, D], F32R)
        w_lo = sc.sb("w_lo", [P, KT, D], F32R)
        qkvT = sc.sb("qkvT", [P, 3, KT, S])
        v_rows = sc.sb("v_rows", [S, D])
        probs = sc.sb("probs", [S, QUADS, 8, S])
        row_max = sc.sb("row_max", [S, QUADS, 8])
        row_sum = sc.sb("row_sum", [S, QUADS, 8])
        probsT = sc.sb("probsT", [S, QUADS, 8, S])
        at_hi = sc.sb("at_hi", [P, KT, S], F32R)
        at_lo = sc.sb("at_lo", [P, KT, S], F32R)
        x_row = sc.sb("x_row", [S, D])
        x1_row = sc.sb("x1_row", [S, D])
        scores = sc.ps("scores", [P, 2 * QUADS, BANK])
        turn = sc.ps("turn", [P, 2, BANK])
        mixed = sc.ps("mixed", [P, BANK])
        outp = sc.ps("outp", [P, BANK])

        cleared, made = sc.sem("cleared"), sc.sem("made")
        w_loaded = [sc.sem(f"w_loaded{u}") for u in range(2)]
        w_hi_ready, w_split = sc.sem("w_hi_ready"), sc.sem("w_split")
        qkv_loaded, x_loaded = sc.sem("qkv_loaded"), sc.sem("x_loaded")
        scores_ready, masked = sc.sem("scores_ready"), sc.sem("masked")
        centred, exp_ready = sc.sem("centred"), sc.sem("exp_ready")
        soft_step, probs_ready = sc.sem("soft_step"), sc.sem("probs_ready")
        turned, turn_used = sc.sem("turned"), sc.sem("turn_used")
        mixed_ready, at_hi_ready, at_split = sc.sem("mixed_ready"), sc.sem("at_hi_ready"), sc.sem("at_split")
        outp_ready, x1_ready = sc.sem("outp_ready"), sc.sem("x1_ready")
        x1_stored = sc.sem("x1_stored")
        block = ctx.enter_context(nc.Block())


        @block.sync
        def _(sp):
            sp.dma_start(qkvT[:, 0], qkv_d[0][:, 0]).then_inc(qkv_loaded, 16)
            sp.dma_start(qkvT[:, 1], qkv_d[1][:, 0]).then_inc(qkv_loaded, 16)
            sp.dma_start(qkvT[:, 2], qkv_d[2][:, 0]).then_inc(qkv_loaded, 16)
            for kt in range(KT):
                if kt >= 2:
                    sp.wait_ge(w_split, kt - 1)
                sp.dma_start(w_raw[:, kt % 2], w_out_d[kt]).then_inc(w_loaded[kt % 2], 16)
            sp.dma_start(x_row[:, :], x_d[0]).then_inc(x_loaded, 16)

            def load_qkv(b):
                sp.wait_ge(turned, 3 * (b - 1) + 1)
                for n in range(3):
                    sp.dma_start(qkvT[:, n], qkv_d[n][:, b]).then_inc(qkv_loaded, 16)

            def store_x1(b):
                sp.wait_ge(x1_ready, 2 * b + 2)
                sp.dma_start(x1_d[b], x1_row[:, :]).then_inc(x1_stored, 16)

            load_qkv(1)
            with sp.Fori(1, B - 1) as b:
                load_qkv(b + 1)
                store_x1(b - 1)
                sp.dma_start(x_row[:, :], x_d[b]).then_inc(x_loaded, 16)
            store_x1(B - 2)
            sp.dma_start(x_row[:, :], x_d[B - 1]).then_inc(x_loaded, 16)
            store_x1(B - 1)
            sp.wait_ge(x1_stored, 16 * B)

        @block.gpsimd
        def _(pool):
            make_identity(pool, ident, cleared, made)
            pool.memset(causal[:, :], 0.0).then_inc(cleared, 1)
            pool.wait_ge(cleared, 2)
            pool.affine_select(out=causal[:, :], in_=causal[:, :], compare_op=ALU.is_ge, fill=-1e10,
                               base=0, pattern=[[-1, S]], channel_multiplier=1).then_inc(made, 1)
            cast.start_some(pool, *CASTS_SELF)

        @block.vector
        def _(dve):
            STEPS = 2 * 3

            def centre(b, q):
                dve.wait_ge(scores_ready, 2 * b + q + 1)
                rows = probs[:, q].rearrange("s (e j) k -> s e j k", e=2)
                dve.tensor_tensor(rows, scores[0:S, 2 * q:2 * q + 2, 0:QP * S].rearrange(
                    "s e (j k) -> s e j k", j=QP),
                    causal[:, :].unsqueeze(1).unsqueeze(1).broadcast_to([S, 2, QP, S]),
                    ALU.add).then_inc(masked, 1)
                dve.wait_ge(masked, 2 * b + q + 1)
                dve.tensor_reduce(row_max[:, q], probs[:, q], AX.X, ALU.max).then_inc(soft_step, 1)
                dve.wait_ge(soft_step, STEPS * b + q + 1)
                dve.tensor_tensor(probs[:, q], probs[:, q],
                                  row_max[:, q].unsqueeze(2).broadcast_to([S, 8, S]),
                                  ALU.subtract).then_inc(centred, 1)

            def normalise(b, q):
                dve.wait_ge(exp_ready, 2 * b + q + 1)
                dve.tensor_reduce(row_sum[:, q], probs[:, q], AX.X, ALU.add).then_inc(soft_step, 1)
                dve.wait_ge(soft_step, STEPS * b + 2 + 2 * q + 1)
                dve.reciprocal(row_sum[:, q], row_sum[:, q]).then_inc(soft_step, 1)
                dve.wait_ge(soft_step, STEPS * b + 2 + 2 * q + 2)
                dve.tensor_tensor(probs[:, q], probs[:, q],
                                  row_sum[:, q].unsqueeze(2).broadcast_to([S, 8, S]),
                                  ALU.mult).then_inc(probs_ready, 1)

            def add_residual(b, h):
                dve.wait_ge(outp_ready, 2 * b + h + 1)
                if h == 0:
                    dve.wait_ge(x_loaded, 16 * b + 16)
                    wait(dve, x1_stored, 16 * b)
                cols = slice(h * BANK, (h + 1) * BANK)
                dve.tensor_tensor(x1_row[:, cols], outp[0:S, :], x_row[:, cols],
                                  ALU.add).then_inc(x1_ready, 1)

            def split_mixed(b):
                for q in range(QUADS):
                    dve.wait_ge(at_hi_ready, 2 * b + q + 1)
                    hi = at_hi[:, q * QP:(q + 1) * QP]
                    dve.tensor_tensor(at_lo[:, q * QP:(q + 1) * QP],
                                      mixed[:, 0:QP * S].rearrange("p (j s) -> p j s", j=QP),
                                      hi.bitcast(F32), ALU.subtract).then_inc(at_split, 1)

            dve.wait_ge(made, 2)
            for q in range(QUADS):
                centre(0, q)
            for q in range(QUADS):
                normalise(0, q)
            split_mixed(0)
            for kt in range(KT):
                dve.wait_ge(w_hi_ready, kt + 1)
                dve.tensor_tensor(w_lo[:, kt], w_raw[:, kt % 2], w_hi[:, kt].bitcast(F32),
                                  ALU.subtract).then_inc(w_split, 1)
            with dve.Fori(1, B) as b:
                for q in range(QUADS):
                    centre(b, q)
                for q in range(QUADS):
                    normalise(b, q)
                    add_residual(b - 1, q)
                split_mixed(b)
            for h in range(2):
                add_residual(B - 1, h)

        @block.scalar
        def _(act):
            def attend(b):
                act.wait_ge(turned, 3 * b + 1)
                wait(act, mixed_ready, 2 * b)
                act.copy(v_rows[:, :].rearrange("s (c n) -> s c n", c=2),
                         turn[0:S, :, :]).then_inc(turn_used, 1)
                for q in range(QUADS):
                    act.wait_ge(centred, 2 * b + q + 1)
                    act.activation(probs[:, q], probs[:, q], ACT.Exp).then_inc(exp_ready, 1)
                for q in range(QUADS):
                    act.wait_ge(turned, 3 * b + 2 + q)
                    act.copy(probsT[:, q].rearrange("k (e j) s -> k e (j s)", e=2),
                             turn[0:S, :, 0:QP * S]).then_inc(turn_used, 1)
                for q in range(QUADS):
                    act.wait_ge(mixed_ready, 2 * b + q + 1)
                    act.copy(at_hi[:, q * QP:(q + 1) * QP],
                             mixed[:, 0:QP * S].rearrange("p (j s) -> p j s", j=QP)).then_inc(at_hi_ready, 1)

            attend(0)
            for kt in range(KT):
                act.wait_ge(w_loaded[kt % 2], 16 * (kt // 2) + 16)
                act.copy(w_hi[:, kt], w_raw[:, kt % 2]).then_inc(w_hi_ready, 1)
            with act.Fori(1, B) as b:
                attend(b)

        @block.tensor
        def _(pe):
            def attend_scores(b):
                pe.wait_ge(qkv_loaded, 48 * b + 48)
                for q in range(QUADS):
                    wait(pe, masked, 2 * (b - 1) + q + 1)
                    for j in range(QP):
                        for e in range(2):
                            rows = slice(e * HD, (e + 1) * HD)
                            mm = pe.matmul(scores[0:S, 2 * q + e, j * S:(j + 1) * S],
                                           qkvT[rows, 0, q * QP + j, :], qkvT[rows, 1, q * QP + j, :],
                                           start=True, stop=True)
                    mm.then_inc(scores_ready, 1)
                wait(pe, turn_used, 3 * b)
                for nt in range(KT):
                    mm = pe.transpose(turn[0:S, nt // 4, (nt % 4) * P:(nt % 4 + 1) * P],
                                      qkvT[:, 2, nt, :], ident[:, :])
                mm.then_inc(turned, 1)

            def attend_mix(b):
                for q in range(QUADS):
                    pe.wait_ge(probs_ready, 2 * b + q + 1)
                    pe.wait_ge(turn_used, 3 * b + 1 + q)
                    for e in range(2):
                        for j in range(QP):
                            mm = pe.transpose(turn[0:S, e, j * S:(j + 1) * S], probs[:, q, e * QP + j, :],
                                              ident[0:S, 0:S])
                    mm.then_inc(turned, 1)
                for q in range(QUADS):
                    pe.wait_ge(turn_used, 3 * b + 2 + q)
                    wait(pe, at_split, 2 * b + q)
                    for j in range(QP):
                        for e in range(2):
                            head = 2 * (q * QP + j) + e
                            mm = pe.matmul(mixed[e * HD:(e + 1) * HD, j * S:(j + 1) * S],
                                           v_rows[:, head * HD:(head + 1) * HD], probsT[:, q, e * QP + j, :],
                                           start=True, stop=True)
                    mm.then_inc(mixed_ready, 1)

            def project(b):
                pe.wait_ge(at_split, 2 * b + 2)
                for h in range(2):
                    wait(pe, x1_ready, 2 * b + h)
                    for kt in range(KT):
                        cols = slice(h * BANK, (h + 1) * BANK)
                        mm = split_matmul(pe, outp[0:S, :], at_hi[:, kt, :], at_lo[:, kt, :],
                                          w_hi[:, kt, cols], w_lo[:, kt, cols], kt == 0, kt == KT - 1)
                    mm.then_inc(outp_ready, 1)

            pe.wait_ge(made, 1)
            attend_scores(0)
            attend_mix(0)
            pe.wait_ge(w_split, KT)
            with pe.Fori(1, B) as b:
                attend_scores(b)
                project(b - 1)
                attend_mix(b)
            project(B - 1)


MIX_LAG = 2
K_SLOTS = 4


class Part:

    def __init__(self, width, real, tiles, batches, groups, raw_slots):
        self.width, self.real, self.tiles = width, real, tiles
        self.batches, self.groups, self.raw_slots = batches, groups, raw_slots
        self.cols = batches * width
        self.of_group = B // groups
        self.units = self.of_group // batches
        self.rows = tiles[0][1]
        self.runs = []
        for t, (_, rows) in enumerate(tiles):
            if self.runs and self.runs[-1][2] == rows:
                self.runs[-1][1] += 1
            else:
                self.runs.append([t, 1, rows])
        self.steps = KT * self.units
        self.lag = MIX_LAG // batches
        assert self.cols <= BANK and 2 * self.units % K_SLOTS == 0

    def over_steps(self, eng, lag, step):
        u = self.units
        for c in range(u):
            step(0, c)
        with eng.Fori(0, KT // 2 - 1) as g:
            for c in range(u, 3 * u):
                step(g, c)
        for c in range(u, 2 * u + lag):
            step(KT // 2 - 1, c)

    def at(self, g, c):
        return 2 * self.units * g + c, 2 * g + c // self.units

    def on(self, step):
        return not isinstance(step, int) or 0 <= step < self.steps

    def ring(self, group, stage):
        return group * (2 * self.steps + self.units) + (0, self.steps, self.steps + self.units)[stage]

    def squares(self, group, step):
        return 2 * (group * self.steps + step)


IMG_PART = Part(IMG + 1, IMG, [(0, 86), (86, 86), (172, 86)], 1, 1, 2)
TXT_SHORT = Part(160, 160, [(0, 80), (80, 80)], 2, 1, 2)
TXT_FULL = Part(TXT + 1, TXT, [(0, P), (P, P), (2 * P, P), (3 * P, TXT - 3 * P)], 1, 2, 1)
MASKED = -2.0 ** 127
SCALE = HD ** -0.5


class CrossSems:

    def __init__(self, sc):
        sem = sc.sem
        self.ctx_loaded = [sem(f"ctx_loaded{u}") for u in range(2)]
        self.ctx_hi_ready = sem("ctx_hi_ready")
        self.ctx_split = sem("ctx_split")
        self.w_loaded = [sem(f"w_loaded{u}") for u in range(2)]
        self.w_hi_ready = sem("w_hi_ready")
        self.w_split = sem("w_split")
        self.acc_ready = sem("acc_ready")
        self.act_step = sem("act_step")
        self.acc_used = sem("acc_used")
        self.k_stored = [sem(f"k_stored{u}") for u in range(K_SLOTS)]
        self.squared = sem("squared")
        self.inverted = sem("inverted")
        self.k_loaded = [sem(f"k_loaded{u}") for u in range(K_SLOTS)]
        self.k_ready = sem("k_ready")
        self.q_loaded = [sem(f"q_loaded{u}") for u in range(2)]
        self.old_loaded = [sem(f"old_loaded{u}") for u in range(2)]
        self.v_turned = sem("v_turned")
        self.v_used = sem("v_used")
        self.scores_ready = sem("scores_ready")
        self.masked = sem("masked")
        self.max_ready = sem("max_ready")
        self.shift_ready = sem("shift_ready")
        self.exp_ready = sem("exp_ready")
        self.sum_inverted = sem("sum_inverted")
        self.probs_ready = sem("probs_ready")
        self.p_turned = sem("p_turned")
        self.p_used = sem("p_used")
        self.mixed_ready = sem("mixed_ready")
        self.mixed_used = sem("mixed_used")
        self.stored = [sem(f"stored{u}") for u in range(2)]


class CrossMemory:

    def __init__(self, sc, parts):
        cols = max(p.cols for p in parts)
        width = max(p.width for p in parts)
        rows = max(p.rows for p in parts)
        tiles = max(len(p.tiles) for p in parts)
        v_tiles = max(len(p.tiles) * p.batches for p in parts)
        all_cols = max(p.cols * p.units for p in parts)
        raw = max(p.raw_slots * p.cols for p in parts)
        self.ident = sc.sb("ident", [P, P])
        self.ones = sc.sb("ones", [P, P])
        self.eps = sc.sb("eps", [P, 1])
        self.bias = sc.sb("bias", [P, 2, KT])
        self.ctx_hi = sc.sb("ctx_hi", [P, KT, all_cols], F32R)
        self.ctx_lo = sc.sb("ctx_lo", [P, KT, all_cols], F32R)
        self.raw = sc.sb("raw", [P, KT * raw])
        self.w_raw = sc.sb("w_raw", [P, 2, KT, P])
        self.w_hi = sc.sb("w_hi", [P, 2, KT, P], F32R)
        self.w_lo = sc.sb("w_lo", [P, 2, KT, P], F32R)
        self.norm = sc.sb("norm", [P, all_cols])
        self.square = sc.sb("square", [P, cols])
        self.kT = sc.sb("kT", [P, K_SLOTS, cols])
        self.vT = sc.sb("vT", [P, 2, cols])
        self.v = sc.sb("v", [rows, K_SLOTS, v_tiles, P])
        self.row_max = sc.sb("row_max", [S, 2, 2])
        self.shift = sc.sb("shift", [S, 2, 2])
        self.row_sum = sc.sb("row_sum", [S, 2, 2])
        self.probs = sc.sb("probs", [S, 2, 2, width])
        self.probsT = sc.sb("probsT", [rows, 2, tiles, S])
        self.acc = sc.ps("acc", [P, 2, BANK])
        self.scores = sc.ps("scores", [P, 2, BANK])
        self.v_turn = sc.ps("v_turn", [P, BANK])
        self.p_turn = sc.ps("p_turn", [P, 2, BANK])
        self.mixed = sc.ps("mixed", [P, BANK])

    def ctx_raw(self, part, slot):
        n = KT * part.cols
        return self.raw[:, slot * n:(slot + 1) * n].rearrange("p (k n) -> p k n", k=KT)

    def q(self, slot):
        return self.raw[:, slot * B * S:(slot + 1) * B * S]

    def attn(self, slot):
        return self.q(2 + slot)


def cross_sp(sp, m, s, part, ctx_d, w_d, k_d, q_d, old_d, out_d):
    U, BS, slots = part.units, part.batches, part.raw_slots

    def load_ctx(group, u):
        cu = group * U + u
        wait(sp, s.ctx_split, cu - slots + 1)
        for i in range(BS):
            b = group * part.of_group + u * BS + i
            sp.dma_start(m.ctx_raw(part, u % slots)[:, :, i * part.width:(i + 1) * part.width],
                         ctx_d[b][:, :, 0:part.width]).then_inc(s.ctx_loaded[u % slots], 16)

    def load_w(group, w, slot):
        wait(sp, s.w_split, 2 * KT * group + w - 1)
        sp.dma_start(m.w_raw[:, slot], w_d[w]).then_inc(s.w_loaded[slot], 16)

    for group in range(part.groups):
        first = group * part.steps
        tokens = slice(group * part.of_group * S, (group + 1) * part.of_group * S)

        def step_k(g, c):
            t, nt = part.at(g, c)
            if isinstance(t, int) and t + slots < U:
                load_ctx(group, t + slots)
            if c % U == 0:
                load_w(group, nt + 1, (c // U + 1) % 2)
            sp.wait_ge(s.acc_used, part.ring(group, 0) + t + 1)
            sp.dma_start(k_d[nt, c % U][:, 0:part.cols],
                         m.kT[:, c % K_SLOTS, 0:part.cols]).then_inc(s.k_stored[c % K_SLOTS], 16)

        def load_k(g, c):
            t, nt = part.at(g, c)
            if part.on(t):
                wait(sp, s.scores_ready, BS * (first + t - K_SLOTS + 1))
                sp.dma_start(m.kT[:, c % K_SLOTS, 0:part.cols],
                             k_d[nt, c % U][:, 0:part.cols]).then_inc(s.k_loaded[c % K_SLOTS], 16)

        def load_q(nt, slot):
            wait(sp, s.scores_ready, BS * (first + U * (nt - 1)))
            sp.dma_start(m.q(slot)[:, 0:part.of_group * S], q_d[nt][:, tokens]).then_inc(s.q_loaded[slot], 16)

        def load_old(nt, slot, before):
            if old_d is not None:
                wait(sp, s.stored[slot], 16 * before)
                sp.dma_start(m.attn(slot)[:, 0:part.of_group * S],
                             old_d[nt][:, tokens]).then_inc(s.old_loaded[slot], 16)

        def store(nt, slot):
            sp.wait_ge(s.mixed_used, BS * (first + U * (nt + 1)))
            sp.dma_start(out_d[nt][:, tokens], m.attn(slot)[:, 0:part.of_group * S]).then_inc(s.stored[slot], 16)

        def step_v(g, c):
            t, nt = part.at(g, c)
            other = (c // U + 1) % 2
            load_k(g, c + K_SLOTS - 1)
            last = isinstance(nt, int) and nt == KT - 1
            if c % U == 0 and not last:
                load_w(group, KT + nt + 1, other)
                load_q(nt + 1, other)
            if c % U == U // 2 and not (isinstance(nt, int) and nt == 0):
                store(nt - 1, other)
            if c % U == U - 1 and not last:
                load_old(nt + 1, other, KT // 2 * group + g + (c // U + 1) // 2)

        if group:
            for u in range(2):
                sp.wait_ge(s.stored[u], 16 * (KT // 2) * group)
        load_w(group, 0, 0)
        for u in range(min(slots, U)):
            load_ctx(group, u)
        part.over_steps(sp, 0, step_k)
        for u in range(K_SLOTS):
            sp.wait_ge(s.k_stored[u], 16 * (part.steps // K_SLOTS) * (group + 1))
        sp.wait_ge(s.squared, part.squares(group, part.steps))
        sp.wait_ge(s.ctx_split, U * (group + 1))
        load_q(0, 0)
        load_old(0, 0, KT // 2 * group)
        for c in range(K_SLOTS - 1):
            load_k(0, c)
        part.over_steps(sp, 0, step_v)
        store(KT - 1, (KT - 1) % 2)
    for u in range(2):
        sp.wait_ge(s.stored[u], 16 * (KT // 2) * part.groups)


def cross_pool(pool, m, s, part, cast, casts):
    U = part.units
    every = KT * U // casts[1][1]
    for group in range(part.groups):
        def step(g, c):
            t, _ = part.at(g, c)
            if group == 0 and c % every == 0:
                cast.start(pool, casts[1][0] // 2 + U // every * g + c // every // 2, c // every % 2)
            pool.wait_ge(s.k_loaded[c % K_SLOTS],
                         16 * (part.steps // K_SLOTS * group + 2 * U // K_SLOTS * g + c // K_SLOTS + 1))
            k = m.kT[:, c % K_SLOTS, 0:part.cols]
            cols = c % U * part.cols
            pool.tensor_tensor(k, k, m.norm[:, cols:cols + part.cols], ALU.mult).then_inc(s.k_ready, 1)

        if group == 0:
            cast.start_some(pool, *casts[0])
        pool.wait_ge(s.inverted, U * (group + 1))
        part.over_steps(pool, 0, step)


def cross_act(act, m, s, part, masked):
    U, BS, n, slots = part.units, part.batches, part.cols, part.raw_slots

    for group in range(part.groups):
        first = group * part.steps
        keys, sums, values = (part.ring(group, stage) for stage in range(3))

        def split_ctx(u):
            cu = group * U + u
            act.wait_ge(s.ctx_loaded[u % slots], 16 * BS * (cu // slots + 1))
            wait(act, s.acc_ready, keys)
            act.copy(m.ctx_hi[:, :, u * n:(u + 1) * n], m.ctx_raw(part, u % slots)).then_inc(s.ctx_hi_ready, 1)

        def split_w(g, w, slot, used):
            act.wait_ge(s.w_loaded[slot], 16 * (KT * group + g + 1))
            wait(act, s.acc_ready, used)
            act.copy(m.w_hi[:, slot], m.w_raw[:, slot]).then_inc(s.w_hi_ready, 1)

        def step_k(g, c):
            t, nt = part.at(g, c)
            if isinstance(t, int) and t + slots < U:
                split_ctx(t + slots)
            act.wait_ge(s.acc_ready, keys + t + 1)
            wait(act, s.k_stored[c % K_SLOTS],
                 16 * (part.steps // K_SLOTS * group + 2 * U // K_SLOTS * g + c // K_SLOTS))
            wait(act, s.squared, part.squares(group, t - K_SLOTS + 1))
            act.sem_inc(s.act_step, 1)
            act.activation(m.kT[:, c % K_SLOTS, 0:n], m.acc[:, c % 2, 0:n], ACT.Identity,
                           bias=m.bias[:, 0, bass.ts(nt, 1)]).then_inc(s.acc_used, 1)
            if c % U == U // 2:
                split_w(g + (c // U + 1) // 2, nt + 1, (c // U + 1) % 2, keys + U * nt)

        def collect_v(g, c):
            t, nt = part.at(g, c)
            if part.on(t):
                act.wait_ge(s.acc_ready, values + t + 1)
                wait(act, s.v_turned, first + t - 1)
                act.sem_inc(s.act_step, 1)
                act.activation(m.vT[:, c % 2, 0:n], m.acc[:, (values + c) % 2, 0:n], ACT.Identity,
                               bias=m.bias[:, 1, bass.ts(nt, 1)]).then_inc(s.acc_used, 1)

        def exponentials(t, c, i):
            if part.on(t):
                a, slot = BS * (first + t) + i, (BS * c + i) % 2
                act.wait_ge(s.shift_ready, a + 1)
                for e in range(2):
                    src = (m.probs[:, slot, e, 0:part.real] if masked else m.scores[0:S, e, 0:part.real])
                    done = act.activation(m.probs[:, slot, e, 0:part.real], src, ACT.Exp,
                                          bias=m.shift[:, slot, e:e + 1], scale=SCALE,
                                          accum_out=m.row_sum[:, slot, e:e + 1])
                done.then_inc(s.exp_ready, 1)

        def collect_probs(a):
            act.wait_ge(s.p_turned, a + 1)
            for t, count, rows in part.runs:
                done = act.copy(m.probsT[0:rows, :, t:t + count, :],
                                m.p_turn[0:rows, :, t * S:(t + count) * S].rearrange(
                                    "k e (t s) -> k e t s", t=count))
            done.then_inc(s.p_used, 1)

        def step_v(g, c):
            t, nt = part.at(g, c)
            for i in range(BS):
                exponentials(t, c, i)
                if i == BS - 1:
                    collect_v(g, c + 1)
                    if c % U == U // 2 and not (isinstance(nt, int) and nt >= KT - 1):
                        split_w(g + (c // U + 1) // 2 + KT // 2, KT + nt + 1, (c // U + 1) % 2, values + U * nt)
                if part.on(t if i else t - 1):
                    collect_probs(BS * (first + t) + i - 1)

        split_w(0, 0, 0, keys)
        for u in range(min(slots, U)):
            split_ctx(u)
        part.over_steps(act, 0, step_k)
        for u in range(U):
            act.wait_ge(s.acc_ready, sums + u + 1)
            act.activation(m.norm[:, u * n:(u + 1) * n], m.acc[:, (sums + u) % 2, 0:n], ACT.Sqrt,
                           bias=m.eps[:, :], scale=1.0 / D).then_inc(s.acc_used, 1)
        collect_v(0, 0)
        part.over_steps(act, part.lag, step_v)


def cross_dve(dve, m, s, part, mask, add):
    U, BS, n, slots = part.units, part.batches, part.cols, part.raw_slots

    for group in range(part.groups):
        first = group * part.steps
        keys, sums, _ = (part.ring(group, stage) for stage in range(3))

        def split_ctx(u):
            dve.wait_ge(s.ctx_hi_ready, group * U + u + 1)
            cols = slice(u * n, (u + 1) * n)
            dve.tensor_tensor(m.ctx_lo[:, :, cols], m.ctx_raw(part, u % slots), m.ctx_hi[:, :, cols].bitcast(F32),
                              ALU.subtract).then_inc(s.ctx_split, 1)

        def split_w(w, slot):
            dve.wait_ge(s.w_hi_ready, 2 * KT * group + w + 1)
            dve.tensor_tensor(m.w_lo[:, slot], m.w_raw[:, slot], m.w_hi[:, slot].bitcast(F32),
                              ALU.subtract).then_inc(s.w_split, 1)

        def step_k(g, c):
            t, nt = part.at(g, c)
            if isinstance(t, int) and t + slots < U:
                split_ctx(t + slots)
            dve.wait_ge(s.acc_used, keys + t + 1)
            k, u = m.kT[:, c % K_SLOTS, 0:n], c % U
            total = m.norm[:, u * n:(u + 1) * n]
            if isinstance(t, int) and t < U:
                dve.tensor_tensor(total, k, k, ALU.mult).then_inc(s.squared, 2)
            else:
                done = part.squares(group, t)
                dve.wait_ge(s.squared, done)
                dve.tensor_tensor(m.square[:, 0:n], k, k, ALU.mult).then_inc(s.squared, 1)
                dve.wait_ge(s.squared, done + 1)
                dve.tensor_tensor(total, total, m.square[:, 0:n], ALU.add).then_inc(s.squared, 1)
            if c % U == U // 2:
                split_w(nt + 1, (c // U + 1) % 2)

        def maxima(t, c, i):
            if not part.on(t):
                return
            a, slot = BS * (first + t) + i, (BS * c + i) % 2
            dve.wait_ge(s.scores_ready, a + 1)
            src = m.scores[0:S, :, 0:part.real]
            if mask is not None:
                src = m.probs[:, slot, :, 0:part.real]
                dve.tensor_tensor(src, m.scores[0:S, :, 0:part.real],
                                  mask[:, 0:part.real].unsqueeze(1).broadcast_to([S, 2, part.real]),
                                  ALU.add).then_inc(s.masked, 1)
                dve.wait_ge(s.masked, a + 1)
            dve.tensor_reduce(m.row_max[:, slot, :], src, AX.X, ALU.max).then_inc(s.max_ready, 1)
            dve.wait_ge(s.max_ready, a + 1)
            dve.tensor_scalar(m.shift[:, slot, :], m.row_max[:, slot, :], -SCALE, None,
                              ALU.mult).then_inc(s.shift_ready, 1)

        def normalise(a, slot):
            dve.wait_ge(s.exp_ready, a + 1)
            dve.reciprocal(m.row_sum[:, slot, :], m.row_sum[:, slot, :]).then_inc(s.sum_inverted, 1)
            dve.wait_ge(s.sum_inverted, a + 1)
            for e in range(2):
                p = m.probs[:, slot, e, 0:part.real]
                done = dve.tensor_scalar(p, p, m.row_sum[:, slot, e:e + 1], None, ALU.mult)
            done.then_inc(s.probs_ready, 1)

        def collect(g, c, i):
            t, _ = part.at(g, c)
            if not part.on(t):
                return
            dve.wait_ge(s.mixed_ready, BS * (first + t) + i + 1)
            slot, u = c // U % 2, c % U
            if u == 0 and i == 0:
                before = KT // 2 * group + g + c // U // 2
                if add:
                    dve.wait_ge(s.old_loaded[slot], 16 * before + 16)
                else:
                    wait(dve, s.stored[slot], 16 * before)
            col = (u * BS + i) * S
            dst, src = m.attn(slot)[:, col:col + S], m.mixed[:, 0:S]
            if add:
                done = dve.tensor_tensor(dst, src, dst, ALU.add)
            else:
                done = dve.tensor_copy(dst, src)
            done.then_inc(s.mixed_used, 1)

        def step_v(g, c):
            t, nt = part.at(g, c)
            for i in range(BS):
                maxima(t, c, i)
                if part.on(t if i else t - 1):
                    normalise(BS * (first + t) + i - 1, (BS * c + i - 1) % 2)
                collect(g, c - part.lag, i)
                if i == BS - 1 and c % U == U // 2 and not (isinstance(nt, int) and nt >= KT - 1):
                    split_w(KT + nt + 1, (c // U + 1) % 2)
            if part.on(t):
                dve.wait_ge(s.v_turned, first + t + 1)
                for i in range(BS):
                    for tile, count, rows in part.runs:
                        at = i * len(part.tiles) + tile
                        done = dve.tensor_copy(m.v[0:rows, c % K_SLOTS, at:at + count, :],
                                               m.v_turn[0:rows, at * P:(at + count) * P].rearrange(
                                                   "k (t n) -> k t n", t=count))
                done.then_inc(s.v_used, 1)

        split_w(0, 0)
        for u in range(min(slots, U)):
            split_ctx(u)
        part.over_steps(dve, 0, step_k)
        for u in range(U):
            dve.wait_ge(s.acc_used, sums + u + 1)
            norm = m.norm[:, u * n:(u + 1) * n]
            dve.reciprocal(norm, norm).then_inc(s.inverted, 1)
        part.over_steps(dve, part.lag, step_v)


def cross_pe(pe, m, s, part, masked):
    U, BS, n = part.units, part.batches, part.cols
    scores_left = s.masked if masked else s.exp_ready
    half = KT // BS

    for group in range(part.groups):
        first = group * part.steps
        keys, sums, values = (part.ring(group, stage) for stage in range(3))

        def product(r, bank, slot, u, kts):
            if kts[0] == 0:
                wait(pe, s.acc_used, r - 1)
            for kt in kts:
                cols = slice(u * n, (u + 1) * n)
                mm = split_matmul(pe, m.acc[:, bank, 0:n], m.w_hi[:, slot, kt, :], m.w_lo[:, slot, kt, :],
                                  m.ctx_hi[:, kt, cols], m.ctx_lo[:, kt, cols], kt == 0, kt == KT - 1)
            if kts[-1] == KT - 1:
                mm.then_inc(s.acc_ready, 1)

        def step_k(g, c):
            t, nt = part.at(g, c)
            if c % U == 0:
                pe.wait_ge(s.w_split, 2 * KT * group + nt + 1)
            if isinstance(t, int) and t < U:
                pe.wait_ge(s.ctx_split, group * U + t + 1)
            product(keys + t, (keys + c) % 2, c // U % 2, c % U, range(KT))

        def value(g, c, i):
            t, nt = part.at(g, c)
            if part.on(t):
                if c % U == 0 and i == 0:
                    pe.wait_ge(s.w_split, 2 * KT * group + KT + nt + 1)
                product(values + t, (values + c) % 2, c // U % 2, c % U, range(i * half, (i + 1) * half))

        def scores(g, c, i):
            t, _ = part.at(g, c)
            if not part.on(t):
                return
            slot, u = c // U % 2, c % U
            if i == 0:
                if u == 0:
                    pe.wait_ge(s.q_loaded[slot], 16 * (KT // 2 * group + g + c // U // 2 + 1))
                pe.wait_ge(s.k_ready, first + t + 1)
            wait(pe, scores_left, BS * (first + t) + i)
            col = (u * BS + i) * S
            for e in range(2):
                rows = slice(e * HD, (e + 1) * HD)
                mm = pe.matmul(m.scores[0:S, e, 0:part.real], m.q(slot)[rows, col:col + S],
                               m.kT[rows, c % K_SLOTS, i * part.width:i * part.width + part.real],
                               start=True, stop=True)
            mm.then_inc(s.scores_ready, 1)

        def turn_probs(a, slot):
            pe.wait_ge(s.probs_ready, a + 1)
            wait(pe, s.p_used, a)
            for e in range(2):
                for t, (start, rows) in enumerate(part.tiles):
                    mm = pe.transpose(m.p_turn[0:rows, e, t * S:(t + 1) * S],
                                      m.probs[:, slot, e, start:start + rows], m.ident[0:S, 0:S])
            mm.then_inc(s.p_turned, 1)

        def mix(g, c, i):
            t, _ = part.at(g, c)
            if not part.on(t):
                return
            a = BS * (first + t) + i
            if i == 0:
                pe.wait_ge(s.v_used, first + t + 1)
            pe.wait_ge(s.p_used, a + 1)
            wait(pe, s.mixed_used, a)
            for tile, (_, rows) in enumerate(part.tiles):
                for e in range(2):
                    at = i * len(part.tiles) + tile
                    mm = pe.matmul(m.mixed[e * HD:(e + 1) * HD, 0:S],
                                   m.v[0:rows, c % K_SLOTS, at, e * HD:(e + 1) * HD],
                                   m.probsT[0:rows, e, tile, :], start=tile == 0, stop=tile == len(part.tiles) - 1)
            mm.then_inc(s.mixed_ready, 1)

        def turn_v(g, c):
            t, _ = part.at(g, c)
            if not part.on(t):
                return
            pe.wait_ge(s.acc_used, values + t + 1)
            wait(pe, s.v_used, first + t)
            for i in range(BS):
                for tile, (start, rows) in enumerate(part.tiles):
                    at, col = i * len(part.tiles) + tile, i * part.width + start
                    mm = pe.transpose(m.v_turn[0:rows, at * P:(at + 1) * P],
                                      m.vT[:, c % 2, col:col + rows], m.ident[:, :])
            mm.then_inc(s.v_turned, 1)

        def step_v(g, c):
            t, _ = part.at(g, c)
            for i in range(BS):
                scores(g, c, i)
                mix(g, c - part.lag, i)
                value(g, c + 1, i)
                if part.on(t if i else t - 1):
                    turn_probs(BS * (first + t) + i - 1, (BS * c + i - 1) % 2)
            turn_v(g, c)

        part.over_steps(pe, 0, step_k)
        pe.wait_ge(s.squared, part.squares(group, part.steps))
        for u in range(U):
            wait(pe, s.acc_used, sums + u - 1)
            pe.matmul(m.acc[:, (sums + u) % 2, 0:n], m.ones[:, :], m.norm[:, u * n:(u + 1) * n],
                      start=True, stop=True).then_inc(s.acc_ready, 1)
        for i in range(BS):
            value(0, 0, i)
        part.over_steps(pe, part.lag, step_v)


def cross_image_phase(nc, sems, cast, ctx_d, w_d, bias_d, k_d, q_d, out_d):
    part = IMG_PART
    with ExitStack() as ctx:
        sc = Scope(nc, ctx, sems, "img")
        m, s = CrossMemory(sc, [part]), CrossSems(sc)
        cleared, made, bias_loaded = sc.sem("cleared"), sc.sem("made"), sc.sem("bias_loaded")
        block = ctx.enter_context(nc.Block())

        @block.sync
        def _(sp):
            for n in range(2):
                sp.dma_start(m.bias[:, n, :], bias_d[n]).then_inc(bias_loaded, 16)
            cross_sp(sp, m, s, part, ctx_d, w_d, k_d, q_d, None, out_d)

        @block.gpsimd
        def _(pool):
            make_identity(pool, m.ident, cleared, made)
            pool.memset(m.ones[:, :], 1.0)
            pool.memset(m.probs[:, :, :, part.real:part.width], 0.0)
            pool.memset(m.eps[:, :], RMS_EPS).then_inc(made, 1)
            cross_pool(pool, m, s, part, cast, CASTS_IMG)

        @block.vector
        def _(dve):
            cross_dve(dve, m, s, part, None, False)

        @block.scalar
        def _(act):
            act.wait_ge(made, 2)
            act.wait_ge(bias_loaded, 32)
            cross_act(act, m, s, part, False)

        @block.tensor
        def _(pe):
            pe.wait_ge(made, 2)
            cross_pe(pe, m, s, part, False)


def cross_text_phase(nc, sems, cast, ctx_d, w_d, bias_d, lens_d, k_d, q_d, old_d, out_d):
    with ExitStack() as ctx:
        sc = Scope(nc, ctx, sems, "txt")
        m = CrossMemory(sc, [TXT_SHORT, TXT_FULL])
        s = CrossSems(sc)
        mask = sc.sb("mask", [S, TXT])
        length = sc.sb("length", [S, 1])
        outside = sc.sb("outside", [S, 2])
        full = sc.sb("full", [S, 1], I32)
        cleared, made, bias_loaded = sc.sem("cleared"), sc.sem("made"), sc.sem("bias_loaded")
        len_loaded, len_step, mask_ready = sc.sem("len_loaded"), sc.sem("len_step"), sc.sem("mask_ready")
        key_index = m.probs[:, 0, 0, 0:TXT].bitcast(I32)
        len_int = full[:, :]
        block = ctx.enter_context(nc.Block())

        def by_length(eng, run):
            eng.wait_ge(mask_ready, 3)
            is_full = eng.value_load(full[0:1, 0:1], min_val=0, max_val=1)
            with eng.If(is_full > 0):
                run(TXT_FULL)
            with eng.Else():
                run(TXT_SHORT)

        @block.sync
        def _(sp):
            sp.dma_start(len_int, lens_d).then_inc(len_loaded, 16)
            for n in range(2):
                sp.dma_start(m.bias[:, n, :], bias_d[n]).then_inc(bias_loaded, 16)
            by_length(sp, lambda part: cross_sp(sp, m, s, part, ctx_d, w_d, k_d, q_d, old_d, out_d))

        @block.gpsimd
        def _(pool):
            make_identity(pool, m.ident, cleared, made)
            pool.iota(key_index, [[1, TXT]], base=0, channel_multiplier=0).then_inc(made, 1)
            pool.memset(m.ones[:, :], 1.0)
            pool.memset(m.eps[:, :], RMS_EPS).then_inc(made, 1)
            by_length(pool, lambda part: cross_pool(pool, m, s, part, cast, CASTS_TXT))

        @block.vector
        def _(dve):
            dve.wait_ge(len_loaded, 16)
            dve.wait_ge(made, 2)
            dve.tensor_copy(length[:, :], len_int).then_inc(len_step, 1)
            dve.tensor_copy(mask[:, :], key_index).then_inc(len_step, 1)
            dve.wait_ge(len_step, 2)
            dve.tensor_scalar(mask[:, :], mask[:, :], length[:, :], MASKED, ALU.is_ge,
                              ALU.mult).then_inc(mask_ready, 1)
            dve.tensor_scalar(outside[:, 0:1], length[:, :], float(TXT_SHORT.real), None,
                              ALU.is_gt).then_inc(len_step, 1)
            dve.tensor_scalar(outside[:, 1:2], length[:, :], 1.0, None, ALU.is_lt).then_inc(len_step, 1)
            dve.wait_ge(len_step, 4)
            dve.tensor_reduce(outside[:, 0:1], outside[:, :], AX.X, ALU.max).then_inc(mask_ready, 1)
            dve.wait_ge(mask_ready, 2)
            dve.tensor_copy(full[:, :], outside[:, 0:1]).then_inc(mask_ready, 1)
            by_length(dve, lambda part: cross_dve(dve, m, s, part, mask, True))

        @block.scalar
        def _(act):
            act.wait_ge(made, 3)
            act.wait_ge(bias_loaded, 32)
            by_length(act, lambda part: cross_act(act, m, s, part, True))

        @block.tensor
        def _(pe):
            pe.wait_ge(made, 3)
            by_length(pe, lambda part: cross_pe(pe, m, s, part, True))


EXPERTS, TOP_K, FF = 64, 8, 384
FT = FF // P
ROWS = B * S * TOP_K
MAX_TILES_OF = -(-B * S // P)
MATS, MAT = 3, KT * FF


class Routing:

    def __init__(self, sc):
        self.x2 = sc.sb("x2", [S, B, D])
        self.weights = sc.sb("weights", [S, B, TOP_K])
        self.places = sc.sb("places", [S, B * TOP_K], I32)
        self.table = sc.sb("table", [1, 3, EXPERTS], I32)


def route_phase(nc, sems, r, x1_d, attn_d, w_out_d, b_out_d, gate_d, rows_d):
    with ExitStack() as ctx:
        sc = Scope(nc, ctx, sems, "route")
        ident = sc.sb("ident", [P, P])
        eps = sc.sb("eps", [P, 1])
        before = sc.sb("before", [S, S], BF16)
        ones = sc.sb("ones", [S, P], BF16)
        w_raw = sc.sb("w_raw", [P, 2, D])
        w_hi = sc.sb("w_hi", [P, KT, D], F32R)
        w_lo = sc.sb("w_lo", [P, KT, D], F32R)
        b_out = sc.sb("b_out", [S, D])
        gate = sc.sb("gate", [P, KT, EXPERTS])
        at_raw = sc.sb("at_raw", [P, 2, KT, S])
        at_hi = sc.sb("at_hi", [P, 2, KT, S], F32R)
        at_lo = sc.sb("at_lo", [P, 2, KT, S], F32R)
        x1 = sc.sb("x1", [S, 2, D])
        xn = sc.sb("xn", [S, 2, D])
        xn_bf = sc.sb("xn_bf", [S, B, D], BF16)
        xnT = sc.sb("xnT", [P, KT, S])
        stats = sc.sb("stats", [S, 2, 2, 6])
        mean_var = sc.sb("mean_var", [S, 2, 2])
        std = sc.sb("std", [S, 2])
        zeros = sc.sb("zeros", [P, D], BF16)
        logits = sc.sb("logits", [S, B, EXPERTS])
        logit_max = sc.sb("logit_max", [S, B])
        top = sc.sb("top", [S, B, TOP_K])
        rest = sc.sb("rest", [S, B, EXPERTS])
        chosen = sc.sb("chosen", [S, B, EXPERTS])
        chosen_bf = sc.sb("chosen_bf", [S, B, EXPERTS], BF16)
        top_sum = sc.sb("top_sum", [S, B])
        prior = sc.sb("prior", [P, B + 1, EXPERTS])
        place = sc.sb("place", [S, B, EXPERTS])
        top_place = sc.sb("top_place", [S, B, TOP_K])
        match = sc.sb("match", [S, B, TOP_K, EXPERTS])
        row_end = sc.sb("row_end", [P, EXPERTS])
        row_start = sc.sb("row_start", [P, EXPERTS])
        tiles_of = sc.sb("tiles_of", [P, EXPERTS])
        tile_end = sc.sb("tile_end", [P, EXPERTS])
        tile_start = sc.sb("tile_start", [P, EXPERTS])
        unit = sc.sb("unit", [P, EXPERTS])
        expert_int = sc.sb("expert_int", [1, EXPERTS], I32)
        expert_no = sc.sb("expert_no", [1, EXPERTS])
        outp = sc.ps("outp", [P, 2, BANK])
        turn = sc.ps("turn", [P, 2, BANK])
        logit_ps = sc.ps("logit_ps", [P, BANK])
        rank_ps = sc.ps("rank_ps", [P, BANK])
        count_ps = sc.ps("count_ps", [P, BANK])

        cleared, made, const_made = sc.sem("cleared"), sc.sem("made"), sc.sem("const_made")
        w_loaded = [sc.sem(f"w_loaded{u}") for u in range(2)]
        w_hi_ready, w_split = sc.sem("w_hi_ready"), sc.sem("w_split")
        small_loaded = sc.sem("small_loaded")
        at_loaded = [sc.sem(f"at_loaded{u}") for u in range(2)]
        x1_loaded = [sc.sem(f"x1_loaded{u}") for u in range(2)]
        x1_biased = sc.sem("x1_biased")
        at_hi_ready, at_split = sc.sem("at_hi_ready"), sc.sem("at_split")
        outp_ready, x2_ready, x2_seen = sc.sem("outp_ready"), sc.sem("x2_ready"), sc.sem("x2_seen")
        stats_done, stats_seen, var_ready = sc.sem("stats_done"), sc.sem("stats_seen"), sc.sem("var_ready")
        std_ready, rstd_ready, xn_ready = sc.sem("std_ready"), sc.sem("rstd_ready"), sc.sem("xn_ready")
        xn_bf_ready = sc.sem("xn_bf_ready")
        turned, xnT_ready = sc.sem("turned"), sc.sem("xnT_ready")
        router_ready, logits_ready = sc.sem("router_ready"), sc.sem("logits_ready")
        step = sc.sem("step")
        centred, exp_ready = sc.sem("centred"), sc.sem("exp_ready")
        chosen_ready, ranked = sc.sem("chosen_ready"), sc.sem("ranked")
        places_ready = sc.sem("places_ready")
        pad_stored, sent = sc.sem("pad_stored"), sc.sem("sent")
        block = ctx.enter_context(nc.Block())

        @block.sync
        def _(sp):
            attn_rows = attn_d.rearrange("k p (b s) -> b p k s", b=B)
            sp.dma_start(b_out[:, :], b_out_d.partition_broadcast(S)).then_inc(small_loaded, 16)
            sp.dma_start(gate[:, :, :], gate_d).then_inc(small_loaded, 16)

            def load(b, u):
                wait(sp, at_split, b - 1)
                sp.dma_start(at_raw[:, u], attn_rows[b]).then_inc(at_loaded[u], 16)
                wait(sp, x2_ready, 2 * (b - 1))
                sp.dma_start(x1[:, u], x1_d[b]).then_inc(x1_loaded[u], 16)

            for u in range(2):
                load(u, u)
            for kt in range(KT):
                wait(sp, w_split, kt - 1)
                sp.dma_start(w_raw[:, kt % 2], w_out_d[kt]).then_inc(w_loaded[kt % 2], 16)
            with sp.Fori(1, B // 2) as g:
                for u in range(2):
                    load(2 * g + u, u)
            sp.wait_ge(const_made, 1)
            sp.dma_start(rows_d[ROWS:ROWS + P, :], zeros[:, :]).then_inc(pad_stored, 16)
            sp.wait_ge(pad_stored, 16)

        @block.gpsimd
        def _(pool):
            make_identity(pool, ident, cleared, made)
            pool.memset(eps[:, :], LN_EPS)
            pool.memset(unit[:, :], 1.0)
            pool.memset(ones[:, :], 1.0)
            pool.memset(prior[:, 0, :], 0.0)
            pool.iota(expert_int[:, :], [[1, EXPERTS]], base=0, channel_multiplier=0)
            pool.memset(before[:, :], 1.0).then_inc(cleared, 1)
            pool.wait_ge(cleared, 2)
            pool.affine_select(out=before[:, :], in_=before[:, :], compare_op=ALU.is_ge, fill=0.0,
                               base=-1, pattern=[[1, S]], channel_multiplier=-1).then_inc(made, 1)
            pool.memset(zeros[:, :], 0.0).then_inc(const_made, 1)
            pool.wait_ge(small_loaded, 32)

            def add_bias(b, u):
                pool.wait_ge(x1_loaded[u], 16 * (b // 2) + 16 if isinstance(b, int) else 8 * (b - u) + 16)
                pool.tensor_tensor(x1[:, u], x1[:, u], b_out[:, :], ALU.add).then_inc(x1_biased, 1)

            def narrow(b, u):
                pool.wait_ge(xn_ready, b + 1)
                pool.tensor_copy(xn_bf[:, b], xn[:, u]).then_inc(xn_bf_ready, 1)

            add_bias(0, 0)
            add_bias(1, 1)
            with pool.Fori(0, B // 2 - 1) as g:
                for u in range(2):
                    narrow(2 * g + u, u)
                    add_bias(2 * g + 2 + u, u)
            for u in range(2):
                narrow(B - 2 + u, u)
            pool.wait_ge(places_ready, 1)
            pool.wait_ge(xn_bf_ready, B)
            for b in range(B):
                for k in range(TOP_K):
                    c = b * TOP_K + k
                    pool.indirect_dma_start(
                        out=rows_d[0:ROWS, :], out_offset=bass.IndirectOffsetOnAxis(ap=r.places[:, c:c + 1], axis=0),
                        in_=xn_bf[:, b, :], in_offset=None).then_inc(sent, 16)
            pool.wait_ge(sent, 16 * B * TOP_K)

        @block.vector
        def _(dve):
            def split_at(b, u):
                dve.wait_ge(at_hi_ready, b + 1)
                dve.tensor_tensor(at_lo[:, u], at_raw[:, u], at_hi[:, u].bitcast(F32),
                                  ALU.subtract).then_inc(at_split, 1)

            def norm(b, u):
                dve.wait_ge(x1_biased, b + 1)
                for h in range(2):
                    cols = slice(h * BANK, (h + 1) * BANK)
                    dve.wait_ge(outp_ready, 2 * b + h + 1)
                    dve.tensor_tensor(r.x2[:, b, cols], outp[0:S, h, :], x1[:, u, cols],
                                      ALU.add).then_inc(x2_ready, 1)
                dve.wait_ge(x2_ready, 2 * b + 2)
                dve.sem_inc(x2_seen, 1)
                for h in range(2):
                    dve.bn_stats(stats[:, u, h, :],
                                 r.x2[:, b, h * BANK:(h + 1) * BANK]).then_inc(stats_done, 1)
                dve.wait_ge(stats_done, 2 * b + 2)
                dve.sem_inc(stats_seen, 1)
                dve.bn_aggr(mean_var[:, u, :], stats[:, u].rearrange("p c s -> p (c s)")).then_inc(var_ready, 1)
                dve.wait_ge(std_ready, b + 1)
                dve.reciprocal(std[:, u:u + 1], std[:, u:u + 1]).then_inc(rstd_ready, 1)
                dve.wait_ge(rstd_ready, b + 1)
                wait(dve, turned, b - 1)
                wait(dve, xn_bf_ready, b - 1)
                dve.tensor_scalar(xn[:, u, :], r.x2[:, b, :], mean_var[:, u, 0:1], std[:, u:u + 1],
                                  ALU.subtract, ALU.mult).then_inc(xn_ready, 1)

            split_at(0, 0)
            split_at(1, 1)
            for kt in range(KT):
                dve.wait_ge(w_hi_ready, kt + 1)
                dve.tensor_tensor(w_lo[:, kt], w_raw[:, kt % 2], w_hi[:, kt].bitcast(F32),
                                  ALU.subtract).then_inc(w_split, 1)
            for u in range(2):
                norm(u, u)
                split_at(2 + u, u)
            with dve.Fori(1, B // 2 - 1) as g:
                for u in range(2):
                    norm(2 * g + u, u)
                    split_at(2 * g + 2 + u, u)
            for u in range(2):
                norm(B - 2 + u, u)

            steps = [0]

            def link(ins):
                steps[0] += 1
                ins.then_inc(step, 1)
                dve.wait_ge(step, steps[0])

            dve.wait_ge(logits_ready, B)
            link(dve.tensor_reduce(logit_max[:, :], logits[:, :, :], AX.X, ALU.max))
            dve.tensor_tensor(logits[:, :, :], logits[:, :, :],
                              logit_max[:, :].unsqueeze(2).broadcast_to([S, B, EXPERTS]),
                              ALU.subtract).then_inc(centred, 1)
            dve.wait_ge(exp_ready, 1)
            for b in range(B):
                last = dve.max(top[:, b, :], logits[:, b, :])
            link(last)
            for b in range(B):
                last = dve.match_replace(rest[:, b, :], top[:, b, :], logits[:, b, :], -1.0)
            link(last)
            link(dve.tensor_scalar(chosen[:, :, :], rest[:, :, :], 0.0, None, ALU.is_lt))
            dve.tensor_copy(chosen_bf[:, :, :], chosen[:, :, :]).then_inc(chosen_ready, 1)
            link(dve.tensor_reduce(top_sum[:, :], top[:, :, :], AX.X, ALU.add))
            link(dve.reciprocal(top_sum[:, :], top_sum[:, :]))
            link(dve.tensor_tensor(logits[:, :, :], logits[:, :, :],
                                   top_sum[:, :].unsqueeze(2).broadcast_to([S, B, EXPERTS]), ALU.mult))
            dve.wait_ge(ranked, 1)
            for b in range(B):
                link(dve.tensor_tensor(prior[:, b + 1, :], prior[:, b, :],
                                       count_ps[:, b * EXPERTS:(b + 1) * EXPERTS], ALU.add))
            total = prior[:, B, :]
            link(dve.tensor_tensor_scan(row_end[:, :], unit[:, :], total, 0.0, ALU.mult, ALU.add))
            link(dve.tensor_tensor(row_start[:, :], row_end[:, :], total, ALU.subtract))
            link(dve.tensor_tensor(place[:, :, :], prior[0:S, 0:B, :],
                                   rank_ps[0:S, :].rearrange("s (b e) -> s b e", b=B), ALU.add))
            link(dve.scalar_tensor_tensor(out=place[:, :, :], in0=place[:, :, :], scalar=1.0,
                                          in1=row_start[0:S, :].unsqueeze(1).broadcast_to([S, B, EXPERTS]),
                                          op0=ALU.add, op1=ALU.add))
            link(dve.tensor_tensor(place[:, :, :], place[:, :, :], chosen[:, :, :], ALU.mult))
            for b in range(B):
                last = dve.max(top_place[:, b, :], place[:, b, :])
            link(last)
            dve.tensor_scalar(r.places[:, :], top_place[:, :, :].rearrange("s b k -> s (b k)"), -1.0, None,
                              ALU.add).then_inc(places_ready, 1)
            link(dve.tensor_scalar(tiles_of[:, :], total, float(P), 1.0, ALU.is_gt, ALU.add))
            for n in range(2, MAX_TILES_OF):
                link(dve.scalar_tensor_tensor(out=tiles_of[:, :], in0=total, scalar=float(n * P),
                                              in1=tiles_of[:, :], op0=ALU.is_gt, op1=ALU.add))
            link(dve.tensor_tensor_scan(tile_end[:, :], unit[:, :], tiles_of[:, :], 0.0, ALU.mult, ALU.add))
            link(dve.tensor_tensor(tile_start[:, :], tile_end[:, :], tiles_of[:, :], ALU.subtract))
            link(dve.tensor_copy(expert_no[:, :], expert_int[:, :]))
            link(dve.tensor_tensor(tile_start[0:1, :], tile_start[0:1, :], expert_no[:, :], ALU.subtract))
            for n, row in enumerate((row_start, tiles_of, tile_start)):
                link(dve.tensor_copy(r.table[:, n, :], row[0:1, :]))
            shape = [S, B, TOP_K, EXPERTS]
            link(dve.tensor_tensor(match[:, :, :, :], place[:, :, :].unsqueeze(2).broadcast_to(shape),
                                   top_place[:, :, :].unsqueeze(3).broadcast_to(shape), ALU.is_equal))
            link(dve.tensor_tensor(match[:, :, :, :], match[:, :, :, :],
                                   logits[:, :, :].unsqueeze(2).broadcast_to(shape), ALU.mult))
            link(dve.tensor_reduce(r.weights[:, :, :], match[:, :, :, :], AX.X, ALU.add))

        @block.scalar
        def _(act):
            act.wait_ge(made, 2)

            def split_at(b, u):
                act.wait_ge(at_loaded[u], 16 * (b // 2) + 16 if isinstance(b, int) else 8 * (b - u) + 16)
                wait(act, outp_ready, 2 * (b - 1))
                act.copy(at_hi[:, u], at_raw[:, u]).then_inc(at_hi_ready, 1)

            def root(b, u):
                act.wait_ge(var_ready, b + 1)
                act.activation(std[:, u:u + 1], mean_var[:, u, 1:2], ACT.Sqrt,
                               bias=eps[0:S, :]).then_inc(std_ready, 1)

            def collect(b):
                act.wait_ge(turned, b + 1)
                act.copy(xnT[:, :, :].rearrange("p (c k) s -> p c (k s)", c=2),
                         turn[:, :, 0:SH]).then_inc(xnT_ready, 1)
                act.wait_ge(router_ready, b + 1)
                act.copy(logits[:, b, :], logit_ps[0:S, 0:EXPERTS]).then_inc(logits_ready, 1)

            split_at(0, 0)
            split_at(1, 1)
            for kt in range(KT):
                act.wait_ge(w_loaded[kt % 2], 16 * (kt // 2) + 16)
                act.copy(w_hi[:, kt], w_raw[:, kt % 2]).then_inc(w_hi_ready, 1)
            with act.Fori(0, B // 2 - 1) as g:
                for u in range(2):
                    root(2 * g + u, u)
                    split_at(2 * g + 2 + u, u)
                    collect(2 * g + u)
            for u in range(2):
                root(B - 2 + u, u)
                collect(B - 2 + u)
            act.wait_ge(centred, 1)
            act.activation(logits[:, :, :], logits[:, :, :], ACT.Exp).then_inc(exp_ready, 1)

        @block.tensor
        def _(pe):
            def project(b, u):
                pe.wait_ge(at_split, b + 1)
                for h in range(2):
                    cols = slice(h * BANK, (h + 1) * BANK)
                    wait(pe, x2_ready, 2 * (b - 1) + h + 1)
                    for kt in range(KT):
                        mm = split_matmul(pe, outp[0:S, h, :], at_hi[:, u, kt, :], at_lo[:, u, kt, :],
                                          w_hi[:, kt, cols], w_lo[:, kt, cols], kt == 0, kt == KT - 1)
                    mm.then_inc(outp_ready, 1)

            def router(b, u):
                pe.wait_ge(xn_ready, b + 1)
                wait(pe, xnT_ready, b)
                for kt in range(KT):
                    mm = pe.transpose(turn[:, kt // 4, (kt % 4) * S:(kt % 4 + 1) * S],
                                      xn[:, u, kt * P:(kt + 1) * P], ident[0:S, 0:S])
                mm.then_inc(turned, 1)
                pe.wait_ge(xnT_ready, b + 1)
                wait(pe, logits_ready, b)
                for kt in range(KT):
                    mm = pe.matmul(logit_ps[0:S, 0:EXPERTS], xnT[:, kt, :], gate[:, kt, :],
                                   start=kt == 0, stop=kt == KT - 1)
                mm.then_inc(router_ready, 1)

            pe.wait_ge(made, 2)
            pe.wait_ge(small_loaded, 32)
            pe.wait_ge(w_split, KT)
            project(0, 0)
            project(1, 1)
            router(0, 0)
            project(2, 0)
            router(1, 1)
            with pe.Fori(1, B // 2 - 1) as g:
                project(2 * g + 1, 1)
                router(2 * g, 0)
                project(2 * g + 2, 0)
                router(2 * g + 1, 1)
            project(B - 1, 1)
            router(B - 2, 0)
            router(B - 1, 1)
            pe.wait_ge(chosen_ready, 1)
            picks = chosen_bf[:, :, :].rearrange("s b e -> s (b e)")
            pe.matmul(rank_ps[0:S, :], before[:, :], picks, start=True, stop=True)
            pe.matmul(count_ps[:, :], ones[:, :], picks, start=True, stop=True).then_inc(ranked, 1)


class Precast:

    def __init__(self, nc, src_d, dst_d):
        self.src_d, self.dst_d = src_d, dst_d
        self.done = [nc.alloc_semaphore(name=f"precast_done{u}") for u in range(2)]
        self.step = nc.alloc_semaphore(name="precast_step")

    def start(self, pool, pair, u):
        wait(pool, self.done[u], 16 * pair)
        pool.sem_inc(self.step, 1)
        n = 2 * pair + u
        pool.dma_start(self.dst_d[n], self.src_d[n]).then_inc(self.done[u], 16)

    def start_some(self, pool, first, count):
        for u in range(2):
            self.start(pool, first // 2, u)
        with pool.Fori(first // 2 + 1, (first + count) // 2) as pair:
            for u in range(2):
                self.start(pool, pair, u)


W_SLOTS = 4


def over_experts(eng, lag, step):
    for c in range(W_SLOTS):
        step(0, c)
    with eng.Fori(1, EXPERTS // W_SLOTS - 1) as g:
        for c in range(W_SLOTS):
            step(g, c)
    for c in range(W_SLOTS + lag):
        step(EXPERTS // W_SLOTS - 1, c)


def has_expert(e):
    return not isinstance(e, int) or 0 <= e < EXPERTS


def experts_phase(nc, sems, r, cast, rows_d, out_d):
    LAG = 2
    with ExitStack() as ctx:
        sc = Scope(nc, ctx, sems, "moe")
        ident = sc.sb("ident", [P, P], BF16)
        w = sc.sb("w", [P, W_SLOTS, MATS, MAT], BF16)
        rows = sc.sb("rows", [P, W_SLOTS, D], BF16)
        rowsT = sc.sb("rowsT", [P, 2, KT, P], BF16)
        silu = sc.sb("silu", [P, 2, FT * P])
        inner = sc.sb("inner", [P, 2, FT, P], BF16)
        out = sc.sb("out", [P, W_SLOTS, D], BF16)
        x_rows = sc.sb("x_rows", [P, D], BF16)
        x_rowsT = sc.sb("x_rowsT", [P, KT, P], BF16)
        x_silu = sc.sb("x_silu", [P, FT * P])
        x_inner = sc.sb("x_inner", [P, FT, P], BF16)
        x_out = sc.sb("x_out", [P, D], BF16)
        turn = sc.ps("turn", [P, KT, P], BF16)
        x_turn = sc.ps("x_turn", [P, KT, P], BF16)
        gate_ps = sc.ps("gate_ps", [P, 2, BANK])
        up_ps = sc.ps("up_ps", [P, 2, BANK])
        out_ps = sc.ps("out_ps", [P, 2, BANK])

        cleared, made = sc.sem("cleared"), sc.sem("made")
        w_loaded = [sc.sem(f"w_loaded{u}") for u in range(W_SLOTS)]
        rows_loaded = [sc.sem(f"rows_loaded{u}") for u in range(W_SLOTS)]
        turned, rowsT_ready = sc.sem("turned"), sc.sem("rowsT_ready")
        gate_ready, up_ready = sc.sem("gate_ready"), sc.sem("up_ready")
        silu_ready, inner_ready = sc.sem("silu_ready"), sc.sem("inner_ready")
        out_ready = sc.sem("out_ready")
        left_copied, right_copied = sc.sem("left_copied"), sc.sem("right_copied")
        stored, all_stored = sc.sem("stored"), sc.sem("all_stored")
        x_loaded, x_turned, x_rowsT_ready = sc.sem("x_loaded"), sc.sem("x_turned"), sc.sem("x_rowsT_ready")
        x_gate_ready, x_up_ready = sc.sem("x_gate_ready"), sc.sem("x_up_ready")
        x_silu_ready, x_inner_ready = sc.sem("x_silu_ready"), sc.sem("x_inner_ready")
        x_out_ready, x_copied = sc.sem("x_out_ready"), sc.sem("x_copied")
        x_stored, x_done = sc.sem("x_stored"), sc.sem("x_done")
        block = ctx.enter_context(nc.Block())

        def first_row(eng, e):
            return eng.value_load(r.table[0:1, 0, bass.ts(e, 1)], min_val=0, max_val=ROWS)

        def further(eng, e, tile):
            if not has_expert(e):
                return
            tiles = eng.value_load(r.table[0:1, 1, bass.ts(e, 1)], min_val=1, max_val=MAX_TILES_OF)
            with eng.If(tiles > 1):
                before = eng.value_load(r.table[0:1, 2, bass.ts(e, 1)], min_val=0, max_val=ROWS // P)
                with eng.Fori(0, MAX_TILES_OF - 1) as n:
                    with eng.If(n + 1 < tiles):
                        tile(n + 1, n + before)

        def mat(slot, n, columns):
            return w[:, slot, n, :].rearrange("p (k f) -> p k f", f=columns)

        @block.sync
        def _(sp):
            def load(g, c):
                e, slot = W_SLOTS * g + c, c % W_SLOTS
                if has_expert(e):
                    first = first_row(sp, e)
                    wait(sp, out_ready, e - W_SLOTS + 1)
                    sp.dma_start(rows[:, slot], rows_d[bass.ds(first, P), :]).then_inc(rows_loaded[slot], 16)
                    sp.dma_start(w[:, slot], cast.dst_d[bass.ds(e * MATS, MATS)].rearrange(
                        "m p n -> p m n")).then_inc(w_loaded[slot], 16)

            def step(g, c):
                e = W_SLOTS * g + c

                def load_further(j, x):
                    first = first_row(sp, e)
                    sp.wait_ge(x_turned, x + 1)
                    sp.dma_start(x_rows[:, :], rows_d[bass.ds(first + j * P, P), :]).then_inc(x_loaded, 16)

                further(sp, e, load_further)
                load(g, c + W_SLOTS - 1)

            for u in range(2):
                sp.wait_ge(cast.done[u], 16 * EXPERTS * MATS // 2)
            for c in range(W_SLOTS - 1):
                load(0, c)
            over_experts(sp, 0, step)

        @block.gpsimd
        def _(pool):
            make_identity(pool, ident, cleared, made)

        @block.vector
        def _(dve):
            def turn_rows(e, c):
                if has_expert(e):
                    dve.wait_ge(turned, e + 1)
                    wait(dve, up_ready, e - 1)
                    dve.tensor_copy(rowsT[:, c % 2], turn[:, :, :]).then_inc(rowsT_ready, 1)

            def step(g, c):
                e = W_SLOTS * g + c
                turn_rows(e + 1, c + 1)
                if has_expert(e):
                    dve.wait_ge(silu_ready, e + 1)
                    dve.wait_ge(up_ready, e + 1)
                    wait(dve, out_ready, e - 1)
                    dve.tensor_tensor(inner[:, c % 2].rearrange("p f s -> p (f s)"), silu[:, c % 2],
                                      up_ps[:, c % 2, 0:FT * P], ALU.mult).then_inc(inner_ready, 1)
                if has_expert(e - 1):
                    dve.wait_ge(out_ready, e)
                    wait(dve, stored, 16 * (e - W_SLOTS))
                    dve.tensor_copy(out[:, (c - 1) % W_SLOTS, BANK:D], out_ps[:, 1, :]).then_inc(right_copied, 1)

                def tile(j, x):
                    dve.wait_ge(x_turned, x + 2)
                    dve.tensor_copy(x_rowsT[:, :, :], x_turn[:, :, :]).then_inc(x_rowsT_ready, 1)
                    dve.wait_ge(x_silu_ready, x + 1)
                    dve.wait_ge(x_up_ready, x + 1)
                    dve.tensor_tensor(x_inner[:, :, :].rearrange("p f s -> p (f s)"), x_silu[:, :],
                                      up_ps[:, c % 2, 0:FT * P], ALU.mult).then_inc(x_inner_ready, 1)
                    dve.wait_ge(x_out_ready, x + 1)
                    dve.wait_ge(x_stored, 16 * x + 16)
                    dve.tensor_copy(x_out[:, BANK:D], out_ps[:, 1, :]).then_inc(x_copied, 1)

                further(dve, e, tile)

            turn_rows(0, 0)
            over_experts(dve, LAG, step)

        @block.scalar
        def _(act):
            act.sem_inc(x_stored, 16)

            def step(g, c):
                e = W_SLOTS * g + c
                if has_expert(e):
                    act.wait_ge(gate_ready, e + 1)
                    wait(act, inner_ready, e - 1)
                    act.activation(silu[:, c % 2], gate_ps[:, c % 2, 0:FT * P], ACT.Silu).then_inc(silu_ready, 1)
                if has_expert(e - 1):
                    act.wait_ge(out_ready, e)
                    wait(act, stored, 16 * (e - W_SLOTS))
                    act.copy(out[:, (c - 1) % W_SLOTS, 0:BANK], out_ps[:, 0, :]).then_inc(left_copied, 1)
                if has_expert(e - 2):
                    first = first_row(act, e - 2)
                    act.wait_ge(left_copied, e - 1)
                    act.wait_ge(right_copied, e - 1)
                    wait(act, stored, 16 * (e - 2))
                    act.dma_start(out_d[bass.ds(first, P), :], out[:, (c - 2) % W_SLOTS]).then_inc(stored, 16)

                def tile(j, x):
                    first = first_row(act, e)
                    act.wait_ge(x_gate_ready, x + 1)
                    act.activation(x_silu[:, :], gate_ps[:, c % 2, 0:FT * P], ACT.Silu).then_inc(x_silu_ready, 1)
                    act.wait_ge(x_out_ready, x + 1)
                    act.copy(x_out[:, 0:BANK], out_ps[:, 0, :]).then_inc(x_copied, 1)
                    act.wait_ge(x_copied, 2 * x + 2)
                    act.dma_start(out_d[bass.ds(first + j * P, P), :],
                                  x_out[:, :]).then_inc(x_stored, 16)
                    act.wait_ge(x_stored, 16 * x + 32)
                    act.sem_inc(all_stored, 1)

                further(act, e, tile)

            over_experts(act, LAG, step)
            act.wait_ge(stored, 16 * EXPERTS)

        @block.tensor
        def _(pe):
            pe.sem_inc(x_turned, 1)
            pe.wait_ge(made, 1)

            def turn_rows(g, c):
                e = W_SLOTS * g + c
                if has_expert(e):
                    pe.wait_ge(rows_loaded[c % W_SLOTS], 16 * (g + c // W_SLOTS + 1))
                    wait(pe, rowsT_ready, e)
                    for k in range(KT):
                        mm = pe.transpose(turn[:, k, :], rows[:, c % W_SLOTS, k::KT], ident[:, :])
                    mm.then_inc(turned, 1)

            def products(slot, u, x, ready):
                for n, ps in enumerate((gate_ps, up_ps)):
                    for f in range(FT):
                        for k in range(KT):
                            mm = pe.matmul(ps[:, u, f * P:(f + 1) * P], mat(slot, n, FF)[:, k, f::FT], x[:, k, :],
                                           start=k == 0, stop=k == KT - 1)
                    mm.then_inc(ready[n], 1)

            def narrow(slot, x, ready):
                for h in range(2):
                    for f in range(FT):
                        mm = pe.matmul(out_ps[:, h, :], x[:, f, :], mat(slot, 2, D)[:, f, h * BANK:(h + 1) * BANK],
                                       start=f == 0, stop=f == FT - 1)
                mm.then_inc(ready, 1)

            def step(g, c):
                e = W_SLOTS * g + c
                turn_rows(g, c + 1)
                if has_expert(e):
                    pe.wait_ge(w_loaded[c % W_SLOTS], 16 * (g + c // W_SLOTS + 1))
                    pe.wait_ge(rowsT_ready, e + 1)
                    wait(pe, silu_ready, e - 1)
                    wait(pe, inner_ready, e - 1)
                    products(c % W_SLOTS, c % 2, rowsT[:, c % 2], (gate_ready, up_ready))
                if has_expert(e - 1):
                    pe.wait_ge(inner_ready, e)
                    wait(pe, left_copied, e - 1)
                    wait(pe, right_copied, e - 1)
                    narrow((c - 1) % W_SLOTS, inner[:, (c - 1) % 2], out_ready)

                def tile(j, x):
                    pe.wait_ge(x_loaded, 16 * x + 16)
                    for k in range(KT):
                        mm = pe.transpose(x_turn[:, k, :], x_rows[:, k::KT], ident[:, :])
                    mm.then_inc(x_turned, 1)
                    pe.wait_ge(x_rowsT_ready, x + 1)
                    pe.wait_ge(inner_ready, e + 1)
                    products(c % W_SLOTS, c % 2, x_rowsT, (x_gate_ready, x_up_ready))
                    pe.wait_ge(x_inner_ready, x + 1)
                    wait(pe, left_copied, e)
                    wait(pe, right_copied, e)
                    narrow(c % W_SLOTS, x_inner, x_out_ready)
                    pe.wait_ge(x_copied, 2 * x + 2)
                    pe.sem_inc(x_done, 1)

                further(pe, e, tile)

            turn_rows(0, 0)
            over_experts(pe, LAG, step)


def combine_phase(nc, sems, r, rows_d, out_d):
    GATHERS = 4
    with ExitStack() as ctx:
        sc = Scope(nc, ctx, sems, "comb")
        part = sc.sb("part", [S, GATHERS, D], BF16)
        gathered = [sc.sem(f"gathered{n}") for n in range(GATHERS)]
        added, stored = sc.sem("added"), sc.sem("stored")
        block = ctx.enter_context(nc.Block())

        @block.gpsimd
        def _(pool):
            for c in range(B * TOP_K):
                wait(pool, added, c - GATHERS + 1)
                pool.indirect_dma_start(
                    out=part[:, c % GATHERS, :], out_offset=None, in_=rows_d[0:ROWS, :],
                    in_offset=bass.IndirectOffsetOnAxis(ap=r.places[:, c:c + 1], axis=0)
                ).then_inc(gathered[c % GATHERS], 16)

        @block.vector
        def _(dve):
            for c in range(B * TOP_K):
                b, k = c // TOP_K, c % TOP_K
                dve.wait_ge(gathered[c % GATHERS], 16 * (c // GATHERS) + 16)
                wait(dve, added, c)
                dve.scalar_tensor_tensor(out=r.x2[:, b, :], in0=part[:, c % GATHERS, :],
                                         scalar=r.weights[:, b, k:k + 1], in1=r.x2[:, b, :],
                                         op0=ALU.mult, op1=ALU.add).then_inc(added, 1)

        @block.sync
        def _(sp):
            for b in range(B):
                sp.wait_ge(added, TOP_K * (b + 1))
                sp.dma_start(out_d[b], r.x2[:, b, :]).then_inc(stored, 16)
            sp.wait_ge(stored, 16 * B)


def decoder_kernel(nc, a, out):
    def scratch(name, shape, dt=F32):
        return nc.dram_tensor(name, shape, dt).ap()

    qkv_d = [scratch(f"self_{n}_dram", (P, B, KT, S)) for n in ("q", "k", "v")]
    q_d = [scratch(f"cross_q_{n}_dram", (KT, P, B * S)) for n in ("img", "txt")]
    x1_d = scratch("x1_dram", (B, S, D))
    img_d = scratch("attn_img_dram", (KT, P, B * S))
    attn_d = scratch("attn_dram", (KT, P, B * S))
    k_d = scratch("cross_k_dram", (KT, B, P, BANK))
    rows_d = scratch("expert_rows_dram", (ROWS + MAX_TILES_OF * P, D), BF16)
    results_d = scratch("expert_results_dram", (ROWS + MAX_TILES_OF * P, D), BF16)
    cast_d = scratch("experts_bf16_dram", (EXPERTS * MATS, P, MAT), BF16)
    sems = []
    cast = Precast(nc, a["moe"], cast_d)
    with ExitStack() as memory:
        ln_project_phase(nc, sems, cast, CASTS_QKV, "qkv", a["x"], a["w_qkv"], qkv_d, [HD ** -0.5, 1.0, 1.0])
        self_attention_phase(nc, sems, cast, a["x"], qkv_d, a["w_self_out"], x1_d)
        ln_project_phase(nc, sems, cast, CASTS_Q, "q", x1_d, a["wq"], q_d, [1.0], bias_d=a["bq"],
                         rms=(a["gq"], [a["gk_img"], a["gk"]]))
        cross_image_phase(nc, sems, cast, a["ctx_img"], a["w_img"], (a["bk_img"], a["bv_img"]), k_d, q_d[0], img_d)
        clear_semaphores(nc, sems)
        cross_text_phase(nc, sems, cast, a["ctx_txt"], a["w_txt"], (a["bk"], a["bv"]), a["lens"], k_d, q_d[1],
                         img_d, attn_d)
        clear_semaphores(nc, sems)
        r = Routing(Scope(nc, memory, sems, "routing"))
        route_phase(nc, sems, r, x1_d, attn_d, a["wo"], a["bo"], a["gate"], rows_d)
        experts_phase(nc, sems, r, cast, rows_d, results_d)
        combine_phase(nc, sems, r, results_d, out)



def _layouts(i):
    def columns(w):
        n = w.shape[1] // P
        return w.reshape(KT, P, n, P).transpose(2, 1, 0, 3)

    def rows(w):
        return w.reshape(KT, P, w.shape[1])

    def vector(v):
        return v.reshape(KT, P).T

    def context(c):
        c = c.transpose(0, 2, 1).reshape(B, KT, P, c.shape[1]).transpose(0, 2, 1, 3)
        return np.pad(c, ((0, 0), (0, 0), (0, 0), (0, 1)))

    ctx = i["ctx_2048"]
    return {
        "x": i["x"], "ctx_img": context(ctx[:, :IMG]), "ctx_txt": context(ctx[:, IMG:]),
        "w_qkv": columns(i["L0_attn_w_qkv"]), "w_self_out": rows(i["L0_attn_w_out"]),
        "lens": np.broadcast_to(i["L0_xattn_context_lens"].reshape(1, 1), (S, 1)),
        "wq": columns(i["L0_xattn_Wq"]), "bq": vector(i["L0_xattn_bq"]), "gq": vector(i["L0_xattn_gq"]),
        "w_txt": np.concatenate([columns(i["L0_xattn_Wk"]), columns(i["L0_xattn_Wv"])]),
        "bk": vector(i["L0_xattn_bk"]), "gk": vector(i["L0_xattn_gk"]),
        "bv": vector(i["L0_xattn_bv"]),
        "w_img": np.concatenate([columns(i["L0_xattn_Wk_img"]), columns(i["L0_xattn_Wv_img"])]),
        "bk_img": vector(i["L0_xattn_bk_img"]),
        "gk_img": vector(i["L0_xattn_gk_img"]),
        "bv_img": vector(i["L0_xattn_bv_img"]),
        "wo": rows(i["L0_xattn_Wo"]), "bo": i["L0_xattn_bo"],
        "gate": i["L0_ffn_gate_w"].reshape(KT, P, EXPERTS).transpose(1, 0, 2),
        "moe": np.stack([i[f"L0_ffn_{n}_proj"].reshape(EXPERTS, P, MAT) for n in ("gate", "up", "down")],
                        axis=1).reshape(EXPERTS * MATS, P, MAT),
    }


def kernel(**inputs):
    import concourse.bacc as bacc
    from concourse.bass_utils import run_bass_kernel_spmd

    nc = bacc.Bacc("TRN2", target_bir_lowering=False, num_devices=1)
    laid_out = _layouts({name: np.asarray(value) for name, value in inputs.items()})
    arrays, args = {}, {}
    for name, value in laid_out.items():
        value = np.ascontiguousarray(value)
        arrays[f"in_{name}_dram"] = value
        args[name] = nc.dram_tensor(f"in_{name}_dram", value.shape, mybir.dt.from_np(value.dtype),
                                    kind="ExternalInput").ap()
    out = nc.dram_tensor("out_dram", (B, S, D), F32, kind="ExternalOutput").ap()
    decoder_kernel(nc, args, out)
    result = run_bass_kernel_spmd(nc, [arrays], core_ids=[0])
    return result.results[0]["out_dram"]
```

```python
from contextlib import ExitStack

import concourse.bass as bass
import concourse.mybir as mybir
import numpy as np

F32 = mybir.dt.float32
F32R = mybir.dt.float32r
BF16 = mybir.dt.bfloat16
I32 = mybir.dt.int32
ALU = mybir.AluOpType
ACT = mybir.ActivationFunctionType
AX = mybir.AxisListType

P = 128
B, S, D = 8, 100, 1024
HEADS, HD = 16, 64
KT = D // P
BANK = 512
IMG, TXT = 257, 465
LN_EPS, RMS_EPS = 1e-5, 1e-6
HALF = B // 2
SH = HALF * S
CASTS_SELF, CASTS_Q = (0, 72), (72, 26)
CASTS_IMG, CASTS_TXT = ((98, 18), (116, 32)), ((148, 12), (160, 32))


def wait(eng, sem, value):
    if not isinstance(value, int) or value > 0:
        eng.wait_ge(sem, value)


class Scope:

    def __init__(self, nc, ctx, sems, name):
        self.nc, self.ctx, self.sems, self.name = nc, ctx, sems, name

    def sb(self, name, shape, dt=F32):
        return self.ctx.enter_context(self.nc.sbuf_tensor(f"{self.name}_{name}", shape, dt))

    def ps(self, name, shape, dt=F32):
        return self.ctx.enter_context(self.nc.psum_tensor(f"{self.name}_{name}", shape, dt))

    def sem(self, name):
        self.sems.append(self.nc.alloc_semaphore(name=f"{self.name}_{name}"))
        return self.sems[-1]


def clear_semaphores(nc, sems):
    nc.clear_and_free_semaphores(sems)
    nc.all_engine_barrier()
    sems.clear()


def make_identity(eng, ident, cleared, made):
    eng.memset(ident[:, :], 0.0).then_inc(cleared, 1)
    eng.wait_ge(cleared, 1)
    n = ident.shape[1]
    eng.affine_select(out=ident[:, :], in_=ident[:, :], compare_op=ALU.not_equal, fill=1.0, base=0,
                      pattern=[[-1, n]], channel_multiplier=1).then_inc(made, 1)


def split_matmul(eng, out, w_hi, w_lo, a_hi, a_lo, first, last):
    eng.matmul(out, w_hi, a_hi, start=first, stop=False)
    eng.matmul(out, w_hi, a_lo, start=False, stop=False)
    return eng.matmul(out, w_lo, a_hi, start=False, stop=last)


def self_attention_phase(nc, sems, cast, x_d, w_d, x1_d, clear_d):
    QKV, QKV_TILES = 3, 3 * KT
    STEPS = 2 * KT
    WO_TILES = KT // 2
    CLEARS = 19
    X_SLOTS, R_SLOTS = 4, 4
    with ExitStack() as ctx:
        sc = Scope(nc, ctx, sems, "self")
        ident = sc.sb("ident", [P, P])
        causal = sc.sb("causal", [S, S])
        eps = sc.sb("eps", [P, 1])
        zeros = sc.sb("zeros", [P, D], BF16)
        stats = sc.sb("stats", [S, X_SLOTS, 2, 6])
        mean_var = sc.sb("mean_var", [S, X_SLOTS, 2])
        rstd = sc.sb("rstd", [S, X_SLOTS])
        shift = sc.sb("shift", [S, X_SLOTS])
        xnT_hi = sc.sb("xnT_hi", [P, KT * B * S], F32R)
        xnT_lo = sc.sb("xnT_lo", [P, KT * B * S], F32R)
        at_hi = sc.sb("at_hi", [P, KT, B * S], F32R)
        at_lo = sc.sb("at_lo", [P, KT, B * S], F32R)
        w_raw = sc.sb("w_raw", [P, QKV, D])
        w_hi = sc.sb("w_hi", [P, QKV, KT, P], F32R)
        w_lo = sc.sb("w_lo", [P, QKV, KT, P], F32R)
        wo_hi = sc.sb("wo_hi", [P, KT, BANK], F32R)
        wo_lo = sc.sb("wo_lo", [P, KT, BANK], F32R)
        xn = sc.sb("xn", [S, 2, D])
        sizes = (QKV * 2 * SH, HALF * P, 2 * HALF * S, 2 * HALF * S)
        work = sc.sb("work", [P, sum(sizes)])
        starts = [sum(sizes[:n]) for n in range(len(sizes))]
        qkvT, v_rows, probs, probsT = (work[:, a:a + n] for a, n in zip(starts, sizes))
        qkvT = qkvT.rearrange("p (n h s) -> p n h s", n=QKV, h=2)
        v_rows = v_rows[0:S].rearrange("s (b n) -> s b n", b=HALF)
        probs = probs[0:S].rearrange("s (e b k) -> s e b k", e=2, b=HALF)
        probsT = probsT[0:S].rearrange("s (e b k) -> s e b k", e=2, b=HALF)
        x_row = work[0:S, 0:X_SLOTS * D].rearrange("s (u d) -> s u d", u=X_SLOTS)
        residual = xn[:, :, :].rearrange("s u (h n) -> s (u h) n", h=2)
        row_max = sc.sb("row_max", [S, 2, HALF])
        row_sum = sc.sb("row_sum", [S, 2, HALF])
        acc = sc.ps("acc", [P, 2, BANK])
        scores = sc.ps("scores", [P, 2, BANK])
        p_turn = sc.ps("p_turn", [P, 2, BANK])
        v_turn = sc.ps("v_turn", [P, BANK])
        mixed = sc.ps("mixed", [P, BANK])

        xT_hi = xnT_hi[:, :].rearrange("p (k n) -> p k n", k=KT)
        xT_lo = xnT_lo[:, :].rearrange("p (k n) -> p k n", k=KT)
        wo = ((wo_hi, wo_lo), tuple(t[:, 0:KT * BANK].rearrange("p (k n) -> p k n", k=KT)
                                    for t in (xnT_hi, xnT_lo)))

        cleared, made, blanked = sc.sem("cleared"), sc.sem("made"), sc.sem("blanked")
        x_loaded = [sc.sem(f"x_loaded{u}") for u in range(X_SLOTS)]
        w_loaded = [sc.sem(f"w_loaded{u}") for u in range(QKV)]
        stats_done, stats_seen, var_ready = sc.sem("stats_done"), sc.sem("stats_seen"), sc.sem("var_ready")
        std_ready, rstd_ready, shift_ready = sc.sem("std_ready"), sc.sem("rstd_ready"), sc.sem("shift_ready")
        xn_ready, x_turned = sc.sem("xn_ready"), sc.sem("x_turned")
        x_hi_ready, x_split = sc.sem("x_hi_ready"), sc.sem("x_split")
        w_hi_ready, w_split = sc.sem("w_hi_ready"), sc.sem("w_split")
        acc_ready, acc_used = sc.sem("acc_ready"), sc.sem("acc_used")
        scores_ready, masked, max_ready = sc.sem("scores_ready"), sc.sem("masked"), sc.sem("max_ready")
        centred, exp_ready = sc.sem("centred"), sc.sem("exp_ready")
        summed, inverted, probs_ready = sc.sem("summed"), sc.sem("inverted"), sc.sem("probs_ready")
        v_turned, v_used = sc.sem("v_turned"), sc.sem("v_used")
        p_turned, p_used = sc.sem("p_turned"), sc.sem("p_used")
        mixed_ready, at_hi_ready, at_split = sc.sem("mixed_ready"), sc.sem("at_hi_ready"), sc.sem("at_split")
        act_step = sc.sem("act_step")
        r_loaded = [sc.sem(f"r_loaded{u}") for u in range(R_SLOTS)]
        x1_ready = sc.sem("x1_ready")
        x1_stored = [sc.sem(f"x1_stored{u}") for u in range(R_SLOTS)]
        block = ctx.enter_context(nc.Block())

        def turned_rows(u):
            return (scores, p_turn)[u % 2]

        def over_pairs(eng, step):
            step(0, 0)
            step(0, 1)
            with eng.Fori(1, KT - 1) as nt:
                step(nt, 0)
                step(nt, 1)
            step(KT - 1, 0)
            step(KT - 1, 1)

        def part(o):
            half = 1 - o // B
            return o % B, slice(half * BANK, (half + 1) * BANK)

        @block.sync
        def _(sp):
            def load_w(i, slot):
                wait(sp, w_split, i - QKV + 1)
                sp.dma_start(w_raw[:, slot], w_d[i]).then_inc(w_loaded[slot], 16)

            for u in range(X_SLOTS):
                sp.dma_start(x_row[:, u], x_d[u]).then_inc(x_loaded[u], 16)
            for i in range(QKV):
                load_w(i, i)
            for u in range(X_SLOTS):
                sp.wait_ge(xn_ready, u + 1)
                sp.dma_start(x_row[:, u], x_d[X_SLOTS + u]).then_inc(x_loaded[u], 16)
            tiles = QKV_TILES + 2 * WO_TILES
            with sp.Fori(1, tiles // QKV) as g:
                for u in range(QKV):
                    load_w(QKV * g + u, u)
            for i in range(tiles // QKV * QKV, tiles):
                load_w(i, i % QKV)

            def load_residual(o):
                b, cols = part(o)
                wait(sp, x1_stored[o % R_SLOTS], 16 * (o // R_SLOTS))
                sp.dma_start(residual[:, o % R_SLOTS], x_d[b][:, cols]).then_inc(r_loaded[o % R_SLOTS], 16)

            sp.wait_ge(x_turned, B)
            for o in range(2):
                load_residual(o)
            for o in range(2 * B):
                if o + 2 < 2 * B:
                    load_residual(o + 2)
                b, cols = part(o)
                sp.wait_ge(x1_ready, o + 1)
                sp.dma_start(x1_d[b][:, cols], residual[:, o % R_SLOTS]).then_inc(x1_stored[o % R_SLOTS], 16)
            for u in range(R_SLOTS):
                sp.wait_ge(x1_stored[u], 16 * (2 * B // R_SLOTS))

        @block.gpsimd
        def _(pool):
            pool.memset(eps[:, :], LN_EPS)
            make_identity(pool, ident, cleared, made)
            pool.memset(causal[:, :], 0.0).then_inc(cleared, 1)
            pool.wait_ge(cleared, 2)
            pool.affine_select(out=causal[:, :], in_=causal[:, :], compare_op=ALU.is_ge, fill=-1e10,
                               base=0, pattern=[[-1, S]], channel_multiplier=1).then_inc(made, 1)
            pool.memset(zeros[:, :], 0.0).then_inc(cleared, 1)
            pool.wait_ge(x_split, B // 2)
            cast.start_some(pool, *CASTS_SELF)
            blank = clear_d.rearrange("(c n p) d -> c p n d", p=P, c=CLEARS)
            pool.wait_ge(cleared, 3)
            for c in range(CLEARS):
                wait(pool, blanked, 16 * c)
                pool.dma_start(blank[c], zeros[:, :].unsqueeze(1).broadcast_to(blank[c].shape)
                               ).then_inc(blanked, 16)
            pool.wait_ge(blanked, 16 * CLEARS)

        @block.vector
        def _(dve):
            def statistics(b):
                u = b % X_SLOTS
                dve.wait_ge(x_loaded[u], 16 * (b // X_SLOTS) + 16)
                for c in range(2):
                    dve.bn_stats(stats[:, u, c, :], x_row[:, u, c * BANK:(c + 1) * BANK]).then_inc(stats_done, 1)
                dve.wait_ge(stats_done, 2 * b + 2)
                dve.sem_inc(stats_seen, 1)
                dve.bn_aggr(mean_var[:, u, :], stats[:, u].rearrange("p c s -> p (c s)")).then_inc(var_ready, 1)

            def scales(b):
                u = b % X_SLOTS
                dve.wait_ge(std_ready, b + 1)
                dve.reciprocal(rstd[:, u:u + 1], rstd[:, u:u + 1]).then_inc(rstd_ready, 1)
                dve.wait_ge(rstd_ready, b + 1)
                dve.tensor_scalar(shift[:, u:u + 1], mean_var[:, u, 0:1], rstd[:, u:u + 1], -1.0,
                                  ALU.mult, ALU.mult).then_inc(shift_ready, 1)

            def split_x(b):
                dve.wait_ge(x_hi_ready, b + 1)
                cols = slice(b * S, (b + 1) * S)
                for c in range(2):
                    ks = slice(c * KT // 2, (c + 1) * KT // 2)
                    done = dve.tensor_tensor(
                        xT_lo[:, ks, cols],
                        turned_rows(b)[:, c, 0:SH].rearrange("p (k s) -> p k s", k=KT // 2),
                        xT_hi[:, ks, cols].bitcast(F32), ALU.subtract)
                done.then_inc(x_split, 1)

            def split_w(i, slot):
                dve.wait_ge(w_hi_ready, i + 1)
                dve.tensor_tensor(w_lo[:, slot].rearrange("p k n -> p (k n)"), w_raw[:, slot],
                                  w_hi[:, slot].rearrange("p k n -> p (k n)").bitcast(F32),
                                  ALU.subtract).then_inc(w_split, 1)

            def split_wo(m):
                i, (hi, lo), ks = QKV_TILES + m, wo[m // WO_TILES], slice(2 * (m % WO_TILES), 2 * (m % WO_TILES) + 2)
                dve.wait_ge(w_hi_ready, i + 1)
                dve.tensor_tensor(lo[:, ks, :], w_raw[:, i % QKV].rearrange("p (k n) -> p k n", k=2),
                                  hi[:, ks, :].bitcast(F32), ALU.subtract).then_inc(w_split, 1)

            for b in range(2):
                statistics(b)
                scales(b)
            for b in range(B):
                if b == 1:
                    for i in range(QKV):
                        split_w(i, i)
                if b + 2 < B:
                    statistics(b + 2)
                    scales(b + 2)
                split_x(b)

            def step(nt, h):
                t = 2 * nt + h
                dve.wait_ge(scores_ready, t + 1)
                dve.tensor_tensor(probs[:, :, :, :],
                                  scores[0:S, :, 0:SH].rearrange("s e (b k) -> s e b k", b=HALF),
                                  causal[:, :].unsqueeze(1).unsqueeze(1).broadcast_to([S, 2, HALF, S]),
                                  ALU.add).then_inc(masked, 1)
                dve.wait_ge(masked, t + 1)
                dve.tensor_reduce(row_max[:, :, :], probs[:, :, :, :], AX.X, ALU.max).then_inc(max_ready, 1)
                dve.wait_ge(max_ready, t + 1)
                dve.tensor_tensor(probs[:, :, :, :], probs[:, :, :, :],
                                  row_max[:, :, :].unsqueeze(3).broadcast_to([S, 2, HALF, S]),
                                  ALU.subtract).then_inc(centred, 1)
                dve.wait_ge(exp_ready, t + 1)
                dve.tensor_reduce(row_sum[:, :, :], probs[:, :, :, :], AX.X, ALU.add).then_inc(summed, 1)
                dve.wait_ge(summed, t + 1)
                dve.reciprocal(row_sum[:, :, :], row_sum[:, :, :]).then_inc(inverted, 1)
                dve.wait_ge(inverted, t + 1)
                dve.tensor_tensor(probs[:, :, :, :], probs[:, :, :, :],
                                  row_sum[:, :, :].unsqueeze(3).broadcast_to([S, 2, HALF, S]),
                                  ALU.mult).then_inc(probs_ready, 1)
                dve.wait_ge(v_turned, t + 1)
                dve.tensor_copy(v_rows[:, :, :], v_turn[0:S, :].rearrange("s (b n) -> s b n", b=HALF)
                                ).then_inc(v_used, 1)
                if isinstance(nt, int) and nt == KT - 1:
                    for m in (range(QKV) if h == 0 else range(QKV, WO_TILES)):
                        split_wo(m)
                elif h == 0:
                    for i in range(QKV):
                        split_w(QKV * (nt + 1) + i, i)
                dve.wait_ge(at_hi_ready, t + 1)
                at = (slice(None), nt, slice(h * SH, (h + 1) * SH))
                dve.tensor_tensor(at_lo[at], mixed[:, 0:SH], at_hi[at].bitcast(F32),
                                  ALU.subtract).then_inc(at_split, 1)

            dve.wait_ge(made, 2)
            over_pairs(dve, step)
            for o in range(2 * B):
                if o < WO_TILES:
                    split_wo(WO_TILES + o)
                dve.wait_ge(acc_ready, QKV * STEPS + o + 1)
                dve.wait_ge(r_loaded[o % R_SLOTS], 16 * (o // R_SLOTS) + 16)
                rows = residual[:, o % R_SLOTS]
                dve.tensor_tensor(rows, acc[0:S, o % 2, :], rows, ALU.add).then_inc(x1_ready, 1)

        @block.scalar
        def _(act):
            def root(b):
                u = b % X_SLOTS
                act.wait_ge(var_ready, b + 1)
                act.activation(rstd[:, u:u + 1], mean_var[:, u, 1:2], ACT.Sqrt,
                               bias=eps[0:S, :]).then_inc(std_ready, 1)

            def norm(b):
                u = b % X_SLOTS
                act.wait_ge(shift_ready, b + 1)
                wait(act, x_turned, b - 1)
                act.activation(xn[:, b % 2], x_row[:, u], ACT.Identity, bias=shift[:, u:u + 1],
                               scale=rstd[:, u:u + 1]).then_inc(xn_ready, 1)

            def split_x(b):
                act.wait_ge(x_turned, b + 1)
                cols = slice(b * S, (b + 1) * S)
                for c in range(2):
                    done = act.copy(xT_hi[:, c * KT // 2:(c + 1) * KT // 2, cols],
                                    turned_rows(b)[:, c, 0:SH].rearrange("p (k s) -> p k s", k=KT // 2))
                done.then_inc(x_hi_ready, 1)

            def split_w(i, slot, turns):
                act.wait_ge(w_loaded[slot], 16 * turns + 16)
                act.copy(w_hi[:, slot].rearrange("p k n -> p (k n)"), w_raw[:, slot]).then_inc(w_hi_ready, 1)

            def split_wo(m):
                i, hi, ks = QKV_TILES + m, wo[m // WO_TILES][0], slice(2 * (m % WO_TILES), 2 * (m % WO_TILES) + 2)
                act.wait_ge(w_loaded[i % QKV], 16 * (i // QKV) + 16)
                act.copy(hi[:, ks, :], w_raw[:, i % QKV].rearrange("p (k n) -> p k n", k=2)).then_inc(w_hi_ready, 1)

            act.wait_ge(made, 1)
            for b in range(2):
                root(b)
                norm(b)
            for b in range(B):
                if b == 1:
                    for i in range(QKV):
                        split_w(i, i, 0)
                if b + 2 < B:
                    root(b + 2)
                split_x(b)
                if b + 2 < B:
                    norm(b + 2)

            def collect(t, h, n):
                act.wait_ge(acc_ready, QKV * t + n + 1)
                act.activation(qkvT[:, n, h], acc[:, (h + n) % 2, 0:SH], ACT.Copy,
                               scale=HD ** -0.5 if n == 0 else 1.0).then_inc(acc_used, 1)

            def step(nt, h):
                t, end = 2 * nt + h, isinstance(nt, int) and nt == KT - 1
                more = not (end and h == 1)
                act.wait_ge(centred, t + 1)
                act.activation(probs[:, :, :, :], probs[:, :, :, :], ACT.Exp).then_inc(exp_ready, 1)
                for n in range(QKV):
                    if more:
                        collect(t + 1, 1 - h, n)
                    if n == 1:
                        act.wait_ge(p_turned, t + 1)
                        act.copy(probsT[:, :, :, :].rearrange("k e b s -> k e (b s)"),
                                 p_turn[0:S, :, 0:SH]).then_inc(p_used, 1)
                    if h == 0:
                        if end:
                            split_wo(n)
                        else:
                            split_w(QKV * (nt + 1) + n, n, nt + 1)
                if end and h == 1:
                    for m in range(QKV, WO_TILES):
                        split_wo(m)
                act.wait_ge(mixed_ready, t + 1)
                act.sem_inc(act_step, 1)
                act.copy(at_hi[:, nt, h * SH:(h + 1) * SH], mixed[:, 0:SH]).then_inc(at_hi_ready, 1)

            for n in range(QKV):
                collect(0, 0, n)
            over_pairs(act, step)
            for m in range(WO_TILES, 2 * WO_TILES):
                split_wo(m)

        @block.tensor
        def _(pe):
            def project(t, nt, h, n):
                if h == 0:
                    pe.wait_ge(w_split, QKV * nt + n + 1)
                wait(pe, acc_used, QKV * t + n - 1)
                cols = slice(h * SH, (h + 1) * SH)
                for kt in range(KT):
                    mm = split_matmul(pe, acc[:, (h + n) % 2, 0:SH], w_hi[:, n, kt, :], w_lo[:, n, kt, :],
                                      xT_hi[:, kt, cols], xT_lo[:, kt, cols], kt == 0, kt == KT - 1)
                mm.then_inc(acc_ready, 1)

            def step(nt, h):
                t = 2 * nt + h
                more = not (isinstance(nt, int) and t == STEPS - 1)
                following = (t + 1, nt + h, 1 - h)
                pe.wait_ge(acc_used, QKV * t + 2)
                for b in range(HALF):
                    for e in range(2):
                        rows, cols = slice(e * HD, (e + 1) * HD), slice(b * S, (b + 1) * S)
                        mm = pe.matmul(scores[0:S, e, cols], qkvT[rows, 0, h, cols], qkvT[rows, 1, h, cols],
                                       start=True, stop=True)
                mm.then_inc(scores_ready, 1)
                if more:
                    project(*following, 0)
                pe.wait_ge(acc_used, QKV * t + 3)
                for b in range(HALF):
                    mm = pe.transpose(v_turn[0:S, b * P:(b + 1) * P], qkvT[:, 2, h, b * S:(b + 1) * S], ident[:, :])
                mm.then_inc(v_turned, 1)
                if more:
                    project(*following, 1)
                pe.wait_ge(probs_ready, t + 1)
                for e in range(2):
                    for b in range(HALF):
                        mm = pe.transpose(p_turn[0:S, e, b * S:(b + 1) * S], probs[:, e, b, :], ident[0:S, 0:S])
                mm.then_inc(p_turned, 1)
                if more:
                    project(*following, 2)
                pe.wait_ge(p_used, t + 1)
                pe.wait_ge(v_used, t + 1)
                wait(pe, at_split, t)
                for b in range(HALF):
                    for e in range(2):
                        mm = pe.matmul(mixed[e * HD:(e + 1) * HD, b * S:(b + 1) * S],
                                       v_rows[:, b, e * HD:(e + 1) * HD], probsT[:, e, b, :], start=True, stop=True)
                mm.then_inc(mixed_ready, 1)

            pe.wait_ge(made, 1)
            for b in range(B):
                pe.wait_ge(xn_ready, b + 1)
                wait(pe, x_split, b - 1)
                for kt in range(KT):
                    col = kt % (KT // 2) * S
                    mm = pe.transpose(turned_rows(b)[:, kt // (KT // 2), col:col + S],
                                      xn[:, b % 2, kt * P:(kt + 1) * P], ident[0:S, 0:S])
                mm.then_inc(x_turned, 1)
                if b == B - 1:
                    pe.wait_ge(x_split, B)
            for n in range(QKV):
                project(0, 0, 0, n)
            over_pairs(pe, step)
            pe.wait_ge(at_split, STEPS)
            for o in range(2 * B):
                b, half = o % B, o // B
                if b == 0:
                    pe.wait_ge(w_split, QKV_TILES + WO_TILES * (half + 1))
                if o < 2:
                    pe.wait_ge(acc_used, QKV * STEPS)
                wait(pe, x1_ready, o - 1)
                hi, lo = wo[half]
                tokens = slice(b * S, (b + 1) * S)
                for kt in range(KT):
                    mm = split_matmul(pe, acc[0:S, o % 2, :], at_hi[:, kt, tokens], at_lo[:, kt, tokens],
                                      hi[:, kt, :], lo[:, kt, :], kt == 0, kt == KT - 1)
                mm.then_inc(acc_ready, 1)


def over_batches(eng, lag, step):
    for u in range(2):
        step(0, u)
    with eng.Fori(1, B // 2 - 1) as g:
        for u in range(2):
            step(g, u)
    for u in range(2 + lag):
        step(B // 2 - 1, u)


def has_batch(b):
    return not isinstance(b, int) or 0 <= b < B


def query_phase(nc, sems, cast, x1_d, w_d, b_d, gq_d, gk_d, q_d):
    OUTS = len(q_d)
    with ExitStack() as ctx:
        sc = Scope(nc, ctx, sems, "query")
        ident = sc.sb("ident", [P, P])
        ln_eps = sc.sb("ln_eps", [P, 1])
        rms_eps = sc.sb("rms_eps", [P, 1])
        x_row = sc.sb("x_row", [S, 2, D])
        xn = sc.sb("xn", [S, 2, D])
        stats = sc.sb("stats", [S, 2, 2, 6])
        mean_var = sc.sb("mean_var", [S, 2, 2])
        rstd = sc.sb("rstd", [S, 2])
        shift = sc.sb("shift", [S, 2])
        xT_hi = sc.sb("xT_hi", [P, 2, KT, S], F32R)
        xT_lo = sc.sb("xT_lo", [P, 2, KT, S], F32R)
        w_raw = sc.sb("w_raw", [P, 2, D])
        w_hi = sc.sb("w_hi", [P, KT, D], F32R)
        w_lo = sc.sb("w_lo", [P, KT, D], F32R)
        bias = sc.sb("bias", [S, D])
        gain = sc.sb("gain", [P, 1 + OUTS, KT])
        q_row = sc.sb("q_row", [S, 2, D])
        square = sc.sb("square", [S, D])
        rms = sc.sb("rms", [S, 2])
        q_out = sc.sb("q_out", [P, OUTS, KT, B * S])
        x_turn = sc.ps("x_turn", [P, 2, BANK])
        q_turn = sc.ps("q_turn", [P, 2, BANK])
        acc = sc.ps("acc", [P, 2, 2, BANK])

        cleared, made, small_loaded = sc.sem("cleared"), sc.sem("made"), sc.sem("small_loaded")
        x_loaded = [sc.sem(f"x_loaded{u}") for u in range(2)]
        w_loaded = [sc.sem(f"w_loaded{u}") for u in range(2)]
        w_hi_ready, w_split = sc.sem("w_hi_ready"), sc.sem("w_split")
        gains_made = sc.sem("gains_made")
        stats_done, stats_seen, var_ready = sc.sem("stats_done"), sc.sem("stats_seen"), sc.sem("var_ready")
        std_ready, rstd_ready, shift_ready = sc.sem("std_ready"), sc.sem("rstd_ready"), sc.sem("shift_ready")
        xn_ready, x_turned = sc.sem("xn_ready"), sc.sem("x_turned")
        x_hi_ready, x_split = sc.sem("x_hi_ready"), sc.sem("x_split")
        acc_ready, biased = sc.sem("acc_ready"), sc.sem("biased")
        squared, rms_ready, inverted = sc.sem("squared"), sc.sem("rms_ready"), sc.sem("inverted")
        scaled, q_turned, gained = sc.sem("scaled"), sc.sem("q_turned"), sc.sem("gained")
        stored = sc.sem("stored")
        block = ctx.enter_context(nc.Block())

        @block.sync
        def _(sp):
            def load_x(b, u):
                wait(sp, xn_ready, b - 1)
                sp.dma_start(x_row[:, u], x1_d[b]).then_inc(x_loaded[u], 16)

            for u in range(2):
                load_x(u, u)
            for kt in range(KT):
                wait(sp, w_split, kt - 1)
                sp.dma_start(w_raw[:, kt % 2], w_d[kt]).then_inc(w_loaded[kt % 2], 16)
                if kt == 1:
                    sp.dma_start(bias[:, :], b_d.partition_broadcast(S)).then_inc(small_loaded, 16)
                    for n, g_d in enumerate((gq_d, *gk_d)):
                        sp.dma_start(gain[:, n, :], g_d).then_inc(small_loaded, 16)
            with sp.Fori(1, B // 2) as g:
                for u in range(2):
                    load_x(2 * g + u, u)
            for n in range(B // 2):
                sp.wait_ge(gained, 2 * (n + 1))
                cols = slice(2 * n * S, 2 * (n + 1) * S)
                for o in range(OUTS):
                    sp.dma_start(q_d[o].rearrange("k p s -> p k s")[:, :, cols],
                                 q_out[:, o, :, cols]).then_inc(stored, 16)
            sp.wait_ge(stored, B // 2 * OUTS * 16)

        @block.gpsimd
        def _(pool):
            pool.memset(ln_eps[:, :], LN_EPS)
            pool.memset(rms_eps[:, :], RMS_EPS)
            make_identity(pool, ident, cleared, made)
            pool.wait_ge(w_split, KT)
            cast.start_some(pool, *CASTS_Q)

        @block.vector
        def _(dve):
            def norm(b, u):
                if not has_batch(b):
                    return
                dve.wait_ge(x_loaded[u], 16 * (b // 2) + 16 if isinstance(b, int) else 8 * (b - u) + 16)
                for c in range(2):
                    dve.bn_stats(stats[:, u, c, :], x_row[:, u, c * BANK:(c + 1) * BANK]).then_inc(stats_done, 1)
                dve.wait_ge(stats_done, 2 * b + 2)
                dve.sem_inc(stats_seen, 1)
                dve.bn_aggr(mean_var[:, u, :], stats[:, u].rearrange("p c s -> p (c s)")).then_inc(var_ready, 1)
                dve.wait_ge(std_ready, b + 1)
                dve.reciprocal(rstd[:, u:u + 1], rstd[:, u:u + 1]).then_inc(rstd_ready, 1)
                dve.wait_ge(rstd_ready, b + 1)
                dve.tensor_scalar(shift[:, u:u + 1], mean_var[:, u, 0:1], rstd[:, u:u + 1], -1.0,
                                  ALU.mult, ALU.mult).then_inc(shift_ready, 1)

            def split_x(b, u):
                if has_batch(b):
                    dve.wait_ge(x_hi_ready, b + 1)
                    dve.tensor_tensor(xT_lo[:, u].rearrange("p (c k) s -> p c (k s)", c=2), x_turn[:, :, 0:SH],
                                      xT_hi[:, u].bitcast(F32).rearrange("p (c k) s -> p c (k s)", c=2),
                                      ALU.subtract).then_inc(x_split, 1)

            def gains(b, u):
                if has_batch(b):
                    dve.wait_ge(q_turned, b + 1)
                    for o in range(OUTS):
                        for c in range(2):
                            ks = slice(c * KT // 2, (c + 1) * KT // 2)
                            done = dve.tensor_tensor(
                                q_out[:, o, ks, bass.ts(b, S)],
                                q_turn[:, c, 0:SH].rearrange("p (k s) -> p k s", k=KT // 2),
                                gain[:, 1 + o, ks].unsqueeze(2).broadcast_to([P, KT // 2, S]), ALU.mult)
                    done.then_inc(gained, 1)

            def step(g, u):
                b, u = 2 * g + u, u % 2
                norm(b + 2, u)
                split_x(b + 1, 1 - u)
                if has_batch(b):
                    wait(dve, q_turned, b - 1)
                    for h in range(2):
                        dve.wait_ge(acc_ready, 2 * b + h + 1)
                        cols = slice(h * BANK, (h + 1) * BANK)
                        dve.tensor_tensor(q_row[:, u, cols], acc[0:S, u, h, :], bias[:, cols],
                                          ALU.add).then_inc(biased, 1)
                    dve.wait_ge(rms_ready, b + 1)
                    dve.reciprocal(rms[:, u:u + 1], rms[:, u:u + 1]).then_inc(inverted, 1)
                gains(b - 1, 1 - u)

            for u in range(2):
                norm(u, u)
            split_x(0, 0)
            for kt in range(KT):
                dve.wait_ge(w_hi_ready, kt + 1)
                dve.tensor_tensor(w_lo[:, kt], w_raw[:, kt % 2], w_hi[:, kt].bitcast(F32),
                                  ALU.subtract).then_inc(w_split, 1)
            dve.wait_ge(small_loaded, 16 * (2 + OUTS))
            for o in range(OUTS):
                dve.tensor_tensor(gain[:, 1 + o, :], gain[:, 1 + o, :], gain[:, 0, :],
                                  ALU.mult).then_inc(gains_made, 1)
            dve.wait_ge(gains_made, OUTS)
            over_batches(dve, 1, step)

        @block.scalar
        def _(act):
            def root(b, u):
                if has_batch(b):
                    act.wait_ge(var_ready, b + 1)
                    act.activation(rstd[:, u:u + 1], mean_var[:, u, 1:2], ACT.Sqrt,
                                   bias=ln_eps[0:S, :]).then_inc(std_ready, 1)

            def norm(b, u):
                if has_batch(b):
                    act.wait_ge(shift_ready, b + 1)
                    wait(act, x_turned, b - 1)
                    act.activation(xn[:, u], x_row[:, u], ACT.Identity, bias=shift[:, u:u + 1],
                                   scale=rstd[:, u:u + 1]).then_inc(xn_ready, 1)

            def split_x(b, u):
                if has_batch(b):
                    act.wait_ge(x_turned, b + 1)
                    wait(act, acc_ready, 2 * (b - 1))
                    act.copy(xT_hi[:, u].rearrange("p (c k) s -> p c (k s)", c=2),
                             x_turn[:, :, 0:SH]).then_inc(x_hi_ready, 1)

            def step(g, u):
                b, u = 2 * g + u, u % 2
                root(b + 2, u)
                split_x(b + 1, 1 - u)
                norm(b + 2, u)
                act.wait_ge(biased, 2 * b + 2)
                act.activation(square[:, :], q_row[:, u], ACT.Square,
                               accum_out=rms[:, u:u + 1]).then_inc(squared, 1)
                act.wait_ge(squared, b + 1)
                act.activation(rms[:, u:u + 1], rms[:, u:u + 1], ACT.Sqrt, bias=rms_eps[0:S, :],
                               scale=1.0 / D).then_inc(rms_ready, 1)
                act.wait_ge(inverted, b + 1)
                act.activation(q_row[:, u], q_row[:, u], ACT.Identity, scale=rms[:, u:u + 1]).then_inc(scaled, 1)

            act.wait_ge(made, 1)
            for u in range(2):
                root(u, u)
                norm(u, u)
            split_x(0, 0)
            for kt in range(KT):
                act.wait_ge(w_loaded[kt % 2], 16 * (kt // 2) + 16)
                act.copy(w_hi[:, kt], w_raw[:, kt % 2]).then_inc(w_hi_ready, 1)
            over_batches(act, 0, step)

        @block.tensor
        def _(pe):
            def turn(dst, src):
                for kt in range(KT):
                    col = kt % (KT // 2) * S
                    mm = pe.transpose(dst[:, kt // (KT // 2), col:col + S], src[:, kt * P:(kt + 1) * P],
                                      ident[0:S, 0:S])
                return mm

            def turn_x(b, u):
                if has_batch(b):
                    pe.wait_ge(xn_ready, b + 1)
                    wait(pe, x_split, b)
                    turn(x_turn, xn[:, u]).then_inc(x_turned, 1)

            def turn_q(b, u):
                if has_batch(b):
                    pe.wait_ge(scaled, b + 1)
                    wait(pe, gained, b)
                    turn(q_turn, q_row[:, u]).then_inc(q_turned, 1)

            def step(g, u):
                b, u = 2 * g + u, u % 2
                turn_x(b + 1, 1 - u)
                if has_batch(b):
                    pe.wait_ge(x_split, b + 1)
                    wait(pe, biased, 2 * (b - 1))
                    for h in range(2):
                        cols = slice(h * BANK, (h + 1) * BANK)
                        for kt in range(KT):
                            if isinstance(b, int) and b == 0 and h == 0:
                                pe.wait_ge(w_split, kt + 1)
                            mm = split_matmul(pe, acc[0:S, u, h, :], xT_hi[:, u, kt, :], xT_lo[:, u, kt, :],
                                              w_hi[:, kt, cols], w_lo[:, kt, cols], kt == 0, kt == KT - 1)
                        mm.then_inc(acc_ready, 1)
                turn_q(b - 1, 1 - u)

            pe.wait_ge(made, 1)
            turn_x(0, 0)
            over_batches(pe, 1, step)


MIX_LAG = 2
K_SLOTS = 4


class Part:

    def __init__(self, width, real, tiles, batches, groups, raw_slots):
        self.width, self.real, self.tiles = width, real, tiles
        self.batches, self.groups, self.raw_slots = batches, groups, raw_slots
        self.cols = batches * width
        self.of_group = B // groups
        self.units = self.of_group // batches
        self.rows = tiles[0][1]
        self.runs = []
        for t, (_, rows) in enumerate(tiles):
            if self.runs and self.runs[-1][2] == rows:
                self.runs[-1][1] += 1
            else:
                self.runs.append([t, 1, rows])
        self.steps = KT * self.units
        self.lag = MIX_LAG // batches
        assert self.cols <= BANK and 2 * self.units % K_SLOTS == 0

    def over_steps(self, eng, lag, step):
        u = self.units
        for c in range(u):
            step(0, c)
        with eng.Fori(0, KT // 2 - 1) as g:
            for c in range(u, 3 * u):
                step(g, c)
        for c in range(u, 2 * u + lag):
            step(KT // 2 - 1, c)

    def at(self, g, c):
        return 2 * self.units * g + c, 2 * g + c // self.units

    def on(self, step):
        return not isinstance(step, int) or 0 <= step < self.steps

    def ring(self, group, stage):
        return group * (2 * self.steps + self.units) + (0, self.steps, self.steps + self.units)[stage]

    def squares(self, group, step):
        return 2 * (group * self.steps + step)


IMG_PART = Part(IMG + 1, IMG, [(0, 86), (86, 86), (172, 86)], 1, 1, 3)
TXT_SHORT = Part(160, 160, [(0, 80), (80, 80)], 2, 1, 2)
TXT_FULL = Part(TXT + 1, TXT, [(0, P), (P, P), (2 * P, P), (3 * P, TXT - 3 * P)], 1, 2, 1)
MASKED = -2.0 ** 127
SCALE = HD ** -0.5


class CrossSems:

    def __init__(self, sc):
        sem = sc.sem
        self.ctx_loaded = [sem(f"ctx_loaded{u}") for u in range(3)]
        self.ctx_hi_ready = sem("ctx_hi_ready")
        self.ctx_split = sem("ctx_split")
        self.w_loaded = [sem(f"w_loaded{u}") for u in range(2)]
        self.w_hi_ready = sem("w_hi_ready")
        self.w_split = sem("w_split")
        self.acc_ready = sem("acc_ready")
        self.act_step = sem("act_step")
        self.acc_used = sem("acc_used")
        self.k_stored = [sem(f"k_stored{u}") for u in range(K_SLOTS)]
        self.squared = sem("squared")
        self.inverted = sem("inverted")
        self.k_loaded = [sem(f"k_loaded{u}") for u in range(K_SLOTS)]
        self.k_ready = sem("k_ready")
        self.q_loaded = [sem(f"q_loaded{u}") for u in range(2)]
        self.old_loaded = [sem(f"old_loaded{u}") for u in range(2)]
        self.v_turned = sem("v_turned")
        self.v_used = sem("v_used")
        self.scores_ready = sem("scores_ready")
        self.masked = sem("masked")
        self.max_ready = sem("max_ready")
        self.shift_ready = sem("shift_ready")
        self.exp_ready = sem("exp_ready")
        self.sum_inverted = sem("sum_inverted")
        self.probs_ready = sem("probs_ready")
        self.p_turned = sem("p_turned")
        self.p_used = sem("p_used")
        self.mixed_ready = sem("mixed_ready")
        self.mixed_used = sem("mixed_used")
        self.stored = [sem(f"stored{u}") for u in range(2)]


class CrossMemory:

    def __init__(self, sc, parts):
        cols = max(p.cols for p in parts)
        width = max(p.width for p in parts)
        rows = max(p.rows for p in parts)
        tiles = max(len(p.tiles) for p in parts)
        v_tiles = max(len(p.tiles) * p.batches for p in parts)
        all_cols = max(p.cols * p.units for p in parts)
        raw = max(p.raw_slots * p.cols for p in parts)
        self.ident = sc.sb("ident", [P, P])
        self.ones = sc.sb("ones", [P, P])
        self.eps = sc.sb("eps", [P, 1])
        self.bias = sc.sb("bias", [P, 2, KT])
        self.ctx_hi = sc.sb("ctx_hi", [P, KT, all_cols], F32R)
        self.ctx_lo = sc.sb("ctx_lo", [P, KT, all_cols], F32R)
        self.raw = sc.sb("raw", [P, KT * raw])
        self.w_raw = sc.sb("w_raw", [P, 2, KT, P])
        self.w_hi = sc.sb("w_hi", [P, 2, KT, P], F32R)
        self.w_lo = sc.sb("w_lo", [P, 2, KT, P], F32R)
        self.norm = sc.sb("norm", [P, all_cols])
        self.square = sc.sb("square", [P, cols])
        self.kT = sc.sb("kT", [P, K_SLOTS, cols])
        self.vT = sc.sb("vT", [P, 2, cols])
        self.v = sc.sb("v", [rows, K_SLOTS, v_tiles, P])
        self.row_max = sc.sb("row_max", [S, 2, 2])
        self.shift = sc.sb("shift", [S, 2, 2])
        self.row_sum = sc.sb("row_sum", [S, 2, 2])
        self.probs = sc.sb("probs", [S, 2, 2, width])
        self.probsT = sc.sb("probsT", [rows, 2, tiles, S])
        self.acc = sc.ps("acc", [P, 2, BANK])
        self.scores = sc.ps("scores", [P, 2, BANK])
        self.v_turn = sc.ps("v_turn", [P, BANK])
        self.p_turn = sc.ps("p_turn", [P, 2, BANK])
        self.mixed = sc.ps("mixed", [P, BANK])

    def ctx_raw(self, part, slot):
        n = KT * part.cols
        return self.raw[:, slot * n:(slot + 1) * n].rearrange("p (k n) -> p k n", k=KT)

    def q(self, slot):
        return self.raw[:, slot * B * S:(slot + 1) * B * S]

    def attn(self, slot):
        return self.q(2 + slot)


def cross_sp(sp, m, s, part, ctx_d, w_d, k_d, q_d, old_d, out_d):
    U, BS, slots = part.units, part.batches, part.raw_slots

    def load_ctx(group, u):
        cu = group * U + u
        wait(sp, s.ctx_split, cu - slots + 1)
        for i in range(BS):
            b = group * part.of_group + u * BS + i
            sp.dma_start(m.ctx_raw(part, u % slots)[:, :, i * part.width:(i + 1) * part.width],
                         ctx_d[b][:, :, 0:part.width]).then_inc(s.ctx_loaded[u % slots], 16)

    def load_w(group, w, slot):
        wait(sp, s.w_split, 2 * KT * group + w - 1)
        sp.dma_start(m.w_raw[:, slot], w_d[w]).then_inc(s.w_loaded[slot], 16)

    for group in range(part.groups):
        first = group * part.steps
        tokens = slice(group * part.of_group * S, (group + 1) * part.of_group * S)

        def step_k(g, c):
            t, nt = part.at(g, c)
            if c % U == 0 and not (isinstance(nt, int) and nt == 0):
                load_w(group, nt + 1, (c // U + 1) % 2)
            if isinstance(t, int) and t == part.steps - U:
                sp.wait_ge(s.ctx_split, U * (group + 1))
                load_q(0, 0)
                load_old(0, 0, KT // 2 * group)
            sp.wait_ge(s.acc_used, part.ring(group, 0) + t + 1)
            sp.dma_start(k_d[nt, c % U][:, 0:part.cols],
                         m.kT[:, c % K_SLOTS, 0:part.cols]).then_inc(s.k_stored[c % K_SLOTS], 16)

        def load_k(g, c):
            t, nt = part.at(g, c)
            if part.on(t):
                wait(sp, s.scores_ready, BS * (first + t - K_SLOTS + 1))
                sp.dma_start(m.kT[:, c % K_SLOTS, 0:part.cols],
                             k_d[nt, c % U][:, 0:part.cols]).then_inc(s.k_loaded[c % K_SLOTS], 16)

        def load_q(nt, slot):
            wait(sp, s.scores_ready, BS * (first + U * (nt - 1)))
            sp.dma_start(m.q(slot)[:, 0:part.of_group * S], q_d[nt][:, tokens]).then_inc(s.q_loaded[slot], 16)

        def load_old(nt, slot, before):
            if old_d is not None:
                wait(sp, s.stored[slot], 16 * before)
                sp.dma_start(m.attn(slot)[:, 0:part.of_group * S],
                             old_d[nt][:, tokens]).then_inc(s.old_loaded[slot], 16)

        def store(nt, slot):
            sp.wait_ge(s.mixed_used, BS * (first + U * (nt + 1)))
            sp.dma_start(out_d[nt][:, tokens], m.attn(slot)[:, 0:part.of_group * S]).then_inc(s.stored[slot], 16)

        def step_v(g, c):
            t, nt = part.at(g, c)
            other = (c // U + 1) % 2
            load_k(g, c + K_SLOTS - 1)
            last = isinstance(nt, int) and nt == KT - 1
            if c % U == 0 and not last:
                load_w(group, KT + nt + 1, other)
                load_q(nt + 1, other)
            if c % U == U // 2 and not (isinstance(nt, int) and nt == 0):
                store(nt - 1, other)
            if c % U == U - 1 and not last:
                load_old(nt + 1, other, KT // 2 * group + g + (c // U + 1) // 2)

        if group:
            for u in range(2):
                sp.wait_ge(s.stored[u], 16 * (KT // 2) * group)
        load_w(group, 0, 0)
        for u in range(U):
            load_ctx(group, u)
            if u == 0:
                load_w(group, 1, 1)
        part.over_steps(sp, 0, step_k)
        for u in range(K_SLOTS):
            sp.wait_ge(s.k_stored[u], 16 * (part.steps // K_SLOTS) * (group + 1))
        sp.wait_ge(s.squared, part.squares(group, part.steps))
        for c in range(K_SLOTS - 1):
            load_k(0, c)
        part.over_steps(sp, 0, step_v)
        store(KT - 1, (KT - 1) % 2)
    for u in range(2):
        sp.wait_ge(s.stored[u], 16 * (KT // 2) * part.groups)


def cross_pool(pool, m, s, part, cast, casts):
    U = part.units
    every = KT * U // casts[1][1]
    for group in range(part.groups):
        def step(g, c):
            t, _ = part.at(g, c)
            if group == 0 and c % every == 0:
                cast.start(pool, casts[1][0] // 2 + U // every * g + c // every // 2, c // every % 2)
            pool.wait_ge(s.k_loaded[c % K_SLOTS],
                         16 * (part.steps // K_SLOTS * group + 2 * U // K_SLOTS * g + c // K_SLOTS + 1))
            k = m.kT[:, c % K_SLOTS, 0:part.cols]
            cols = c % U * part.cols
            pool.tensor_tensor(k, k, m.norm[:, cols:cols + part.cols], ALU.mult).then_inc(s.k_ready, 1)

        if group == 0:
            pool.wait_ge(s.ctx_split, U)
            cast.start_some(pool, *casts[0])
        pool.wait_ge(s.inverted, U * (group + 1))
        part.over_steps(pool, 0, step)


def cross_act(act, m, s, part, masked):
    U, BS, n, slots = part.units, part.batches, part.cols, part.raw_slots

    for group in range(part.groups):
        first = group * part.steps
        keys, sums, values = (part.ring(group, stage) for stage in range(3))

        def split_ctx(u):
            cu = group * U + u
            act.wait_ge(s.ctx_loaded[u % slots], 16 * BS * (cu // slots + 1))
            wait(act, s.acc_ready, keys)
            act.copy(m.ctx_hi[:, :, u * n:(u + 1) * n], m.ctx_raw(part, u % slots)).then_inc(s.ctx_hi_ready, 1)

        def split_w(g, w, slot, used):
            act.wait_ge(s.w_loaded[slot], 16 * (KT * group + g + 1))
            wait(act, s.acc_ready, used)
            act.copy(m.w_hi[:, slot], m.w_raw[:, slot]).then_inc(s.w_hi_ready, 1)

        def step_k(g, c):
            t, nt = part.at(g, c)
            if isinstance(t, int) and t + slots < U:
                split_ctx(t + slots)
            act.wait_ge(s.acc_ready, keys + t + 1)
            wait(act, s.k_stored[c % K_SLOTS],
                 16 * (part.steps // K_SLOTS * group + 2 * U // K_SLOTS * g + c // K_SLOTS))
            wait(act, s.squared, part.squares(group, t - K_SLOTS + 1))
            act.sem_inc(s.act_step, 1)
            act.activation(m.kT[:, c % K_SLOTS, 0:n], m.acc[:, c % 2, 0:n], ACT.Identity,
                           bias=m.bias[:, 0, bass.ts(nt, 1)]).then_inc(s.acc_used, 1)
            if c % U == U // 2:
                split_w(g + (c // U + 1) // 2, nt + 1, (c // U + 1) % 2, keys + U * nt)

        def collect_v(g, c):
            t, nt = part.at(g, c)
            if part.on(t):
                act.wait_ge(s.acc_ready, values + t + 1)
                wait(act, s.v_turned, first + t - 1)
                act.sem_inc(s.act_step, 1)
                act.activation(m.vT[:, c % 2, 0:n], m.acc[:, (values + c) % 2, 0:n], ACT.Identity,
                               bias=m.bias[:, 1, bass.ts(nt, 1)]).then_inc(s.acc_used, 1)

        def exponentials(t, c, i):
            if part.on(t):
                a, slot = BS * (first + t) + i, (BS * c + i) % 2
                act.wait_ge(s.shift_ready, a + 1)
                for e in range(2):
                    src = (m.probs[:, slot, e, 0:part.real] if masked else m.scores[0:S, e, 0:part.real])
                    done = act.activation(m.probs[:, slot, e, 0:part.real], src, ACT.Exp,
                                          bias=m.shift[:, slot, e:e + 1], scale=SCALE,
                                          accum_out=m.row_sum[:, slot, e:e + 1])
                done.then_inc(s.exp_ready, 1)

        def collect_probs(a):
            act.wait_ge(s.p_turned, a + 1)
            for t, count, rows in part.runs:
                done = act.copy(m.probsT[0:rows, :, t:t + count, :],
                                m.p_turn[0:rows, :, t * S:(t + count) * S].rearrange(
                                    "k e (t s) -> k e t s", t=count))
            done.then_inc(s.p_used, 1)

        def step_v(g, c):
            t, nt = part.at(g, c)
            for i in range(BS):
                exponentials(t, c, i)
                if i == BS - 1:
                    collect_v(g, c + 1)
                    if c % U == U // 2 - 1 and not (isinstance(nt, int) and nt >= KT - 1):
                        split_w(g + (c // U + 1) // 2 + KT // 2, KT + nt + 1, (c // U + 1) % 2, values + U * nt)
                if part.on(t if i else t - 1):
                    collect_probs(BS * (first + t) + i - 1)

        split_w(0, 0, 0, keys)
        for u in range(min(slots, U)):
            split_ctx(u)
        part.over_steps(act, 0, step_k)
        for u in range(U):
            act.wait_ge(s.acc_ready, sums + u + 1)
            act.activation(m.norm[:, u * n:(u + 1) * n], m.acc[:, (sums + u) % 2, 0:n], ACT.Sqrt,
                           bias=m.eps[:, :], scale=1.0 / D).then_inc(s.acc_used, 1)
        collect_v(0, 0)
        part.over_steps(act, part.lag, step_v)


def cross_dve(dve, m, s, part, mask, add):
    U, BS, n, slots = part.units, part.batches, part.cols, part.raw_slots

    for group in range(part.groups):
        first = group * part.steps
        keys, sums, _ = (part.ring(group, stage) for stage in range(3))

        def split_ctx(u):
            dve.wait_ge(s.ctx_hi_ready, group * U + u + 1)
            cols = slice(u * n, (u + 1) * n)
            dve.tensor_tensor(m.ctx_lo[:, :, cols], m.ctx_raw(part, u % slots), m.ctx_hi[:, :, cols].bitcast(F32),
                              ALU.subtract).then_inc(s.ctx_split, 1)

        def split_w(w, slot):
            dve.wait_ge(s.w_hi_ready, 2 * KT * group + w + 1)
            dve.tensor_tensor(m.w_lo[:, slot], m.w_raw[:, slot], m.w_hi[:, slot].bitcast(F32),
                              ALU.subtract).then_inc(s.w_split, 1)

        def step_k(g, c):
            t, nt = part.at(g, c)
            if isinstance(t, int) and t + slots < U:
                split_ctx(t + slots)
            dve.wait_ge(s.acc_used, keys + t + 1)
            k, u = m.kT[:, c % K_SLOTS, 0:n], c % U
            total = m.norm[:, u * n:(u + 1) * n]
            if isinstance(t, int) and t < U:
                dve.tensor_tensor(total, k, k, ALU.mult).then_inc(s.squared, 2)
            else:
                done = part.squares(group, t)
                dve.wait_ge(s.squared, done)
                dve.tensor_tensor(m.square[:, 0:n], k, k, ALU.mult).then_inc(s.squared, 1)
                dve.wait_ge(s.squared, done + 1)
                dve.tensor_tensor(total, total, m.square[:, 0:n], ALU.add).then_inc(s.squared, 1)
            if c % U == U // 2:
                split_w(nt + 1, (c // U + 1) % 2)

        def maxima(t, c, i):
            if not part.on(t):
                return
            a, slot = BS * (first + t) + i, (BS * c + i) % 2
            dve.wait_ge(s.scores_ready, a + 1)
            src = m.scores[0:S, :, 0:part.real]
            if mask is not None:
                src = m.probs[:, slot, :, 0:part.real]
                dve.tensor_tensor(src, m.scores[0:S, :, 0:part.real],
                                  mask[:, 0:part.real].unsqueeze(1).broadcast_to([S, 2, part.real]),
                                  ALU.add).then_inc(s.masked, 1)
                dve.wait_ge(s.masked, a + 1)
            dve.tensor_reduce(m.row_max[:, slot, :], src, AX.X, ALU.max).then_inc(s.max_ready, 1)
            dve.wait_ge(s.max_ready, a + 1)
            dve.tensor_scalar(m.shift[:, slot, :], m.row_max[:, slot, :], -SCALE, None,
                              ALU.mult).then_inc(s.shift_ready, 1)

        def normalise(a, slot):
            dve.wait_ge(s.exp_ready, a + 1)
            dve.reciprocal(m.row_sum[:, slot, :], m.row_sum[:, slot, :]).then_inc(s.sum_inverted, 1)
            dve.wait_ge(s.sum_inverted, a + 1)
            for e in range(2):
                p = m.probs[:, slot, e, 0:part.real]
                done = dve.tensor_scalar(p, p, m.row_sum[:, slot, e:e + 1], None, ALU.mult)
            done.then_inc(s.probs_ready, 1)

        def collect(g, c, i):
            t, _ = part.at(g, c)
            if not part.on(t):
                return
            dve.wait_ge(s.mixed_ready, BS * (first + t) + i + 1)
            slot, u = c // U % 2, c % U
            if u == 0 and i == 0:
                before = KT // 2 * group + g + c // U // 2
                if add:
                    dve.wait_ge(s.old_loaded[slot], 16 * before + 16)
                else:
                    wait(dve, s.stored[slot], 16 * before)
            col = (u * BS + i) * S
            dst, src = m.attn(slot)[:, col:col + S], m.mixed[:, 0:S]
            if add:
                done = dve.tensor_tensor(dst, src, dst, ALU.add)
            else:
                done = dve.tensor_copy(dst, src)
            done.then_inc(s.mixed_used, 1)

        def step_v(g, c):
            t, nt = part.at(g, c)
            for i in range(BS):
                maxima(t, c, i)
                if part.on(t if i else t - 1):
                    normalise(BS * (first + t) + i - 1, (BS * c + i - 1) % 2)
                collect(g, c - part.lag, i)
                if i == 0 and part.on(t):
                    dve.wait_ge(s.v_turned, first + t + 1)
                    for n in range(BS):
                        for tile, count, rows in part.runs:
                            at = n * len(part.tiles) + tile
                            done = dve.tensor_copy(m.v[0:rows, c % K_SLOTS, at:at + count, :],
                                                   m.v_turn[0:rows, at * P:(at + count) * P].rearrange(
                                                       "k (t n) -> k t n", t=count))
                    done.then_inc(s.v_used, 1)
            if c % U == U // 2 - 1 and not (isinstance(nt, int) and nt >= KT - 1):
                split_w(KT + nt + 1, (c // U + 1) % 2)

        split_w(0, 0)
        for u in range(min(slots, U)):
            split_ctx(u)
        part.over_steps(dve, 0, step_k)
        for u in range(U):
            dve.wait_ge(s.acc_used, sums + u + 1)
            norm = m.norm[:, u * n:(u + 1) * n]
            dve.reciprocal(norm, norm).then_inc(s.inverted, 1)
        part.over_steps(dve, part.lag, step_v)


def cross_pe(pe, m, s, part, masked):
    U, BS, n = part.units, part.batches, part.cols
    scores_left = s.masked if masked else s.exp_ready
    half = KT // BS

    for group in range(part.groups):
        first = group * part.steps
        keys, sums, values = (part.ring(group, stage) for stage in range(3))

        def product(r, bank, slot, u, kts):
            if kts[0] == 0:
                wait(pe, s.acc_used, r - 1)
            for kt in kts:
                cols = slice(u * n, (u + 1) * n)
                mm = split_matmul(pe, m.acc[:, bank, 0:n], m.w_hi[:, slot, kt, :], m.w_lo[:, slot, kt, :],
                                  m.ctx_hi[:, kt, cols], m.ctx_lo[:, kt, cols], kt == 0, kt == KT - 1)
            if kts[-1] == KT - 1:
                mm.then_inc(s.acc_ready, 1)

        def step_k(g, c):
            t, nt = part.at(g, c)
            if c % U == 0:
                pe.wait_ge(s.w_split, 2 * KT * group + nt + 1)
            if isinstance(t, int) and t < U:
                pe.wait_ge(s.ctx_split, group * U + t + 1)
            product(keys + t, (keys + c) % 2, c // U % 2, c % U, range(KT))

        def value(g, c, i):
            t, nt = part.at(g, c)
            if part.on(t):
                if c % U == 0 and i == 0:
                    pe.wait_ge(s.w_split, 2 * KT * group + KT + nt + 1)
                product(values + t, (values + c) % 2, c // U % 2, c % U, range(i * half, (i + 1) * half))

        def scores(g, c, i):
            t, _ = part.at(g, c)
            if not part.on(t):
                return
            slot, u = c // U % 2, c % U
            if i == 0:
                if u == 0:
                    pe.wait_ge(s.q_loaded[slot], 16 * (KT // 2 * group + g + c // U // 2 + 1))
                pe.wait_ge(s.k_ready, first + t + 1)
            wait(pe, scores_left, BS * (first + t) + i)
            col = (u * BS + i) * S
            for e in range(2):
                rows = slice(e * HD, (e + 1) * HD)
                mm = pe.matmul(m.scores[0:S, e, 0:part.real], m.q(slot)[rows, col:col + S],
                               m.kT[rows, c % K_SLOTS, i * part.width:i * part.width + part.real],
                               start=True, stop=True)
            mm.then_inc(s.scores_ready, 1)

        def turn_probs(a, slot):
            pe.wait_ge(s.probs_ready, a + 1)
            wait(pe, s.p_used, a)
            for e in range(2):
                for t, (start, rows) in enumerate(part.tiles):
                    mm = pe.transpose(m.p_turn[0:rows, e, t * S:(t + 1) * S],
                                      m.probs[:, slot, e, start:start + rows], m.ident[0:S, 0:S])
            mm.then_inc(s.p_turned, 1)

        def mix(g, c, i):
            t, _ = part.at(g, c)
            if not part.on(t):
                return
            a = BS * (first + t) + i
            if i == 0:
                pe.wait_ge(s.v_used, first + t + 1)
            pe.wait_ge(s.p_used, a + 1)
            wait(pe, s.mixed_used, a)
            for tile, (_, rows) in enumerate(part.tiles):
                for e in range(2):
                    at = i * len(part.tiles) + tile
                    mm = pe.matmul(m.mixed[e * HD:(e + 1) * HD, 0:S],
                                   m.v[0:rows, c % K_SLOTS, at, e * HD:(e + 1) * HD],
                                   m.probsT[0:rows, e, tile, :], start=tile == 0, stop=tile == len(part.tiles) - 1)
            mm.then_inc(s.mixed_ready, 1)

        def turn_v(g, c):
            t, _ = part.at(g, c)
            if not part.on(t):
                return
            pe.wait_ge(s.acc_used, values + t + 1)
            wait(pe, s.v_used, first + t)
            for i in range(BS):
                for tile, (start, rows) in enumerate(part.tiles):
                    at, col = i * len(part.tiles) + tile, i * part.width + start
                    mm = pe.transpose(m.v_turn[0:rows, at * P:(at + 1) * P],
                                      m.vT[:, c % 2, col:col + rows], m.ident[:, :])
            mm.then_inc(s.v_turned, 1)

        def step_v(g, c):
            t, _ = part.at(g, c)
            for i in range(BS):
                scores(g, c, i)
                value(g, c + 1, i)
                if i == 0:
                    turn_v(g, c)
                mix(g, c - part.lag, i)
                if part.on(t if i else t - 1):
                    turn_probs(BS * (first + t) + i - 1, (BS * c + i - 1) % 2)

        part.over_steps(pe, 0, step_k)
        pe.wait_ge(s.squared, part.squares(group, part.steps))
        for u in range(U):
            wait(pe, s.acc_used, sums + u - 1)
            pe.matmul(m.acc[:, (sums + u) % 2, 0:n], m.ones[:, :], m.norm[:, u * n:(u + 1) * n],
                      start=True, stop=True).then_inc(s.acc_ready, 1)
        for i in range(BS):
            value(0, 0, i)
        part.over_steps(pe, part.lag, step_v)


def cross_image_phase(nc, sems, cast, ctx_d, w_d, bias_d, k_d, q_d, out_d):
    part = IMG_PART
    with ExitStack() as ctx:
        sc = Scope(nc, ctx, sems, "img")
        m, s = CrossMemory(sc, [part]), CrossSems(sc)
        cleared, made, bias_loaded = sc.sem("cleared"), sc.sem("made"), sc.sem("bias_loaded")
        block = ctx.enter_context(nc.Block())

        @block.sync
        def _(sp):
            for n in range(2):
                sp.dma_start(m.bias[:, n, :], bias_d[n]).then_inc(bias_loaded, 16)
            cross_sp(sp, m, s, part, ctx_d, w_d, k_d, q_d, None, out_d)

        @block.gpsimd
        def _(pool):
            make_identity(pool, m.ident, cleared, made)
            pool.memset(m.ones[:, :], 1.0)
            pool.memset(m.probs[:, :, :, part.real:part.width], 0.0)
            pool.memset(m.eps[:, :], RMS_EPS).then_inc(made, 1)
            cross_pool(pool, m, s, part, cast, CASTS_IMG)

        @block.vector
        def _(dve):
            cross_dve(dve, m, s, part, None, False)

        @block.scalar
        def _(act):
            act.wait_ge(made, 2)
            act.wait_ge(bias_loaded, 32)
            cross_act(act, m, s, part, False)

        @block.tensor
        def _(pe):
            pe.wait_ge(made, 2)
            cross_pe(pe, m, s, part, False)


def cross_text_phase(nc, sems, cast, ctx_d, w_d, bias_d, lens_d, k_d, q_d, old_d, out_d):
    with ExitStack() as ctx:
        sc = Scope(nc, ctx, sems, "txt")
        m = CrossMemory(sc, [TXT_SHORT, TXT_FULL])
        s = CrossSems(sc)
        mask = sc.sb("mask", [S, TXT])
        length = sc.sb("length", [S, 1])
        outside = sc.sb("outside", [S, 2])
        full = sc.sb("full", [S, 1], I32)
        cleared, made, bias_loaded = sc.sem("cleared"), sc.sem("made"), sc.sem("bias_loaded")
        len_loaded, len_step, mask_ready = sc.sem("len_loaded"), sc.sem("len_step"), sc.sem("mask_ready")
        key_index = m.probs[:, 0, 0, 0:TXT].bitcast(I32)
        len_int = full[:, :]
        block = ctx.enter_context(nc.Block())

        def by_length(eng, run):
            eng.wait_ge(mask_ready, 3)
            is_full = eng.value_load(full[0:1, 0:1], min_val=0, max_val=1)
            with eng.If(is_full > 0):
                run(TXT_FULL)
            with eng.Else():
                run(TXT_SHORT)

        @block.sync
        def _(sp):
            sp.dma_start(len_int, lens_d).then_inc(len_loaded, 16)
            for n in range(2):
                sp.dma_start(m.bias[:, n, :], bias_d[n]).then_inc(bias_loaded, 16)
            by_length(sp, lambda part: cross_sp(sp, m, s, part, ctx_d, w_d, k_d, q_d, old_d, out_d))

        @block.gpsimd
        def _(pool):
            make_identity(pool, m.ident, cleared, made)
            pool.iota(key_index, [[1, TXT]], base=0, channel_multiplier=0).then_inc(made, 1)
            pool.memset(m.ones[:, :], 1.0)
            pool.memset(m.eps[:, :], RMS_EPS).then_inc(made, 1)
            by_length(pool, lambda part: cross_pool(pool, m, s, part, cast, CASTS_TXT))

        @block.vector
        def _(dve):
            dve.wait_ge(len_loaded, 16)
            dve.wait_ge(made, 2)
            dve.tensor_copy(length[:, :], len_int).then_inc(len_step, 1)
            dve.tensor_copy(mask[:, :], key_index).then_inc(len_step, 1)
            dve.wait_ge(len_step, 2)
            dve.tensor_scalar(mask[:, :], mask[:, :], length[:, :], MASKED, ALU.is_ge,
                              ALU.mult).then_inc(mask_ready, 1)
            dve.tensor_scalar(outside[:, 0:1], length[:, :], float(TXT_SHORT.real), None,
                              ALU.is_gt).then_inc(len_step, 1)
            dve.tensor_scalar(outside[:, 1:2], length[:, :], 1.0, None, ALU.is_lt).then_inc(len_step, 1)
            dve.wait_ge(len_step, 4)
            dve.tensor_reduce(outside[:, 0:1], outside[:, :], AX.X, ALU.max).then_inc(mask_ready, 1)
            dve.wait_ge(mask_ready, 2)
            dve.tensor_copy(full[:, :], outside[:, 0:1]).then_inc(mask_ready, 1)
            by_length(dve, lambda part: cross_dve(dve, m, s, part, mask, True))

        @block.scalar
        def _(act):
            act.wait_ge(made, 3)
            act.wait_ge(bias_loaded, 32)
            by_length(act, lambda part: cross_act(act, m, s, part, True))

        @block.tensor
        def _(pe):
            pe.wait_ge(made, 3)
            by_length(pe, lambda part: cross_pe(pe, m, s, part, True))


EXPERTS, TOP_K, FF = 64, 8, 384
FT = FF // P
ROWS = B * S * TOP_K
MAX_TILES_OF = -(-B * S // P)
MAX_TILES = ROWS // P + EXPERTS
MATS, MAT = 3, KT * FF


class Routing:

    def __init__(self, sc):
        self.x2 = sc.sb("x2", [S, B, D])
        self.logits = sc.sb("logits", [S, B, EXPERTS])
        self.weights = sc.sb("weights", [S, B, TOP_K])
        self.results = sc.sb("results", [S, B * TOP_K], I32)
        self.table = sc.sb("table", [1, 4, EXPERTS], I32)
        self.w = [sc.sb(f"w{e}", [P, MATS, MAT], BF16) for e in range(W_SLOTS - 1)]
        self.w_loaded = [sc.sem(f"w_loaded{e}") for e in range(W_SLOTS)]


W_SLOTS = 4
TILES, FIRST, FURTHER, THIRD = range(4)


def route_phase(nc, sems, r, cast, x1_d, attn_d, w_out_d, b_out_d, gate_d, xn_d):
    with ExitStack() as ctx:
        sc = Scope(nc, ctx, sems, "route")
        ident = sc.sb("ident", [P, P])
        eps = sc.sb("eps", [P, 1])
        w_raw = sc.sb("w_raw", [P, 2, D])
        w_hi = sc.sb("w_hi", [P, KT, D], F32R)
        w_lo = sc.sb("w_lo", [P, KT, D], F32R)
        b_out = sc.sb("b_out", [S, D])
        gate = sc.sb("gate", [P, KT, EXPERTS])
        at_raw = sc.sb("at_raw", [P, 2, KT, S])
        at_hi = sc.sb("at_hi", [P, 2, KT, S], F32R)
        at_lo = sc.sb("at_lo", [P, 2, KT, S], F32R)
        x1 = sc.sb("x1", [S, 2, D])
        xn = sc.sb("xn", [S, 2, D])
        xnT = sc.sb("xnT", [P, KT, S])
        stats = sc.sb("stats", [S, 2, 2, 6])
        mean_var = sc.sb("mean_var", [S, 2, 2])
        std = sc.sb("std", [S, 2])
        outp = sc.ps("outp", [P, 2, BANK])
        turn = sc.ps("turn", [P, 2, BANK])
        logit_ps = sc.ps("logit_ps", [P, BANK])

        cleared, made = sc.sem("cleared"), sc.sem("made")
        w_loaded = [sc.sem(f"w_loaded{u}") for u in range(2)]
        w_hi_ready, w_split = sc.sem("w_hi_ready"), sc.sem("w_split")
        small_loaded = sc.sem("small_loaded")
        at_loaded = [sc.sem(f"at_loaded{u}") for u in range(2)]
        x1_loaded = [sc.sem(f"x1_loaded{u}") for u in range(2)]
        x1_biased = sc.sem("x1_biased")
        at_hi_ready, at_split = sc.sem("at_hi_ready"), sc.sem("at_split")
        outp_ready, x2_ready, x2_seen = sc.sem("outp_ready"), sc.sem("x2_ready"), sc.sem("x2_seen")
        stats_done, stats_seen, var_ready = sc.sem("stats_done"), sc.sem("stats_seen"), sc.sem("var_ready")
        std_ready, rstd_ready, xn_ready = sc.sem("std_ready"), sc.sem("rstd_ready"), sc.sem("xn_ready")
        sent, send_step = [sc.sem(f"sent{u}") for u in range(2)], sc.sem("send_step")
        turned, xnT_ready = sc.sem("turned"), sc.sem("xnT_ready")
        router_ready, logits_ready = sc.sem("router_ready"), sc.sem("logits_ready")
        block = ctx.enter_context(nc.Block())

        @block.sync
        def _(sp):
            attn_rows = attn_d.rearrange("k p (b s) -> b p k s", b=B)

            def load_at(b, u):
                wait(sp, at_split, b - 1)
                sp.dma_start(at_raw[:, u], attn_rows[b]).then_inc(at_loaded[u], 16)

            def load_x1(b, u):
                wait(sp, x2_ready, 2 * (b - 1))
                sp.dma_start(x1[:, u], x1_d[b]).then_inc(x1_loaded[u], 16)

            load_at(0, 0)
            for kt in range(KT):
                wait(sp, w_split, kt - 1)
                sp.dma_start(w_raw[:, kt % 2], w_out_d[kt]).then_inc(w_loaded[kt % 2], 16)
                if kt == 1:
                    sp.dma_start(b_out[:, :], b_out_d.partition_broadcast(S)).then_inc(small_loaded, 16)
                    sp.dma_start(gate[:, :, :], gate_d).then_inc(small_loaded, 16)
                    load_at(1, 1)
                    for u in range(2):
                        load_x1(u, u)
            with sp.Fori(1, B // 2) as g:
                for u in range(2):
                    load_at(2 * g + u, u)
                    load_x1(2 * g + u, u)
            for u in range(2):
                sp.wait_ge(cast.done[u], 16 * EXPERTS * MATS // 2)
            for e in range(W_SLOTS - 1):
                sp.dma_start(r.w[e][:, :, :], cast.of_expert(e)).then_inc(r.w_loaded[e], 16)

        @block.gpsimd
        def _(pool):
            make_identity(pool, ident, cleared, made)
            pool.memset(eps[:, :], LN_EPS).then_inc(made, 1)
            pool.wait_ge(small_loaded, 32)

            def add_bias(b, u):
                pool.wait_ge(x1_loaded[u], 16 * (b // 2) + 16 if isinstance(b, int) else 8 * (b - u) + 16)
                pool.tensor_tensor(x1[:, u], x1[:, u], b_out[:, :], ALU.add).then_inc(x1_biased, 1)

            def send(b, u):
                pool.wait_ge(xn_ready, b + 1)
                pool.sem_inc(send_step, 1)
                pool.dma_start(xn_d[bass.ts(b, S), :], xn[:, u]).then_inc(sent[u], 16)

            add_bias(0, 0)
            add_bias(1, 1)
            with pool.Fori(0, B // 2 - 1) as g:
                for u in range(2):
                    send(2 * g + u, u)
                    add_bias(2 * g + 2 + u, u)
            for u in range(2):
                send(B - 2 + u, u)
            for u in range(2):
                pool.wait_ge(sent[u], 16 * B // 2)

        @block.vector
        def _(dve):
            def split_at(b, u):
                dve.wait_ge(at_hi_ready, b + 1)
                dve.tensor_tensor(at_lo[:, u], at_raw[:, u], at_hi[:, u].bitcast(F32),
                                  ALU.subtract).then_inc(at_split, 1)

            def norm(b, u):
                dve.wait_ge(x1_biased, b + 1)
                for h in range(2):
                    cols = slice(h * BANK, (h + 1) * BANK)
                    dve.wait_ge(outp_ready, 2 * b + h + 1)
                    dve.tensor_tensor(r.x2[:, b, cols], outp[0:S, h, :], x1[:, u, cols],
                                      ALU.add).then_inc(x2_ready, 1)
                dve.wait_ge(x2_ready, 2 * b + 2)
                dve.sem_inc(x2_seen, 1)
                for h in range(2):
                    dve.bn_stats(stats[:, u, h, :],
                                 r.x2[:, b, h * BANK:(h + 1) * BANK]).then_inc(stats_done, 1)
                dve.wait_ge(stats_done, 2 * b + 2)
                dve.sem_inc(stats_seen, 1)
                dve.bn_aggr(mean_var[:, u, :], stats[:, u].rearrange("p c s -> p (c s)")).then_inc(var_ready, 1)
                dve.wait_ge(std_ready, b + 1)
                dve.reciprocal(std[:, u:u + 1], std[:, u:u + 1]).then_inc(rstd_ready, 1)
                dve.wait_ge(rstd_ready, b + 1)
                wait(dve, turned, b - 1)
                wait(dve, sent[u], 8 * (b - u))
                dve.tensor_scalar(xn[:, u, :], r.x2[:, b, :], mean_var[:, u, 0:1], std[:, u:u + 1],
                                  ALU.subtract, ALU.mult).then_inc(xn_ready, 1)

            split_at(0, 0)
            for kt in range(KT):
                dve.wait_ge(w_hi_ready, kt + 1)
                dve.tensor_tensor(w_lo[:, kt], w_raw[:, kt % 2], w_hi[:, kt].bitcast(F32),
                                  ALU.subtract).then_inc(w_split, 1)
            split_at(1, 1)
            for u in range(2):
                norm(u, u)
                split_at(2 + u, u)
            with dve.Fori(1, B // 2 - 1) as g:
                for u in range(2):
                    norm(2 * g + u, u)
                    split_at(2 * g + 2 + u, u)
            for u in range(2):
                norm(B - 2 + u, u)

        @block.scalar
        def _(act):
            act.wait_ge(made, 2)

            def split_at(b, u):
                act.wait_ge(at_loaded[u], 16 * (b // 2) + 16 if isinstance(b, int) else 8 * (b - u) + 16)
                wait(act, outp_ready, 2 * (b - 1))
                act.copy(at_hi[:, u], at_raw[:, u]).then_inc(at_hi_ready, 1)

            def root(b, u):
                act.wait_ge(var_ready, b + 1)
                act.activation(std[:, u:u + 1], mean_var[:, u, 1:2], ACT.Sqrt,
                               bias=eps[0:S, :]).then_inc(std_ready, 1)

            def collect(b):
                act.wait_ge(turned, b + 1)
                act.copy(xnT[:, :, :].rearrange("p (c k) s -> p c (k s)", c=2),
                         turn[:, :, 0:SH]).then_inc(xnT_ready, 1)
                act.wait_ge(router_ready, b + 1)
                act.copy(r.logits[:, b, :], logit_ps[0:S, 0:EXPERTS]).then_inc(logits_ready, 1)

            split_at(0, 0)
            for kt in range(KT):
                act.wait_ge(w_loaded[kt % 2], 16 * (kt // 2) + 16)
                act.copy(w_hi[:, kt], w_raw[:, kt % 2]).then_inc(w_hi_ready, 1)
            split_at(1, 1)
            with act.Fori(0, B // 2 - 1) as g:
                for u in range(2):
                    root(2 * g + u, u)
                    split_at(2 * g + 2 + u, u)
                    collect(2 * g + u)
            for u in range(2):
                root(B - 2 + u, u)
                collect(B - 2 + u)

        @block.tensor
        def _(pe):
            def project(b, u):
                pe.wait_ge(at_split, b + 1)
                for h in range(2):
                    cols = slice(h * BANK, (h + 1) * BANK)
                    wait(pe, x2_ready, 2 * (b - 1) + h + 1)
                    for kt in range(KT):
                        if isinstance(b, int) and b == 0 and h == 0:
                            pe.wait_ge(w_split, kt + 1)
                        mm = split_matmul(pe, outp[0:S, h, :], at_hi[:, u, kt, :], at_lo[:, u, kt, :],
                                          w_hi[:, kt, cols], w_lo[:, kt, cols], kt == 0, kt == KT - 1)
                    mm.then_inc(outp_ready, 1)

            def router(b, u):
                pe.wait_ge(xn_ready, b + 1)
                wait(pe, xnT_ready, b)
                for kt in range(KT):
                    mm = pe.transpose(turn[:, kt // 4, (kt % 4) * S:(kt % 4 + 1) * S],
                                      xn[:, u, kt * P:(kt + 1) * P], ident[0:S, 0:S])
                mm.then_inc(turned, 1)
                pe.wait_ge(xnT_ready, b + 1)
                wait(pe, logits_ready, b)
                for kt in range(KT):
                    mm = pe.matmul(logit_ps[0:S, 0:EXPERTS], xnT[:, kt, :], gate[:, kt, :],
                                   start=kt == 0, stop=kt == KT - 1)
                mm.then_inc(router_ready, 1)

            pe.wait_ge(made, 2)
            project(0, 0)
            pe.wait_ge(small_loaded, 32)
            project(1, 1)
            router(0, 0)
            project(2, 0)
            router(1, 1)
            with pe.Fori(1, B // 2 - 1) as g:
                project(2 * g + 1, 1)
                router(2 * g, 0)
                project(2 * g + 2, 0)
                router(2 * g + 1, 1)
            project(B - 1, 1)
            router(B - 2, 0)
            router(B - 1, 1)

class Precast:

    def __init__(self, nc, src_d, dst_d):
        self.src_d, self.dst_d = src_d, dst_d
        self.done = [nc.alloc_semaphore(name=f"precast_done{u}") for u in range(2)]
        self.step = nc.alloc_semaphore(name="precast_step")

    def start(self, pool, pair, u):
        wait(pool, self.done[u], 16 * pair)
        pool.sem_inc(self.step, 1)
        n = 2 * pair + u
        pool.dma_start(self.dst_d[n], self.src_d[n]).then_inc(self.done[u], 16)

    def of_expert(self, e):
        return self.dst_d[bass.ds(e * MATS, MATS)].rearrange("m p n -> p m n")

    def start_some(self, pool, first, count):
        for u in range(2):
            self.start(pool, first // 2, u)
        with pool.Fori(first // 2 + 1, (first + count) // 2) as pair:
            for u in range(2):
                self.start(pool, pair, u)


def over_experts(eng, lag, step):
    for c in range(W_SLOTS):
        step(0, c)
    with eng.Fori(1, EXPERTS // W_SLOTS - 1) as g:
        for c in range(W_SLOTS):
            step(g, c)
    for c in range(W_SLOTS + lag):
        step(EXPERTS // W_SLOTS - 1, c)


def has_expert(e):
    return not isinstance(e, int) or 0 <= e < EXPERTS


def experts_phase(nc, sems, r, cast, xn_d, out_d):
    LAG = 2
    with ExitStack() as ctx:
        sc = Scope(nc, ctx, sems, "moe")
        ident = sc.sb("ident", [P, P], BF16)
        w = [*r.w, sc.sb("w_last", [P, MATS, MAT], BF16)]
        rows = sc.sb("rows", [P, W_SLOTS, 2, D], BF16)
        rowsT = sc.sb("rowsT", [P, 2, KT, P], BF16)
        silu = sc.sb("silu", [P, 2, FT * P])
        inner = sc.sb("inner", [P, 2, FT, P], BF16)
        out = sc.sb("out", [P, W_SLOTS, D], BF16)
        x_rowsT = sc.sb("x_rowsT", [P, KT, P], BF16)
        x_silu = sc.sb("x_silu", [P, FT * P])
        x_inner = sc.sb("x_inner", [P, FT, P], BF16)
        x_out = sc.sb("x_out", [P, D], BF16)
        before = sc.sb("before", [S, S], BF16)
        ones = sc.sb("ones", [S, P], BF16)
        logit_max = sc.sb("logit_max", [S, B])
        top = sc.sb("top", [S, B, TOP_K])
        rest = sc.sb("rest", [S, B, EXPERTS])
        chosen = sc.sb("chosen", [S, B, EXPERTS])
        chosen_bf = sc.sb("chosen_bf", [S, B, EXPERTS], BF16)
        top_sum = sc.sb("top_sum", [S, B])
        prior = sc.sb("prior", [P, B + 1, EXPERTS])
        place = sc.sb("place", [S, B, EXPERTS])
        picked = sc.sb("picked", [S, B, EXPERTS])
        result = sc.sb("result", [S, B, EXPERTS])
        top_result = sc.sb("top_result", [S, B, TOP_K])
        match = sc.sb("match", [S, B, TOP_K, EXPERTS])
        tiles_of = sc.sb("tiles_of", [P, EXPERTS])
        tile_end = sc.sb("tile_end", [P, EXPERTS])
        tile_start = sc.sb("tile_start", [P, EXPERTS])
        unit = sc.sb("unit", [P, EXPERTS])
        expert_int = sc.sb("expert_int", [1, EXPERTS], I32)
        expert_no = sc.sb("expert_no", [1, EXPERTS])
        behind = sc.sb("behind", [1, EXPERTS])
        thirds_of = sc.sb("thirds_of", [1, EXPERTS])
        third_end = sc.sb("third_end", [1, EXPERTS])
        third_start = sc.sb("third_start", [1, EXPERTS])
        seat_int = sc.sb("seat_int", [S, 2 * P], I32)
        seat = sc.sb("seat", [S, 2 * P])
        number_int = sc.sb("number_int", [S, B, 2], I32)
        number = sc.sb("number", [S, B, 2], BF16)
        seated = sc.sb("seated", [S, 2, B, 2 * P], BF16)
        index = sc.sb("index", [P, W_SLOTS, 2], I32)
        x_seated = sc.sb("x_seated", [S, B, P], BF16)
        x_index = sc.sb("x_index", [P, 1], I32)
        turn = sc.ps("turn", [P, KT, P], BF16)
        number_ps = sc.ps("number_ps", [P, BANK])
        gate_ps = sc.ps("gate_ps", [P, 2, BANK])
        up_ps = sc.ps("up_ps", [P, 2, BANK])
        out_ps = sc.ps("out_ps", [P, 2, BANK])
        rank_ps, count_ps = out_ps[:, 0, :], out_ps[:, 1, :]

        cleared, made = sc.sem("cleared"), sc.sem("made")
        link_step = sc.sem("link_step")
        centred, exp_ready = sc.sem("centred"), sc.sem("exp_ready")
        chosen_ready, ranked = sc.sem("chosen_ready"), sc.sem("ranked")
        table_ready, table_seen = sc.sem("table_ready"), sc.sem("table_seen")
        seated_ready, numbered = sc.sem("seated_ready"), sc.sem("numbered")
        index_ready = sc.sem("index_ready")
        x_moved, x_seated_ready = sc.sem("x_moved"), sc.sem("x_seated_ready")
        x_numbered, x_index_ready = sc.sem("x_numbered"), sc.sem("x_index_ready")
        w_loaded = r.w_loaded
        rows_loaded = [sc.sem(f"rows_loaded{u}") for u in range(W_SLOTS)]
        turned, rowsT_ready = sc.sem("turned"), sc.sem("rowsT_ready")
        gate_ready, up_ready = sc.sem("gate_ready"), sc.sem("up_ready")
        silu_ready, inner_ready = sc.sem("silu_ready"), sc.sem("inner_ready")
        out_ready = sc.sem("out_ready")
        left_copied, right_copied = sc.sem("left_copied"), sc.sem("right_copied")
        stored = [sc.sem(f"stored{u}") for u in range(W_SLOTS)]
        x_loaded, x_landed = sc.sem("x_loaded"), sc.sem("x_landed")
        gather_step = sc.sem("gather_step")
        x_turned, x_rowsT_ready = sc.sem("x_turned"), sc.sem("x_rowsT_ready")
        x_gate_ready, x_up_ready = sc.sem("x_gate_ready"), sc.sem("x_up_ready")
        x_silu_ready, x_inner_ready = sc.sem("x_silu_ready"), sc.sem("x_inner_ready")
        x_out_ready, x_copied = sc.sem("x_out_ready"), sc.sem("x_copied")
        x_stored, x_done, x_ended = sc.sem("x_stored"), sc.sem("x_done"), sc.sem("x_ended")
        block = ctx.enter_context(nc.Block())

        def await_table(eng):
            eng.wait_ge(table_ready, 1)
            eng.sem_inc(table_seen, 1)

        def first_tile(eng, e):
            return eng.value_load(r.table[0:1, FIRST, bass.ts(e, 1)], min_val=0, max_val=MAX_TILES - 1)

        def further(eng, e, tile):
            if not has_expert(e):
                return
            tiles = eng.value_load(r.table[0:1, TILES, bass.ts(e, 1)], min_val=1, max_val=MAX_TILES_OF)
            with eng.If(tiles > 1):
                tiles_before = eng.value_load(r.table[0:1, FURTHER, bass.ts(e, 1)], min_val=0, max_val=ROWS // P)
                with eng.Fori(1, tiles) as j:
                    tile(j, j - 1 + tiles_before)

        def mat(slot, n, columns):
            return w[slot][:, n, :].rearrange("p (k f) -> p k f", f=columns)

        @block.sync
        def _(sp):
            def load(g, c):
                e, slot = W_SLOTS * g + c, c % W_SLOTS
                if has_expert(e):
                    wait(sp, out_ready, e - W_SLOTS + 1)
                    sp.dma_start(w[slot][:, :, :], cast.of_expert(e)).then_inc(w_loaded[slot], 16)

            over_experts(sp, 0, lambda g, c: load(g, c + W_SLOTS - 1))

        @block.gpsimd
        def _(pool):
            make_identity(pool, ident, cleared, made)
            pool.memset(unit[:, :], 1.0)
            pool.memset(ones[:, :], 1.0)
            pool.memset(prior[:, 0, :], 0.0)
            pool.iota(expert_int[:, :], [[1, EXPERTS]], base=0, channel_multiplier=0)
            pool.iota(seat_int[:, :], [[1, 2 * P]], base=1, channel_multiplier=0)
            pool.iota(number_int[:, :, 0], [[S, B]], base=0, channel_multiplier=0)
            pool.iota(number_int[:, :, 1], [[0, B]], base=0, channel_multiplier=1)
            pool.memset(before[:, :], 1.0).then_inc(cleared, 1)
            pool.wait_ge(cleared, 2)
            pool.affine_select(out=before[:, :], in_=before[:, :], compare_op=ALU.is_ge, fill=0.0,
                               base=-1, pattern=[[1, S]], channel_multiplier=-1).then_inc(made, 1)

            def gather_tile(dst, rows_of, loaded):
                pool.indirect_dma_start(
                    out=dst, out_offset=None, in_=xn_d[:, :],
                    in_offset=bass.IndirectOffsetOnAxis(ap=rows_of, axis=0)).then_inc(loaded, 16)

            def gather(g, c):
                e, slot = W_SLOTS * g + c, c % W_SLOTS
                if has_expert(e):
                    pool.wait_ge(index_ready, e + 1)
                    pool.sem_inc(gather_step, 1)
                    gather_tile(rows[:, slot, 0], index[:, slot, 0:1], rows_loaded[slot])
                    tiles = pool.value_load(r.table[0:1, TILES, bass.ts(e, 1)], min_val=1, max_val=MAX_TILES_OF)
                    with pool.If(tiles > 1):
                        gather_tile(rows[:, slot, 1], index[:, slot, 1:2], rows_loaded[slot])
                    with pool.Else():
                        pool.dma_start(rows[0:1, slot, 1, 0:KT], xn_d[0:1, 0:KT]).then_inc(rows_loaded[slot], 16)

            def step(g, c):
                e = W_SLOTS * g + c
                gather(g, c + W_SLOTS - 1)

                def tile(j, x):
                    with pool.If(j > 1):
                        pool.wait_ge(x_index_ready, x + 1)
                        pool.sem_inc(gather_step, 1)
                        gather_tile(rows[:, c % W_SLOTS, 1], x_index[:, 0:1], x_loaded)
                        third = pool.value_load(r.table[0:1, THIRD, bass.ts(e, 1)], min_val=0, max_val=ROWS // P)
                        pool.wait_ge(x_loaded, 16 * third + 16 * j - 16)
                        pool.sem_inc(gather_step, 1)
                    pool.sem_inc(x_landed, 1)

                further(pool, e, tile)

            await_table(pool)
            for c in range(W_SLOTS - 1):
                gather(0, c)
            over_experts(pool, 0, step)

        @block.vector
        def _(dve):
            steps = [0]

            def link(ins):
                steps[0] += 1
                ins.then_inc(link_step, 1)
                dve.wait_ge(link_step, steps[0])

            def route():
                link(dve.tensor_reduce(logit_max[:, :], r.logits[:, :, :], AX.X, ALU.max))
                dve.tensor_tensor(r.logits[:, :, :], r.logits[:, :, :],
                                  logit_max[:, :].unsqueeze(2).broadcast_to([S, B, EXPERTS]),
                                  ALU.subtract).then_inc(centred, 1)
                dve.wait_ge(made, 2)
                dve.tensor_copy(expert_no[:, :], expert_int[:, :])
                dve.tensor_copy(seat[:, :], seat_int[:, :])
                dve.tensor_copy(number[:, :, :], number_int[:, :, :])
                dve.wait_ge(exp_ready, 1)
                for b in range(B):
                    last = dve.max(top[:, b, :], r.logits[:, b, :])
                link(last)
                for b in range(B):
                    last = dve.match_replace(rest[:, b, :], top[:, b, :], r.logits[:, b, :], -1.0)
                link(last)
                link(dve.tensor_scalar(chosen[:, :, :], rest[:, :, :], 0.0, None, ALU.is_lt))
                dve.tensor_copy(chosen_bf[:, :, :], chosen[:, :, :]).then_inc(chosen_ready, 1)
                dve.wait_ge(ranked, 1)
                for b in range(B):
                    link(dve.tensor_tensor(prior[:, b + 1, :], prior[:, b, :],
                                           count_ps[:, b * EXPERTS:(b + 1) * EXPERTS], ALU.add))
                link(dve.scalar_tensor_tensor(out=place[:, :, :], in0=prior[0:S, 0:B, :], scalar=1.0,
                                              in1=rank_ps[0:S, :].rearrange("s (b e) -> s b e", b=B),
                                              op0=ALU.add, op1=ALU.add))
                link(dve.tensor_tensor(picked[:, :, :], place[:, :, :], chosen[:, :, :], ALU.mult))

            def tabulate():
                total = prior[:, B, :]
                link(dve.tensor_scalar(tiles_of[:, :], total, float(P), 1.0, ALU.is_gt, ALU.add))
                for n in range(2, MAX_TILES_OF):
                    link(dve.scalar_tensor_tensor(out=tiles_of[:, :], in0=total, scalar=float(n * P),
                                                  in1=tiles_of[:, :], op0=ALU.is_gt, op1=ALU.add))
                link(dve.tensor_tensor_scan(tile_end[:, :], unit[:, :], tiles_of[:, :], 0.0, ALU.mult, ALU.add))
                link(dve.tensor_tensor(tile_start[:, :], tile_end[:, :], tiles_of[:, :], ALU.subtract))
                link(dve.tensor_tensor(behind[:, :], tile_start[0:1, :], expert_no[:, :], ALU.subtract))
                link(dve.tensor_scalar(thirds_of[:, :], tiles_of[0:1, :], -2.0, 0.0, ALU.add, ALU.max))
                link(dve.tensor_tensor_scan(third_end[:, :], unit[0:1, :], thirds_of[:, :], 0.0, ALU.mult, ALU.add))
                link(dve.tensor_tensor(third_start[:, :], third_end[:, :], thirds_of[:, :], ALU.subtract))
                for n, row in ((TILES, tiles_of), (FIRST, tile_start), (FURTHER, behind), (THIRD, third_start)):
                    link(dve.tensor_copy(r.table[:, n, :], row[0:1, :]))
                dve.sem_inc(table_ready, 1)

            def find_results():
                shape = [S, B, EXPERTS]
                link(dve.scalar_tensor_tensor(out=result[:, :, :],
                                              in0=tile_start[0:S, :].unsqueeze(1).broadcast_to(shape),
                                              scalar=float(P), in1=place[:, :, :], op0=ALU.mult, op1=ALU.add))
                link(dve.tensor_tensor(result[:, :, :], result[:, :, :], chosen[:, :, :], ALU.mult))
                for b in range(B):
                    last = dve.max(top_result[:, b, :], result[:, b, :])
                link(last)
                link(dve.tensor_scalar(r.results[:, :], top_result[:, :, :].rearrange("s b k -> s (b k)"), -1.0,
                                       None, ALU.add))

            def find_weights():
                link(dve.tensor_reduce(top_sum[:, :], top[:, :, :], AX.X, ALU.add))
                link(dve.reciprocal(top_sum[:, :], top_sum[:, :]))
                link(dve.tensor_tensor(r.logits[:, :, :], r.logits[:, :, :],
                                       top_sum[:, :].unsqueeze(2).broadcast_to([S, B, EXPERTS]), ALU.mult))

            def order_weights(n):
                shape = [S, B, TOP_K, EXPERTS]
                if n == 0:
                    link(dve.tensor_tensor(match[:, :, :, :], result[:, :, :].unsqueeze(2).broadcast_to(shape),
                                           top_result[:, :, :].unsqueeze(3).broadcast_to(shape), ALU.is_equal))
                if n == 1:
                    link(dve.tensor_tensor(match[:, :, :, :], match[:, :, :, :],
                                           r.logits[:, :, :].unsqueeze(2).broadcast_to(shape), ALU.mult))
                if n == 2:
                    dve.tensor_reduce(r.weights[:, :, :], match[:, :, :, :], AX.X, ALU.add)

            def compare(dst, e, places):
                shape = [S, B, places]
                return dve.tensor_tensor(dst, picked[:, :, bass.ts(e, 1)].broadcast_to(shape),
                                         seat[:, 0:places].unsqueeze(1).broadcast_to(shape), ALU.is_equal)

            def seat_rows(e, c):
                if has_expert(e):
                    wait(dve, numbered, e - 1)
                    compare(seated[:, c % 2], e, 2 * P).then_inc(seated_ready, 1)

            def note_rows(e, c):
                if has_expert(e):
                    wait(dve, turned, e - W_SLOTS + 1)
                    dve.wait_ge(numbered, e + 1)
                    dve.tensor_copy(index[:, c % W_SLOTS, :], number_ps[:, 0:2]).then_inc(index_ready, 1)

            def turn_rows(e, c):
                if has_expert(e):
                    dve.wait_ge(turned, e + 1)
                    wait(dve, up_ready, e - 1)
                    dve.tensor_copy(rowsT[:, c % 2], turn[:, :, :]).then_inc(rowsT_ready, 1)

            def step(g, c):
                e = W_SLOTS * g + c
                turn_rows(e + 1, c + 1)
                note_rows(e + W_SLOTS - 1, c + W_SLOTS - 1)
                seat_rows(e + W_SLOTS, c)
                if has_expert(e):
                    dve.wait_ge(silu_ready, e + 1)
                    dve.wait_ge(up_ready, e + 1)
                    wait(dve, out_ready, e - 1)
                    dve.tensor_tensor(inner[:, c % 2].rearrange("p f s -> p (f s)"), silu[:, c % 2],
                                      up_ps[:, c % 2, 0:FT * P], ALU.mult).then_inc(inner_ready, 1)
                if has_expert(e - 1):
                    dve.wait_ge(out_ready, e)
                    wait(dve, stored[(c - 1) % W_SLOTS], 16 * (g + (c - 1) // W_SLOTS))
                    dve.tensor_copy(out[:, (c - 1) % W_SLOTS, BANK:D], out_ps[:, 1, :]).then_inc(right_copied, 1)

                def tile(j, x):
                    dve.tensor_scalar(picked[:, :, bass.ts(e, 1)], picked[:, :, bass.ts(e, 1)], float(-P), None,
                                      ALU.add).then_inc(x_moved, 1)
                    with dve.If(j > 1):
                        dve.wait_ge(x_moved, x + 1)
                        compare(x_seated[:, :, :], e, P).then_inc(x_seated_ready, 1)
                        dve.wait_ge(x_numbered, x + 1)
                        dve.tensor_copy(x_index[:, :], number_ps[:, 2:3]).then_inc(x_index_ready, 1)
                    with dve.Else():
                        dve.sem_inc(x_seated_ready, 1)
                        dve.sem_inc(x_index_ready, 1)
                    dve.wait_ge(x_turned, x + 1)
                    dve.tensor_copy(x_rowsT[:, :, :], turn[:, :, :]).then_inc(x_rowsT_ready, 1)
                    dve.wait_ge(x_silu_ready, x + 1)
                    dve.wait_ge(x_up_ready, x + 1)
                    dve.tensor_tensor(x_inner[:, :, :].rearrange("p f s -> p (f s)"), x_silu[:, :],
                                      up_ps[:, c % 2, 0:FT * P], ALU.mult).then_inc(x_inner_ready, 1)
                    dve.wait_ge(x_out_ready, x + 1)
                    dve.wait_ge(x_stored, 16 * x + 16)
                    dve.tensor_copy(x_out[:, BANK:D], out_ps[:, 1, :]).then_inc(x_copied, 1)

                further(dve, e, tile)
                if isinstance(e, int) and e == EXPERTS - W_SLOTS:
                    find_results()
                    find_weights()
                elif isinstance(e, int) and EXPERTS - W_SLOTS < e < EXPERTS:
                    order_weights(e - 1 - EXPERTS + W_SLOTS)

            route()
            tabulate()
            for e in range(W_SLOTS):
                seat_rows(e, e)
                note_rows(e - 1, e - 1)
            await_table(dve)
            turn_rows(0, 0)
            over_experts(dve, LAG, step)

        @block.scalar
        def _(act):
            act.sem_inc(x_stored, 16)
            act.wait_ge(centred, 1)
            act.activation(r.logits[:, :, :], r.logits[:, :, :], ACT.Exp).then_inc(exp_ready, 1)
            await_table(act)

            def step(g, c):
                e = W_SLOTS * g + c
                if has_expert(e):
                    act.wait_ge(gate_ready, e + 1)
                    wait(act, inner_ready, e - 1)
                    act.activation(silu[:, c % 2], gate_ps[:, c % 2, 0:FT * P], ACT.Silu).then_inc(silu_ready, 1)
                if has_expert(e - 1):
                    act.wait_ge(out_ready, e)
                    wait(act, stored[(c - 1) % W_SLOTS], 16 * (g + (c - 1) // W_SLOTS))
                    act.copy(out[:, (c - 1) % W_SLOTS, 0:BANK], out_ps[:, 0, :]).then_inc(left_copied, 1)
                if has_expert(e - 2):
                    first = first_tile(act, e - 2)
                    act.wait_ge(left_copied, e - 1)
                    act.wait_ge(right_copied, e - 1)
                    act.dma_start(out_d[bass.ts(first, P), :],
                                  out[:, (c - 2) % W_SLOTS]).then_inc(stored[(c - 2) % W_SLOTS], 16)

                def tile(j, x):
                    first = first_tile(act, e)
                    act.wait_ge(x_gate_ready, x + 1)
                    act.activation(x_silu[:, :], gate_ps[:, c % 2, 0:FT * P], ACT.Silu).then_inc(x_silu_ready, 1)
                    act.wait_ge(x_out_ready, x + 1)
                    act.wait_ge(x_stored, 16 * x + 16)
                    act.copy(x_out[:, 0:BANK], out_ps[:, 0, :]).then_inc(x_copied, 1)
                    act.wait_ge(x_copied, 2 * x + 2)
                    act.dma_start(out_d[bass.ts(first + j, P), :], x_out[:, :]).then_inc(x_stored, 16)

                further(act, e, tile)

            last = act.value_load(r.table[0:1, TILES, EXPERTS - 1:EXPERTS], min_val=1, max_val=MAX_TILES_OF)
            last_before = act.value_load(r.table[0:1, FURTHER, EXPERTS - 1:EXPERTS], min_val=0, max_val=ROWS // P)
            over_experts(act, LAG, step)
            for u in range(W_SLOTS):
                act.wait_ge(stored[u], 16 * EXPERTS // W_SLOTS)
            act.wait_ge(x_stored, 16 * last_before + 16 * last)
            act.sem_inc(x_ended, 1)

        @block.tensor
        def _(pe):
            pe.wait_ge(made, 2)

            def number_rows(col, src):
                for n in range(2 * B):
                    b, part = n // 2, n % 2
                    mm = pe.matmul(number_ps[:, col:col + 1], src[:, b, :], number[:, b, part:part + 1],
                                   start=n == 0, stop=n == 2 * B - 1)
                return mm

            def pick_rows(e, c):
                if has_expert(e):
                    pe.wait_ge(seated_ready, e + 1)
                    wait(pe, index_ready, e)
                    for t in range(2):
                        mm = number_rows(t, seated[:, c % 2, :, t * P:(t + 1) * P])
                    mm.then_inc(numbered, 1)

            def turn_rows(g, c):
                e = W_SLOTS * g + c
                if has_expert(e):
                    pe.wait_ge(rows_loaded[c % W_SLOTS], 32 * (g + c // W_SLOTS + 1))
                    wait(pe, rowsT_ready, e)
                    for k in range(KT):
                        mm = pe.transpose(turn[:, k, :], rows[:, c % W_SLOTS, 0, k::KT], ident[:, :])
                    mm.then_inc(turned, 1)

            def products(slot, u, x, ready):
                for n, ps in enumerate((gate_ps, up_ps)):
                    for f in range(FT):
                        for k in range(KT):
                            mm = pe.matmul(ps[:, u, f * P:(f + 1) * P], mat(slot, n, FF)[:, k, f::FT], x[:, k, :],
                                           start=k == 0, stop=k == KT - 1)
                    mm.then_inc(ready[n], 1)

            def narrow(slot, x, ready):
                for h in range(2):
                    for f in range(FT):
                        mm = pe.matmul(out_ps[:, h, :], x[:, f, :], mat(slot, 2, D)[:, f, h * BANK:(h + 1) * BANK],
                                       start=f == 0, stop=f == FT - 1)
                mm.then_inc(ready, 1)

            def step(g, c):
                e = W_SLOTS * g + c
                turn_rows(g, c + 1)
                if has_expert(e):
                    pe.wait_ge(w_loaded[c % W_SLOTS], 16 * (g + c // W_SLOTS + 1))
                    pe.wait_ge(rowsT_ready, e + 1)
                    wait(pe, silu_ready, e - 1)
                    wait(pe, inner_ready, e - 1)
                    products(c % W_SLOTS, c % 2, rowsT[:, c % 2], (gate_ready, up_ready))
                if has_expert(e - 1):
                    pe.wait_ge(inner_ready, e)
                    wait(pe, left_copied, e - 1)
                    wait(pe, right_copied, e - 1)
                    narrow((c - 1) % W_SLOTS, inner[:, (c - 1) % 2], out_ready)
                pick_rows(e + W_SLOTS, c)

                def tile(j, x):
                    with pe.If(j > 1):
                        pe.wait_ge(x_seated_ready, x + 1)
                        number_rows(2, x_seated).then_inc(x_numbered, 1)
                    with pe.Else():
                        pe.sem_inc(x_numbered, 1)
                    pe.wait_ge(x_landed, x + 1)
                    pe.wait_ge(rowsT_ready, min(e + 2, EXPERTS) if isinstance(e, int) else e + 2)
                    for k in range(KT):
                        mm = pe.transpose(turn[:, k, :], rows[:, c % W_SLOTS, 1, k::KT], ident[:, :])
                    mm.then_inc(x_turned, 1)
                    pe.wait_ge(x_rowsT_ready, x + 1)
                    pe.wait_ge(inner_ready, e + 1)
                    products(c % W_SLOTS, c % 2, x_rowsT, (x_gate_ready, x_up_ready))
                    pe.wait_ge(x_inner_ready, x + 1)
                    wait(pe, left_copied, e)
                    wait(pe, right_copied, e)
                    narrow(c % W_SLOTS, x_inner, x_out_ready)
                    pe.wait_ge(x_copied, 2 * x + 2)
                    pe.sem_inc(x_done, 1)

                further(pe, e, tile)

            pe.wait_ge(chosen_ready, 1)
            picks = chosen_bf[:, :, :].rearrange("s b e -> s (b e)")
            pe.matmul(rank_ps[0:S, :], before[:, :], picks, start=True, stop=True)
            pe.matmul(count_ps[:, :], ones[:, :], picks, start=True, stop=True).then_inc(ranked, 1)
            for e in range(W_SLOTS):
                pick_rows(e, e)
            await_table(pe)
            turn_rows(0, 0)
            over_experts(pe, LAG, step)


ON_PE = (2, 4, 6)


def combine_phase(nc, sems, r, rows_d, out_d):
    ON_DVE = [k for k in range(TOP_K) if k not in ON_PE]
    PARTS = 3
    with ExitStack() as ctx:
        sc = Scope(nc, ctx, sems, "comb")
        ident = sc.sb("ident", [P, P], BF16)
        part = sc.sb("part", [S, TOP_K, D], BF16)
        narrow = sc.sb("narrow", [S, 2, B * TOP_K], BF16)
        parts = sc.sb("parts", [S, PARTS, B * TOP_K])
        rest = sc.sb("rest", [S, B * TOP_K])
        diag = sc.sb("diag", [S, 2, PARTS, S], BF16)
        acc = sc.ps("acc", [P, 2, 2, BANK])
        cleared, made, link_step = sc.sem("cleared"), sc.sem("made"), sc.sem("link_step")
        parts_ready, diag_ready = sc.sem("parts_ready"), sc.sem("diag_ready")
        gathered = [sc.sem(f"gathered{k}") for k in range(TOP_K)]
        weighed = sc.sem("weighed")
        added = sc.sem("added")
        summed, stored = sc.sem("summed"), sc.sem("stored")
        block = ctx.enter_context(nc.Block())

        @block.gpsimd
        def _(pool):
            make_identity(pool, ident, cleared, made)
            for b in range(B):
                for k in range(TOP_K):
                    if k in ON_PE:
                        wait(pool, weighed, len(ON_PE) * (b - 1) + ON_PE.index(k) + 1)
                    else:
                        wait(pool, added, len(ON_DVE) * (b - 1) + ON_DVE.index(k) + 1)
                    c = b * TOP_K + k
                    pool.indirect_dma_start(
                        out=part[:, k, :], out_offset=None, in_=rows_d[0:MAX_TILES * P, :],
                        in_offset=bass.IndirectOffsetOnAxis(ap=r.results[:, c:c + 1], axis=0)
                    ).then_inc(gathered[k], 16)

        @block.vector
        def _(dve):
            weights = r.weights[:, :, :].rearrange("s b k -> s (b k)")
            steps = [0]

            def link(ins):
                steps[0] += 1
                ins.then_inc(link_step, 1)
                dve.wait_ge(link_step, steps[0])

            left = weights
            for n in range(2):
                link(dve.tensor_copy(narrow[:, n, :], left))
                link(dve.tensor_copy(parts[:, n, :], narrow[:, n, :]))
                after = rest[:, :] if n == 0 else parts[:, 2, :]
                link(dve.tensor_tensor(after, left, parts[:, n, :], ALU.subtract))
                left = after
            dve.sem_inc(parts_ready, 1)
            for b in range(B):
                for n, k in enumerate(ON_DVE):
                    dve.wait_ge(gathered[k], 16 * (b + 1))
                    wait(dve, added, len(ON_DVE) * b + n)
                    dve.scalar_tensor_tensor(out=r.x2[:, b, :], in0=part[:, k, :],
                                             scalar=r.weights[:, b, k:k + 1], in1=r.x2[:, b, :],
                                             op0=ALU.mult, op1=ALU.add).then_inc(added, 1)
                dve.wait_ge(added, len(ON_DVE) * (b + 1))
                dve.wait_ge(weighed, len(ON_PE) * (b + 1))
                dve.tensor_tensor(r.x2[:, b, :], acc[0:S, b % 2].rearrange("s h n -> s (h n)"), r.x2[:, b, :],
                                  ALU.add).then_inc(summed, 1)

        @block.scalar
        def _(act):
            act.wait_ge(made, 1)
            act.wait_ge(parts_ready, 1)
            for b in range(B):
                for n, k in enumerate(ON_PE):
                    done = len(ON_PE) * b + n
                    wait(act, weighed, done - 1)
                    for p in range(PARTS):
                        c = b * TOP_K + k
                        last = act.activation(diag[:, done % 2, p, :], ident[0:S, 0:S], ACT.Identity,
                                              scale=parts[:, p, c:c + 1])
                    last.then_inc(diag_ready, 1)

        @block.tensor
        def _(pe):
            for b in range(B):
                wait(pe, summed, b - 1)
                for n, k in enumerate(ON_PE):
                    done = len(ON_PE) * b + n
                    pe.wait_ge(diag_ready, done + 1)
                    pe.wait_ge(gathered[k], 16 * (b + 1))
                    for h in range(2):
                        for p in range(PARTS):
                            mm = pe.matmul(acc[0:S, b % 2, h, :], diag[:, done % 2, p, :],
                                           part[:, k, h * BANK:(h + 1) * BANK],
                                           start=n == 0 and p == 0, stop=k == ON_PE[-1] and p == PARTS - 1)
                    mm.then_inc(weighed, 1)

        @block.sync
        def _(sp):
            for b in range(B):
                sp.wait_ge(summed, b + 1)
                sp.dma_start(out_d[b], r.x2[:, b, :]).then_inc(stored, 16)
            sp.wait_ge(stored, 16 * B)


def decoder_kernel(nc, a, out):
    def scratch(name, shape, dt=F32):
        return nc.dram_tensor(name, shape, dt).ap()

    q_d = [scratch(f"cross_q_{n}_dram", (KT, P, B * S)) for n in ("img", "txt")]
    x1_d = scratch("x1_dram", (B, S, D))
    img_d = scratch("attn_img_dram", (KT, P, B * S))
    attn_d = scratch("attn_dram", (KT, P, B * S))
    k_d = scratch("cross_k_dram", (KT, B, P, BANK))
    xn_d = scratch("expert_rows_dram", (B * S, D), BF16)
    results_d = scratch("expert_results_dram", ((MAX_TILES + MAX_TILES_OF) * P, D), BF16)
    cast_d = scratch("experts_bf16_dram", (EXPERTS * MATS, P, MAT), BF16)
    sems = []
    cast = Precast(nc, a["moe"], cast_d)
    with ExitStack() as memory:
        self_attention_phase(nc, sems, cast, a["x"], a["w_self"], x1_d, results_d[0:MAX_TILES * P])
        query_phase(nc, sems, cast, x1_d, a["wq"], a["bq"], a["gq"], (a["gk_img"], a["gk"]), q_d)
        cross_image_phase(nc, sems, cast, a["ctx_img"], a["w_img"], (a["bk_img"], a["bv_img"]), k_d, q_d[0], img_d)
        clear_semaphores(nc, sems)
        cross_text_phase(nc, sems, cast, a["ctx_txt"], a["w_txt"], (a["bk"], a["bv"]), a["lens"], k_d, q_d[1],
                         img_d, attn_d)
        clear_semaphores(nc, sems)
        r = Routing(Scope(nc, memory, sems, "routing"))
        route_phase(nc, sems, r, cast, x1_d, attn_d, a["wo"], a["bo"], a["gate"], xn_d)
        experts_phase(nc, sems, r, cast, xn_d, results_d)
        combine_phase(nc, sems, r, results_d, out)



def self_weights(w_qkv, w_out):
    qkv = w_qkv.reshape(KT, P, 3, KT, P).transpose(3, 2, 1, 0, 4).reshape(3 * KT, P, D)
    out = w_out.reshape(KT // 2, 2, P, 2, BANK).transpose(3, 0, 2, 1, 4)[::-1].reshape(KT, P, D)
    return np.concatenate([qkv, out])


def _layouts(i):
    def columns(w):
        n = w.shape[1] // P
        return w.reshape(KT, P, n, P).transpose(2, 1, 0, 3)

    def rows(w):
        return w.reshape(KT, P, w.shape[1])

    def vector(v):
        return v.reshape(KT, P).T

    def context(c):
        c = c.transpose(0, 2, 1).reshape(B, KT, P, c.shape[1]).transpose(0, 2, 1, 3)
        return np.pad(c, ((0, 0), (0, 0), (0, 0), (0, 1)))

    ctx = i["ctx_2048"]
    return {
        "x": i["x"], "ctx_img": context(ctx[:, :IMG]), "ctx_txt": context(ctx[:, IMG:]),
        "w_self": self_weights(i["L0_attn_w_qkv"], i["L0_attn_w_out"]),
        "lens": np.broadcast_to(i["L0_xattn_context_lens"].reshape(1, 1), (S, 1)),
        "wq": rows(i["L0_xattn_Wq"]), "bq": i["L0_xattn_bq"], "gq": vector(i["L0_xattn_gq"]),
        "w_txt": np.concatenate([columns(i["L0_xattn_Wk"]), columns(i["L0_xattn_Wv"])]),
        "bk": vector(i["L0_xattn_bk"]), "gk": vector(i["L0_xattn_gk"]),
        "bv": vector(i["L0_xattn_bv"]),
        "w_img": np.concatenate([columns(i["L0_xattn_Wk_img"]), columns(i["L0_xattn_Wv_img"])]),
        "bk_img": vector(i["L0_xattn_bk_img"]),
        "gk_img": vector(i["L0_xattn_gk_img"]),
        "bv_img": vector(i["L0_xattn_bv_img"]),
        "wo": rows(i["L0_xattn_Wo"]), "bo": i["L0_xattn_bo"],
        "gate": i["L0_ffn_gate_w"].reshape(KT, P, EXPERTS).transpose(1, 0, 2),
        "moe": np.stack([i[f"L0_ffn_{n}_proj"].reshape(EXPERTS, P, MAT) for n in ("gate", "up", "down")],
                        axis=1).reshape(EXPERTS * MATS, P, MAT),
    }


def kernel(**inputs):
    import concourse.bacc as bacc
    from concourse.bass_utils import run_bass_kernel_spmd

    nc = bacc.Bacc("TRN2", target_bir_lowering=False, num_devices=1)
    laid_out = _layouts({name: np.asarray(value) for name, value in inputs.items()})
    arrays, args = {}, {}
    for name, value in laid_out.items():
        value = np.ascontiguousarray(value)
        arrays[f"in_{name}_dram"] = value
        args[name] = nc.dram_tensor(f"in_{name}_dram", value.shape, mybir.dt.from_np(value.dtype),
                                    kind="ExternalInput").ap()
    out = nc.dram_tensor("out_dram", (B, S, D), F32, kind="ExternalOutput").ap()
    decoder_kernel(nc, args, out)
    result = run_bass_kernel_spmd(nc, [arrays], core_ids=[0])
    return result.results[0]["out_dram"]
```
